# Optimizing a Trainium2 kernel written in Bass

```python
import numpy as np
import jax
import jax.numpy as jnp

def _softmax(x, axis=-1):
    return jax.nn.softmax(x, axis=axis)

def _gelu(x):
    return jax.nn.gelu(x, approximate=True)

def _silu(x):
    return jax.nn.silu(x)

def _sigmoid(x):
    return jax.nn.sigmoid(x)

def _layernorm(x, axis=-1, eps=1e-05):
    m = jnp.mean(x, axis=axis, keepdims=True)
    v = jnp.var(x, axis=axis, keepdims=True)
    return (x - m) / jnp.sqrt(v + eps)

def _scatter_add(tgt, idx, src, axis=0):
    return tgt.at[idx].add(src)

def _segment_sum(src, seg, n):
    return jax.ops.segment_sum(src, seg, n)
kernel_name = 'mk_gnn_resnorm_d2_gnn_r64_391c11'

def setup_inputs(seed: int=0):
    np.random.seed(seed)
    _w = jnp.asarray

    def _rec_inputs():
        import jax
        import jax.numpy as jnp
        _gk = jax.random.key(seed)
        x = -0.0005121 + 1.001 * jax.random.normal(jax.random.fold_in(_gk, 1), (100000, 32), jnp.float32)
        src = jax.random.randint(jax.random.fold_in(_gk, 2), (50000,), 0, 100000, jnp.int32)
        dst = jax.random.randint(jax.random.fold_in(_gk, 3), (50000,), 0, 100000, jnp.int32)
        _o = jnp.argsort(dst, stable=True)
        src = src[_o]
        dst = dst[_o]
        edge_attr_16 = 0.000196303 + 1.00016 * jax.random.normal(jax.random.fold_in(_gk, 11), (50000, 16), jnp.float32)
        return (x, src, dst, edge_attr_16)
    x, src, dst, edge_attr_16 = _rec_inputs()

    def _L0_gnn_setup():
        import jax, jax.numpy as jnp
        import numpy as np
        N_NODES = 100000
        N_EDGES = 25000
        LATENT_DIM = 32
        NUM_LAYERS = 3
        key = jax.random.key(seed)
        k_x, k_e = jax.random.split(key)
        x = jax.random.normal(k_x, (N_NODES, LATENT_DIM), dtype=jnp.float32)
        edge_index = jax.random.randint(k_e, (2, N_EDGES), 0, N_NODES, dtype=jnp.int64)
        return {'x': x, 'edge_index': edge_index, 'num_layers': NUM_LAYERS}
    _L0_gnn_all = _L0_gnn_setup()
    _L0_gnn_in = {k: v for k, v in _L0_gnn_all.items() if k in ()}
    del _L0_gnn_all

    def _L1_gnn_setup():
        import jax, jax.numpy as jnp
        import numpy as np
        N_NODES = 50000
        N_EDGES = 25000
        D_NODE = 32
        D_EDGE = 16
        H = 64
        F_OUT = 32
        N_OUT = 32

        def _mlp_params(key, d_in, d_h, d_out):
            k1, k2 = jax.random.split(key)
            s1 = 1.0 / np.sqrt(d_in)
            s2 = 1.0 / np.sqrt(d_h)
            return (jax.random.uniform(k1, (d_in, d_h), jnp.float32, -s1, s1), jnp.zeros((d_h,), jnp.float32), jax.random.uniform(k2, (d_h, d_out), jnp.float32, -s2, s2), jnp.zeros((d_out,), jnp.float32))

        def _mlp(h, W1, b1, W2, b2):
            return jax.nn.relu(jax.nn.relu(h @ W1 + b1) @ W2 + b2)
        key = jax.random.key(seed)
        kx, ke, ka, kf, kb, kn = jax.random.split(key, 6)
        x = jax.random.normal(kx, (N_NODES, D_NODE), jnp.float32)
        edge_index = jax.random.randint(ke, (2, N_EDGES), 0, N_NODES, jnp.int64)
        edge_attr = jax.random.normal(ka, (N_EDGES, D_EDGE), jnp.float32)
        d_flow_in = 2 * D_NODE + D_EDGE
        W1f, b1f, W2f, b2f = _mlp_params(kf, d_flow_in, H, F_OUT)
        W1b, b1b, W2b, b2b = _mlp_params(kb, d_flow_in, H, F_OUT)
        W1n, b1n, W2n, b2n = _mlp_params(kn, 2 * F_OUT, H, N_OUT)
        return dict(x=x, edge_index=edge_index, edge_attr=edge_attr, W1f=W1f, b1f=b1f, W2f=W2f, b2f=b2f, W1b=W1b, b1b=b1b, W2b=W2b, b2b=b2b, W1n=W1n, b1n=b1n, W2n=W2n, b2n=b2n)
    _L1_gnn_all = _L1_gnn_setup()
    _L1_gnn_in = {k: v for k, v in _L1_gnn_all.items() if k in ('W1f', 'b1f', 'W2f', 'b2f', 'W1b', 'b1b', 'W2b', 'b2b', 'W1n', 'b1n', 'W2n', 'b2n')}
    del _L1_gnn_all
    return {'x': x, 'src': src, 'dst': dst, 'edge_attr_16': edge_attr_16, 'L1_gnn_W1f': _L1_gnn_in['W1f'], 'L1_gnn_b1f': _L1_gnn_in['b1f'], 'L1_gnn_W2f': _L1_gnn_in['W2f'], 'L1_gnn_b2f': _L1_gnn_in['b2f'], 'L1_gnn_W1b': _L1_gnn_in['W1b'], 'L1_gnn_b1b': _L1_gnn_in['b1b'], 'L1_gnn_W2b': _L1_gnn_in['W2b'], 'L1_gnn_b2b': _L1_gnn_in['b2b'], 'L1_gnn_W1n': _L1_gnn_in['W1n'], 'L1_gnn_b1n': _L1_gnn_in['b1n'], 'L1_gnn_W2n': _L1_gnn_in['W2n'], 'L1_gnn_b2n': _L1_gnn_in['b2n']}

def reference(x, src, dst, edge_attr_16, L1_gnn_W1f, L1_gnn_b1f, L1_gnn_W2f, L1_gnn_b2f, L1_gnn_W1b, L1_gnn_b1b, L1_gnn_W2b, L1_gnn_b2b, L1_gnn_W1n, L1_gnn_b1n, L1_gnn_W2n, L1_gnn_b2n):
    import jax
    import jax.numpy as jnp

    def _L0_gnn_ref(x, edge_index, num_layers):
        import jax, jax.numpy as jnp
        import numpy as np
        N_NODES = 100000
        N_EDGES = 25000
        LATENT_DIM = 32
        NUM_LAYERS = 3
        N = x.shape[0]
        src = edge_index[0]
        dst = edge_index[1]
        cnt = jax.ops.segment_sum(jnp.ones((edge_index.shape[1],), x.dtype), dst, num_segments=N)
        denom = jnp.maximum(cnt, 1.0)[:, None]
        scale = 1.0 / (num_layers + 1)
        final = x * scale
        for _ in range(num_layers):
            summed = jax.ops.segment_sum(x[src], dst, num_segments=N)
            x = summed / denom
            final = final + x * scale
        return final

    def _L1_gnn_ref(x, edge_index, edge_attr, W1f, b1f, W2f, b2f, W1b, b1b, W2b, b2b, W1n, b1n, W2n, b2n):
        import jax, jax.numpy as jnp
        import numpy as np
        N_NODES = 50000
        N_EDGES = 25000
        D_NODE = 32
        D_EDGE = 16
        H = 64
        F_OUT = 32
        N_OUT = 32

        def _mlp_params(key, d_in, d_h, d_out):
            k1, k2 = jax.random.split(key)
            s1 = 1.0 / np.sqrt(d_in)
            s2 = 1.0 / np.sqrt(d_h)
            return (jax.random.uniform(k1, (d_in, d_h), jnp.float32, -s1, s1), jnp.zeros((d_h,), jnp.float32), jax.random.uniform(k2, (d_h, d_out), jnp.float32, -s2, s2), jnp.zeros((d_out,), jnp.float32))

        def _mlp(h, W1, b1, W2, b2):
            return jax.nn.relu(jax.nn.relu(h @ W1 + b1) @ W2 + b2)
        past, future = (edge_index[0], edge_index[1])
        x_past = x[past]
        x_future = x[future]
        fwd_in = jnp.concatenate([x_future, x_past, edge_attr], axis=1)
        flow_fwd = _mlp(fwd_in, W1f, b1f, W2f, b2f)
        fwd_agg = jax.ops.segment_sum(flow_fwd, future, num_segments=x.shape[0])
        bwd_in = jnp.concatenate([x_past, x_future, edge_attr], axis=1)
        flow_bwd = _mlp(bwd_in, W1b, b1b, W2b, b2b)
        bwd_agg = jax.ops.segment_sum(flow_bwd, past, num_segments=x.shape[0])
        flow_total = jnp.concatenate([fwd_agg, bwd_agg], axis=1)
        return _mlp(flow_total, W1n, b1n, W2n, b2n)
    edge_index = jnp.stack([src, dst])
    x = _layernorm(x + _L0_gnn_ref(x, edge_index, 3), axis=-1)
    x = _layernorm(x + _L1_gnn_ref(x, edge_index, edge_attr_16, L1_gnn_W1f, L1_gnn_b1f, L1_gnn_W2f, L1_gnn_b2f, L1_gnn_W1b, L1_gnn_b1b, L1_gnn_W2b, L1_gnn_b2b, L1_gnn_W1n, L1_gnn_b1n, L1_gnn_W2n, L1_gnn_b2n), axis=-1)
    return x

_drawn_inputs = setup_inputs


def setup_inputs(seed=0):
    import zlib

    import numpy as np

    out = dict(_drawn_inputs(seed))
    spreads = {'L1_gnn_b1f': (0.0, 0.8),
     'L1_gnn_b2f': (0.0, 2.0),
     'L1_gnn_b1b': (0.0, 0.8),
     'L1_gnn_b2b': (0.0, 2.0),
     'L1_gnn_b1n': (0.0, 0.298),
     'L1_gnn_b2n': (0.0, 0.1)}
    factors = {'edge_attr_16': 8.0,
     'L1_gnn_W1f': 5.656,
     'L1_gnn_W2f': 4.423,
     'L1_gnn_W1b': 6.071,
     'L1_gnn_W2b': 4.515,
     'L1_gnn_W1n': 3.171}
    for name, (base, spread) in spreads.items():
        noise = np.random.default_rng([zlib.crc32(name.encode()), seed]).standard_normal(out[name].shape)
        drawn = base * np.exp(spread * noise) if base else spread * noise
        out[name] = jnp.asarray(drawn.astype(out[name].dtype))
    for name, factor in factors.items():
        out[name] = (out[name] * factor).astype(out[name].dtype)
    return out
```

```python
from contextlib import ExitStack

import concourse.bass as bass
from concourse import mybir

ALU = mybir.AluOpType
ACT = mybir.ActivationFunctionType
F32 = mybir.dt.float32
I32 = mybir.dt.int32
U32 = mybir.dt.uint32
AX = mybir.AxisListType.X

P = 128
U = 4
Q = 16
EPS = 1e-5


def hold(eng, sem, value):
    if isinstance(value, int):
        if value > 0:
            eng.wait_ge(sem, value)
        return
    eng.wait_ge(sem, value)
    eng.nop(nofuse=True)


class Chain:

    def __init__(self, eng, sem, per_body):
        self.eng, self.sem, self.per_body = eng, sem, per_body
        self.base, self.k = 0, 0

    def body(self, n):
        assert self.k in (0, self.per_body), self.k
        self.base, self.k = n * self.per_body, 0

    def step(self, ins):
        self.k += 1
        ins.then_inc(self.sem, 1)
        hold(self.eng, self.sem, self.base + self.k)


def over(eng, count, body):
    last = 2 if count % 2 == 0 else 1
    pairs = (count - 2 - last) // 2
    body(0, 0, 0)
    body(1, 1, 0)
    with eng.Fori(0, pairs) as i:
        body(i * 2 + 2, 0, i + 1)
        body(i * 2 + 3, 1, i + 1)
    for c in range(count - last, count):
        body(c, c % 2, c // 2)


def gnn(nc, x, src, dst, edge_attr, W1f, b1f, W2f, b2f, W1b, b1b, W2b, b2b, W1n, b1n, W2n, b2n, out):
    N, D = x.shape
    E = src.shape[0]
    DE = edge_attr.shape[1]
    H = W1f.shape[1]
    CE = P * U
    NCH = -(-E // CE)
    NCH += NCH % 2
    PADS = NCH * CE - E
    TAILP = (E - (NCH - 1) * CE) // U
    assert TAILP * U + (NCH - 1) * CE == E and 0 < TAILP <= P
    NT = -(-(N + P + PADS) // (P * 8)) * P * 8
    NQ = P * Q
    NN = N // NQ
    TAILN = (N - NN * NQ) // Q
    assert NN % 2 == 0 and TAILN * Q + NN * NQ == N and 0 < TAILN < P
    F = 2 * D + DE
    W0 = D + 1

    def dram(name, shape, dt):
        return nc.dram_tensor(name, shape, dt).ap()

    pad_ids = [dram("src_padded", [NCH * CE], I32), dram("dst_padded", [NCH * CE], I32)]
    table = [dram("sums0", [NT, 2 * W0], F32), dram("sums1", [NT, 2 * D], F32), dram("sums2", [NT, 2 * D], F32)]
    flows = dram("flows", [NT, 2 * D], F32)
    y_table = dram("y_table", [N, D], F32)

    with ExitStack() as ctx:
        def sb(name, shape, dt=F32):
            return ctx.enter_context(nc.sbuf_tensor(name, shape, dt))

        def sem(name):
            return ctx.enter_context(nc.semaphore(name))

        bank = [ctx.enter_context(nc.psum_tensor(f"bank{i}", [P, 512], F32)) for i in range(8)]

        ident = sb("ident", [P, P])
        before = sb("before", [P, U, P])
        trash = sb("trash", [P, 1])
        half = sb("half", [P, U])
        pad_row = sb("pad_row", [1, PADS], I32)
        zeros = sb("zeros", [P, 2 * NT // P])
        col = [sb("src_col", [P, NCH, U], I32), sb("dst_col", [P, NCH, U], I32)]
        get = [sb("src_get", [P, NCH, U], I32), sb("dst_get", [P, NCH, U], I32)]
        put_dst = sb("put_dst", [P, NCH, U], I32)
        rden = sb("rden", [P, NCH, U])
        eps = sb("eps", [P, 1])
        ones = sb("ones", [1, P])
        w1e = sb("w1e", [F, 2 * H])
        w2e = sb("w2e", [2 * H, 2 * D])
        w1n = sb("w1n", [4 * D, 2 * H])
        w2n = sb("w2n", [2 * H, 2 * D])
        b1e = sb("b1e", [2 * H, 1])
        b1nn = sb("b1nn", [2 * H, 1])
        b2e = sb("b2e", [1, 2 * D])
        b2nn = sb("b2nn", [P, Q, D])

        SRC, DST = 0, 1

        consts_ready, w_clear, loaded, padded, first_zeroed = (
            sem("consts_ready"), sem("w_clear"), sem("loaded"), sem("padded"), sem("first_zeroed"))
        zeros_ready, mid, cols_ready, pad_written = sem("zeros_ready"), sem("mid"), sem("cols_ready"), sem("pad_written")
        with nc.Block() as block:
            @block.gpsimd
            def _(pool):
                nc.gpsimd.iota(pad_row[:, :], [[1, PADS]], base=N + P, channel_multiplier=0).then_inc(padded, 1)
                nc.gpsimd.iota(trash[:, :], [[0, 1]], base=N, channel_multiplier=1,
                               allow_small_or_imprecise_dtypes=True)
                nc.gpsimd.iota(half[:, :], [[0, U // 2], [1, 2]], base=0, channel_multiplier=0,
                               allow_small_or_imprecise_dtypes=True)
                nc.gpsimd.memset(ident[:, :], 0.0).then_inc(mid, 1)
                nc.gpsimd.memset(before[:, :, :], 1.0).then_inc(mid, 1)
                pool.wait_ge(mid, 2)
                nc.gpsimd.affine_select(out=ident[:, :], in_=ident[:, :], compare_op=ALU.not_equal, fill=1.0, base=0,
                                        pattern=[[-1, P]], channel_multiplier=1)
                nc.gpsimd.affine_select(out=before[:, :, :], in_=before[:, :, :], compare_op=ALU.is_gt, fill=0.0,
                                        base=0, pattern=[[0, U], [-1, P]], channel_multiplier=1
                                        ).then_inc(consts_ready, 1)

            @block.vector
            def _(dve):
                nc.vector.memset(zeros[:, :], 0.0).then_inc(zeros_ready, 1)
                for t in (w2e, w1n, w2n):
                    nc.vector.memset(t[:, :], 0.0).then_inc(w_clear, 1)
                nc.vector.memset(ones[:, :], 1.0)
                nc.vector.memset(eps[:, :], EPS)
                dve.wait_ge(cols_ready, 32)
                for k in (SRC, DST):
                    nc.vector.tensor_scalar(get[k][:, :, :], col[k][:, :, :], float(N - 1), None, ALU.min)

            @block.sync
            def _(sp):
                for k, ids in ((SRC, src), (DST, dst)):
                    sp.dma_start(pad_ids[k][0:E].rearrange("(a b) -> a b", a=16),
                                 ids.rearrange("(a b) -> a b", a=16)).then_inc(pad_written, 16)
                sp.wait_ge(padded, 1)
                for k in (SRC, DST):
                    sp.dma_start(pad_ids[k][E:].unsqueeze(0), pad_row[:, :]).then_inc(pad_written, 16)
                sp.wait_ge(pad_written, 64)
                for k in (SRC, DST):
                    sp.dma_start(col[k][:, :, :], pad_ids[k].rearrange("(c p u) -> p c u", p=P, u=U)
                                 ).then_inc(cols_ready, 16)
                sp.wait_ge(zeros_ready, 1)
                reps = W0
                sp.dma_start(table[0].rearrange("(p r) d -> p (r d)", p=P).rearrange("p (a b) -> p a b", a=reps),
                             zeros[:, :].unsqueeze(1).broadcast_to([P, reps, 2 * NT // P])).then_inc(first_zeroed, 16)
                sp.wait_ge(first_zeroed, 16)

            @block.scalar
            def _(act):
                act.wait_ge(w_clear, 3)
                for dst_t, src_t in (
                    (w1e[:, 0:H], W1f), (w1e[0:D, H:], W1b[D:2 * D, :]), (w1e[D:2 * D, H:], W1b[0:D, :]),
                    (w1e[2 * D:, H:], W1b[2 * D:, :]), (w2e[0:H, 0:D], W2f), (w2e[H:, D:], W2b),
                    (w1n[0:2 * D, 0:H], W1n), (w1n[2 * D:, H:], W1n), (w2n[0:H, 0:D], W2n), (w2n[H:, D:], W2n),
                    (b1e[0:H, :], b1f.unsqueeze(1)), (b1e[H:, :], b1b.unsqueeze(1)),
                    (b1nn[0:H, :], b1n.unsqueeze(1)), (b1nn[H:, :], b1n.unsqueeze(1)),
                    (b2e[:, 0:D], b2f.unsqueeze(0)), (b2e[:, D:], b2b.unsqueeze(0)),
                    (b2nn[:, :, :], b2n.unsqueeze(0).unsqueeze(0).broadcast_to([P, Q, D])),
                ):
                    act.dma_start(dst_t, src_t).then_inc(loaded, 16)
                act.wait_ge(loaded, 17 * 16)

        row_of = [ids.rearrange("(c e) -> c e", e=CE) for ids in pad_ids]

        def same_id(rows, k, c):
            return dict(in0=rows.rearrange("p (j u) -> p u j", u=U),
                        in1=get_col(k, c).broadcast_to([P, U, P]), op=ALU.is_equal)

        def get_col(k, c):
            return col[k][:, bass.ds(c, 1), :].rearrange("p a u -> p (a u)").unsqueeze(2)

        def layer(k):
            w_in = D if k == 0 else table[k - 1].shape[1]
            w_out = table[k].shape[1] // 2
            w_g = w_in + (k == 0)
            halves = table[k].rearrange("n (a w) -> (n a) w", a=2)
            source = x if k == 0 else table[k - 1]
            nxt = (table + [flows])[k + 1]
            zero_rows = NT // NCH // P * P
            assert zero_rows * NCH <= NT
            with ExitStack() as lctx:
                def lsb(name, shape, dt=F32):
                    return [lctx.enter_context(nc.sbuf_tensor(f"{name}{k}_{i}", shape, dt)) for i in range(2)]

                def lsem(name, n=0):
                    if n:
                        return [ctx.enter_context(nc.semaphore(f"{name}{k}_{i}")) for i in range(n)]
                    return ctx.enter_context(nc.semaphore(f"{name}{k}"))

                rows = lsb("rows", [P, CE], I32)
                same = lsb("same", [P, U, P])
                got = lsb("got", [P, U, w_g])
                vals = lsb("vals", [P, U, D]) if k else got
                sums = lsb("sums_out", [P, U, w_out])
                ix_get = lsb("ix_get", [P, U], I32)
                ix_put = lsb("ix_put", [P, U], I32)
                prod, cnt, t1 = lsb("prod", [P, U, P])[0], lsb("cnt", [P, U])[0], lsb("t1", [P, U])[0]
                rows_in, gathered, scattered = lsem("rows_in", 2), lsem("gathered", 2), lsem("scattered", 2)
                get_ready, put_ready, same_ready = lsem("get_ready"), lsem("put_ready"), lsem("same_ready")
                vals_ready, summed, sums_ready, zeroed = lsem("vals_ready"), lsem("summed"), lsem("sums_ready"), lsem("zeroed")
                dve_chain = lsem("dve_chain")
                ones_set = lsem("ones_set")

                with nc.Block() as block:
                    @block.sync
                    def _(sp):
                        per = NT // P // NCH
                        left = NT - per * P * NCH
                        w = nxt.shape[1]

                        def body(c, h, j):
                            hold(sp, same_ready, c - 1)
                            sp.dma_start(rows[h][:, :], row_of[DST][bass.ds(c, 1), :].broadcast_to([P, CE])
                                         ).then_inc(rows_in[h], 16)
                            sp.dma_start(nxt[bass.ds(c * (per * P), per * P), :].rearrange("(p r) d -> p (r d)", p=P),
                                         zeros[:, 0:per * w]).then_inc(zeroed, 16)

                        over(sp, NCH, body)
                        for r in range(NT - left, NT, P):
                            sp.dma_start(nxt[r:r + P, :], zeros[:, 0:w]).then_inc(zeroed, 16)
                        sp.wait_ge(zeroed, 16 * (NCH + left // P))

                    @block.vector
                    def _(dve):
                        chain = Chain(dve, dve_chain, (7, 4, 1)[k])
                        if k == 0:
                            for h in range(2):
                                nc.vector.memset(got[h][:, :, D:], 1.0).then_inc(ones_set, 1)

                        def stage_get(c, h):
                            nc.vector.tensor_scalar(ix_get[h][:, :], get[SRC][:, bass.ds(c, 1), :].squeeze(1), 0.0,
                                                    None, ALU.add).then_inc(get_ready, 1)

                        def body(c, h, j):
                            if isinstance(c, int) and c == 0:
                                stage_get(0, 0)
                            if not (isinstance(c, int) and c == NCH - 1):
                                hold(dve, gathered[1 - h], 16 * U * (j + h))
                                stage_get(c + 1, 1 - h)
                            chain.body(c)
                            hold(dve, rows_in[h], 16 * (j + 1))
                            hold(dve, summed, c - 1)
                            ins = nc.vector.tensor_tensor(out=same[h][:, :, :], **same_id(rows[h][:, :], DST, c))
                            ins.then_inc(same_ready, 1)
                            if k == 0:
                                hold(dve, same_ready, c + 1)
                                chain.step(nc.vector.tensor_tensor(out=prod[:, :, :], in0=same[h][:, :, :],
                                                                   in1=before[:, :, :], op=ALU.mult))
                                chain.step(nc.vector.tensor_reduce(cnt[:, :], prod[:, :, :], AX, ALU.add))
                                ids = col[DST][:, bass.ds(c, 1), :].squeeze(1)
                                chain.step(nc.vector.tensor_scalar(cnt[:, :], cnt[:, :], 1.0, None, ALU.min))
                                chain.step(nc.vector.tensor_scalar(t1[:, :], ids, -1.0, trash[:, 0:1],
                                                                   ALU.mult, ALU.add))
                                chain.step(nc.vector.tensor_tensor(out=t1[:, :], in0=t1[:, :], in1=cnt[:, :],
                                                                   op=ALU.mult))
                                chain.step(nc.vector.tensor_tensor(out=t1[:, :], in0=t1[:, :], in1=ids, op=ALU.add))
                                chain.step(nc.vector.tensor_scalar(put_dst[:, bass.ds(c, 1), :].squeeze(1), t1[:, :],
                                                                   2.0, None, ALU.mult))
                            else:
                                hold(dve, gathered[h], 16 * U * (j + 1))
                                hold(dve, summed, c - 1)
                                g = got[h][:, :, :]
                                o = w_in // 2
                                r = rden[:, bass.ds(c, 1), :].squeeze(1)
                                hold(dve, vals_ready, c)
                                if k == 1:
                                    chain.step(nc.vector.tensor_tensor(
                                        out=cnt[:, :].unsqueeze(2), in0=g[:, :, D:D + 1], in1=g[:, :, o + D:o + D + 1],
                                        op=ALU.add))
                                    chain.step(nc.vector.tensor_scalar(t1[:, :], cnt[:, :], 1.0, None, ALU.max))
                                    chain.step(nc.vector.reciprocal(cnt[:, :], t1[:, :]))
                                    nc.vector.tensor_scalar(r, cnt[:, :], 1.0, None, ALU.mult)
                                    r = cnt[:, :]
                                chain.step(nc.vector.tensor_tensor(out=vals[h][:, :, :], in0=g[:, :, 0:D],
                                                                   in1=g[:, :, o:o + D], op=ALU.add))
                                nc.vector.tensor_tensor(out=vals[h][:, :, :], in0=vals[h][:, :, :],
                                                        in1=r.unsqueeze(2).broadcast_to([P, U, D]),
                                                        op=ALU.mult).then_inc(vals_ready, 1)
                            for a in range(2):
                                hold(dve, scattered[a], 16 * (U // 2) * (c - 1))
                            nc.vector.tensor_tensor(out=ix_put[h][:, :], in0=put_dst[:, bass.ds(c, 1), :].squeeze(1),
                                                    in1=half[:, :], op=ALU.add).then_inc(put_ready, 1)

                        over(dve, NCH, body)

                    @block.gpsimd
                    def _(pool):
                        if k == 0:
                            pool.wait_ge(ones_set, 2)

                        def body(s, h, j, gather=True, scatter=True):
                            if gather:
                                hold(pool, get_ready, s + 1)
                                hold(pool, vals_ready if k else summed, s - 1)
                            if scatter:
                                hold(pool, put_ready, s - 1)
                                hold(pool, sums_ready, s - 1)
                            for u in range(U):
                                if gather:
                                    pool.indirect_dma_start(
                                        got[h][:, u, 0:w_in], None, source,
                                        bass.IndirectOffsetOnAxis(ix_get[h][:, u:u + 1].bitcast(U32), 0)
                                    ).then_inc(gathered[h], 16)
                                if scatter:
                                    hold(pool, scattered[u % 2], 16 * ((U // 2) * (s - 2) + u // 2))
                                    pool.indirect_dma_start(
                                        halves, bass.IndirectOffsetOnAxis(ix_put[h][:, u:u + 1].bitcast(U32), 0),
                                        sums[h][:, u, :], None, compute_op=ALU.add).then_inc(scattered[u % 2], 16)

                        body(0, 0, 0, scatter=False)
                        body(1, 1, 0, scatter=False)
                        body(2, 0, 1)
                        body(3, 1, 1)
                        with pool.Fori(0, (NCH - 4) // 2) as i:
                            body(i * 2 + 4, 0, i + 2)
                            body(i * 2 + 5, 1, i + 2)
                        body(NCH, 0, NCH // 2, gather=False)
                        body(NCH + 1, 1, NCH // 2, gather=False)
                        for a in range(2):
                            pool.wait_ge(scattered[a], 16 * (U // 2) * NCH)

                    @block.tensor
                    def _(pe):
                        if k == 0:
                            pe.wait_ge(ones_set, 2)

                        def body(c, h, j):
                            hold(pe, same_ready, c + 1)
                            if k:
                                hold(pe, vals_ready, c + 1)
                            else:
                                hold(pe, gathered[h], 16 * U * (j + 1))
                            hold(pe, sums_ready, c - 1)
                            for u in range(U):
                                ins = nc.tensor.matmul(bank[h][:, u * w_out:(u + 1) * w_out], same[h][:, u, :],
                                                       vals[h][:, u, :], start=True, stop=True)
                            ins.then_inc(summed, 1)

                        over(pe, NCH, body)

                    @block.scalar
                    def _(act):
                        def body(c, h, j):
                            hold(act, summed, c + 1)
                            for a in range(2):
                                hold(act, scattered[a], 16 * (U // 2) * (c - 1))
                            nc.scalar.copy(sums[h][:, :, :], bank[h][:, 0:U * w_out].rearrange(
                                "p (u w) -> p u w", u=U)).then_inc(sums_ready, 1)

                        over(act, NCH, body)

        for k in range(3):
            layer(k)

        def node_views(t, width):
            main = t[0:NN * NQ, :].rearrange("(c p q) d -> c p (q d)", p=P, q=Q)
            tail = t[NN * NQ:N, :].rearrange("(p q) d -> p (q d)", q=Q)

            def view(c, parts):
                return tail if parts < P else main[bass.ds(c, 1), :, :].squeeze(0)
            return view

        def over_nodes(eng, body):
            body(0, 0, 0, P)
            body(1, 1, 0, P)
            with eng.Fori(0, NN // 2 - 1) as i:
                body(i * 2 + 2, 0, i + 1, P)
                body(i * 2 + 3, 1, i + 1, P)
            body(NN, 0, NN // 2, TAILN)

        with ExitStack() as lctx:
            def pair(name, shape, dt=F32):
                return [lctx.enter_context(nc.sbuf_tensor(f"{name}_{i}", shape, dt)) for i in range(2)]

            xb, ta, tb, tc = pair("xb", [P, Q, D]), pair("ta", [P, Q, 2 * W0]), pair("tb", [P, Q, 2 * D]), pair("tc", [P, Q, 2 * D])
            tbc, z, sq = pair("tbc", [P, Q, 2 * D]), pair("z", [P, Q, D]), pair("sq", [P, Q, D])
            s0, yo = pair("s0", [P, Q, D])[0], pair("yo", [P, Q, D])
            q1, q2, mean, var, rs = (pair(n, [P, Q]) for n in ("q1", "q2", "mean", "var", "rs"))
            nodes_in, y_out = [sem("nodes_in0"), sem("nodes_in1")], [sem("y_out0"), sem("y_out1")]
            later_summed, z_ready, sq_ready, var_ready, rs_ready, y_ready, ych = (
                sem("later_summed"), sem("z_ready"), sem("sq_ready"), sem("var_ready"), sem("rs_ready"),
                sem("y_ready"), sem("ych"))
            views = [node_views(t, 0) for t in (x, table[0], table[1], table[2])]
            y_view = node_views(y_table, D)
            with nc.Block() as block:
                @block.sync
                def _(sp):
                    def body(c, h, j, parts):
                        hold(sp, y_ready, c - 1)
                        for b, v in zip((xb, ta, tb, tc), views):
                            sp.dma_start(b[h][0:parts, :, :].rearrange("p q d -> p (q d)"), v(c, parts)
                                         ).then_inc(nodes_in[h], 16)

                    over_nodes(sp, body)

                @block.gpsimd
                def _(pool):
                    def body(c, h, j, parts):
                        hold(pool, nodes_in[h], 64 * (j + 1))
                        hold(pool, y_ready, c - 1)
                        nc.gpsimd.tensor_tensor(out=tbc[h][0:parts, :, :], in0=tb[h][0:parts, :, :],
                                                in1=tc[h][0:parts, :, :], op=ALU.add).then_inc(later_summed, 1)

                    over_nodes(pool, body)

                @block.vector
                def _(dve):
                    chain = Chain(dve, ych, 10)
                    v = nc.vector

                    def body(c, h, j, parts):
                        chain.body(c)
                        s = slice(0, parts)

                        def wide(t):
                            return t.unsqueeze(2).broadcast_to([parts, Q, D])
                        hold(dve, nodes_in[h], 64 * (j + 1))
                        t = ta[h][s, :, :]
                        chain.step(v.tensor_tensor(out=q1[h][s, :].unsqueeze(2), in0=t[:, :, D:W0],
                                                   in1=t[:, :, W0 + D:], op=ALU.add))
                        chain.step(v.tensor_scalar(q2[h][s, :], q1[h][s, :], 1.0, None, ALU.max))
                        chain.step(v.reciprocal(q1[h][s, :], q2[h][s, :]))
                        chain.step(v.tensor_tensor(out=s0[s, :, :], in0=t[:, :, 0:D], in1=t[:, :, W0:W0 + D], op=ALU.add))
                        hold(dve, later_summed, c + 1)
                        chain.step(v.tensor_tensor(out=s0[s, :, :], in0=s0[s, :, :], in1=tbc[h][s, :, 0:D], op=ALU.add))
                        chain.step(v.tensor_tensor(out=s0[s, :, :], in0=s0[s, :, :], in1=tbc[h][s, :, D:], op=ALU.add))
                        chain.step(v.scalar_tensor_tensor(out=s0[s, :, :], in0=s0[s, :, :], scalar=0.25,
                                                          in1=wide(q1[h][s, :]), op0=ALU.mult, op1=ALU.mult))
                        chain.step(v.scalar_tensor_tensor(out=s0[s, :, :], in0=xb[h][s, :, :], scalar=1.25,
                                                          in1=s0[s, :, :], op0=ALU.mult, op1=ALU.add))
                        chain.step(v.tensor_reduce(mean[h][s, :], s0[s, :, :], AX, ALU.add))
                        v.scalar_tensor_tensor(out=z[h][s, :, :], in0=wide(mean[h][s, :]), scalar=-1.0 / D,
                                               in1=s0[s, :, :], op0=ALU.mult, op1=ALU.add).then_inc(z_ready, 1)
                        hold(dve, sq_ready, c + 1)
                        v.tensor_reduce(var[h][s, :], sq[h][s, :, :], AX, ALU.add).then_inc(var_ready, 1)
                        hold(dve, rs_ready, c + 1)
                        chain.step(v.reciprocal(q2[h][s, :], rs[h][s, :]))
                        hold(dve, y_out[h], 16 * j)
                        v.tensor_tensor(out=yo[h][s, :, :], in0=z[h][s, :, :], in1=wide(q2[h][s, :]),
                                        op=ALU.mult).then_inc(y_ready, 1)

                    over_nodes(dve, body)

                @block.scalar
                def _(act):
                    def body(c, h, j, parts):
                        s = slice(0, parts)
                        hold(act, z_ready, c + 1)
                        nc.scalar.activation(sq[h][s, :, :], z[h][s, :, :], ACT.Square).then_inc(sq_ready, 1)
                        hold(act, var_ready, c + 1)
                        nc.scalar.activation(rs[h][s, :], var[h][s, :], ACT.Sqrt, bias=eps[s, 0:1],
                                             scale=1.0 / D).then_inc(rs_ready, 1)
                        hold(act, y_ready, c + 1)
                        act.dma_start(y_view(c, parts), yo[h][s, :, :].rearrange("p q d -> p (q d)")
                                      ).then_inc(y_out[h], 16)

                    over_nodes(act, body)
                    act.wait_ge(y_out[0], 16 * (NN // 2 + 1))
                    act.wait_ge(y_out[1], 16 * (NN // 2))

        with ExitStack() as lctx:
            def pair(name, shape, dt=F32):
                return [lctx.enter_context(nc.sbuf_tensor(f"{name}_{i}", shape, dt)) for i in range(2)]

            rows = [pair("e_rows_src", [P, CE], I32), pair("e_rows_dst", [P, CE], I32)]
            same = [pair("e_same_src", [P, U, P]), pair("e_same_dst", [P, U, P])]
            feat, feat_t, hid = pair("feat", [P, U, F]), pair("feat_t", [F, CE]), pair("hid", [2 * H, CE])
            flow, sums = pair("flow", [P, U, 2 * D]), pair("e_sums", [P, U, 2 * D])
            prod, cnt, t1 = pair("e_prod", [P, U, P])[0], pair("e_cnt", [P, U])[0], pair("e_t1", [P, U])[0]
            ix_get = [pair("e_get_src", [P, U], I32), pair("e_get_dst", [P, U], I32)]
            ix_put = [pair("e_put_src", [P, U], I32), pair("e_put_dst", [P, U], I32)]
            rows_in, attrs_in, gathered = ([sem(f"{n}{h}") for h in range(2)] for n in ("e_rows_in", "e_attrs_in", "e_gathered"))
            scattered = [sem("e_scattered_src"), sem("e_scattered_dst")]
            (get_ready, put_ready, same_ready, turned, turned_out, hid_mm, hid_ready, flow_mm, flow_ready, summed,
             sums_ready, ech) = (sem(f"e_{n}") for n in (
                 "get_ready", "put_ready", "same_ready", "turned", "turned_out", "hid_mm", "hid_ready", "flow_mm",
                 "flow_ready", "summed", "sums_ready", "chain"))
            flow_rows = flows.rearrange("n (a w) -> (n a) w", a=2)
            attr_main = edge_attr[0:(NCH - 1) * CE, :].rearrange("(c p u) d -> c p u d", p=P, u=U)
            attr_tail = edge_attr[(NCH - 1) * CE:E, :].rearrange("(p u) d -> p u d", u=U)
            with nc.Block() as block:
                @block.sync
                def _(sp):
                    def body(c, h, j):
                        hold(sp, same_ready, c - 1)
                        for k in (SRC, DST):
                            sp.dma_start(rows[k][h][:, :], row_of[k][bass.ds(c, 1), :].broadcast_to([P, CE])
                                         ).then_inc(rows_in[h], 16)
                        hold(sp, turned, c - 1)
                        if isinstance(c, int) and c == NCH - 1:
                            sp.dma_start(feat[h][0:TAILP, :, 2 * D:], attr_tail).then_inc(attrs_in[h], 16)
                        else:
                            sp.dma_start(feat[h][:, :, 2 * D:], attr_main[bass.ds(c, 1), :, :, :].squeeze(0)
                                         ).then_inc(attrs_in[h], 16)

                    over(sp, NCH, body)

                @block.gpsimd
                def _(pool):
                    def body(s, h, j, gather=True, scatter=True):
                        if gather:
                            hold(pool, get_ready, s + 1)
                            hold(pool, turned, s - 1)
                        if scatter:
                            hold(pool, put_ready, s - 1)
                            hold(pool, sums_ready, s - 1)
                        for u in range(U):
                            for k, at in ((DST, 0), (SRC, D)):
                                if gather:
                                    pool.indirect_dma_start(
                                        feat[h][:, u, at:at + D], None, y_table,
                                        bass.IndirectOffsetOnAxis(ix_get[k][h][:, u:u + 1].bitcast(U32), 0)
                                    ).then_inc(gathered[h], 16)
                            for k, at in ((DST, 0), (SRC, D)):
                                if scatter:
                                    hold(pool, scattered[k], 16 * (U * (s - 2) + u))
                                    pool.indirect_dma_start(
                                        flow_rows, bass.IndirectOffsetOnAxis(ix_put[k][h][:, u:u + 1].bitcast(U32), 0),
                                        sums[h][:, u, at:at + D], None, compute_op=ALU.add).then_inc(scattered[k], 16)

                    body(0, 0, 0, scatter=False)
                    body(1, 1, 0, scatter=False)
                    body(2, 0, 1)
                    body(3, 1, 1)
                    with pool.Fori(0, (NCH - 4) // 2) as i:
                        body(i * 2 + 4, 0, i + 2)
                        body(i * 2 + 5, 1, i + 2)
                    body(NCH, 0, NCH // 2, gather=False)
                    body(NCH + 1, 1, NCH // 2, gather=False)
                    for k in (SRC, DST):
                        pool.wait_ge(scattered[k], 16 * U * NCH)

                @block.vector
                def _(dve):
                    chain = Chain(dve, ech, 6)
                    v = nc.vector

                    def stage_get(c, h):
                        for k in (SRC, DST):
                            ins = v.tensor_scalar(ix_get[k][h][:, :], get[k][:, bass.ds(c, 1), :].squeeze(1), 0.0,
                                                  None, ALU.add)
                        ins.then_inc(get_ready, 1)

                    def body(c, h, j):
                        if isinstance(c, int) and c == 0:
                            stage_get(0, 0)
                        if not (isinstance(c, int) and c == NCH - 1):
                            hold(dve, gathered[1 - h], 32 * U * (j + h))
                            stage_get(c + 1, 1 - h)
                        chain.body(c)
                        hold(dve, rows_in[h], 32 * (j + 1))
                        hold(dve, summed, c - 1)
                        v.tensor_tensor(out=same[DST][h][:, :, :], **same_id(rows[DST][h][:, :], DST, c))
                        v.tensor_tensor(out=same[SRC][h][:, :, :], **same_id(rows[SRC][h][:, :], SRC, c)
                                        ).then_inc(same_ready, 1)
                        hold(dve, same_ready, c + 1)
                        ids = col[SRC][:, bass.ds(c, 1), :].squeeze(1)
                        hold(dve, put_ready, c)
                        chain.step(v.tensor_tensor(out=prod[:, :, :], in0=same[SRC][h][:, :, :], in1=before[:, :, :],
                                                   op=ALU.mult))
                        chain.step(v.tensor_reduce(cnt[:, :], prod[:, :, :], AX, ALU.add))
                        chain.step(v.tensor_scalar(cnt[:, :], cnt[:, :], 1.0, None, ALU.min))
                        chain.step(v.tensor_scalar(t1[:, :], ids, -1.0, trash[:, 0:1], ALU.mult, ALU.add))
                        chain.step(v.tensor_tensor(out=t1[:, :], in0=t1[:, :], in1=cnt[:, :], op=ALU.mult))
                        chain.step(v.tensor_tensor(out=t1[:, :], in0=t1[:, :], in1=ids, op=ALU.add))
                        for k in (SRC, DST):
                            hold(dve, scattered[k], 16 * U * (c - 1))
                        v.tensor_scalar(ix_put[SRC][h][:, :], t1[:, :], 2.0, 1.0, ALU.mult, ALU.add)
                        v.tensor_scalar(ix_put[DST][h][:, :], put_dst[:, bass.ds(c, 1), :].squeeze(1), 0.0, None,
                                        ALU.add).then_inc(put_ready, 1)
                        hold(dve, flow_mm, c + 1)
                        v.tensor_scalar(flow[h][:, :, :], bank[4 + h][:, 0:U * 2 * D].rearrange(
                            "p (u w) -> p u w", u=U), 0.0, None, ALU.max).then_inc(flow_ready, 1)

                    over(dve, NCH, body)

                @block.tensor
                def _(pe):
                    def body(c, h, j):
                        hold(pe, gathered[h], 32 * U * (j + 1))
                        hold(pe, attrs_in[h], 16 * (j + 1))
                        hold(pe, turned_out, c - 1)
                        for u in range(U):
                            ins = nc.tensor.transpose(bank[h][0:F, u * P:(u + 1) * P], feat[h][:, u, :], ident[:, :])
                        ins.then_inc(turned, 1)
                        hold(pe, turned_out, c + 1)
                        hold(pe, hid_ready, c - 1)
                        nc.tensor.matmul(bank[2 + h][:, :], w1e[:, :], feat_t[h][:, :], start=True, stop=True
                                         ).then_inc(hid_mm, 1)
                        hold(pe, hid_ready, c + 1)
                        hold(pe, flow_ready, c - 1)
                        for u in range(U):
                            o = bank[4 + h][:, u * 2 * D:(u + 1) * 2 * D]
                            nc.tensor.matmul(o, hid[h][:, u * P:(u + 1) * P], w2e[:, :], start=True, stop=False)
                            ins = nc.tensor.matmul(o, ones[:, :], b2e[:, :], start=False, stop=True)
                        ins.then_inc(flow_mm, 1)
                        hold(pe, flow_ready, c + 1)
                        hold(pe, same_ready, c + 1)
                        hold(pe, sums_ready, c - 1)
                        for u in range(U):
                            for k, at in ((DST, 0), (SRC, D)):
                                ins = nc.tensor.matmul(bank[6 + h][:, u * 2 * D + at:u * 2 * D + at + D],
                                                       same[k][h][:, u, :], flow[h][:, u, at:at + D],
                                                       start=True, stop=True)
                        ins.then_inc(summed, 1)

                    over(pe, NCH, body)

                @block.scalar
                def _(act):
                    def body(c, h, j):
                        hold(act, turned, c + 1)
                        hold(act, hid_mm, c - 1)
                        nc.scalar.copy(feat_t[h][:, :], bank[h][0:F, :]).then_inc(turned_out, 1)
                        hold(act, hid_mm, c + 1)
                        hold(act, flow_mm, c - 1)
                        nc.scalar.activation(hid[h][:, :], bank[2 + h][:, :], ACT.Relu, bias=b1e[:, 0:1]
                                             ).then_inc(hid_ready, 1)
                        hold(act, summed, c + 1)
                        for k in (SRC, DST):
                            hold(act, scattered[k], 16 * U * (c - 1))
                        nc.scalar.copy(sums[h][:, :, :], bank[6 + h][:, 0:U * 2 * D].rearrange(
                            "p (u w) -> p u w", u=U)).then_inc(sums_ready, 1)

                    over(act, NCH, body)

        with ExitStack() as lctx:
            def pair(name, shape, dt=F32):
                return [lctx.enter_context(nc.sbuf_tensor(f"{name}_{i}", shape, dt)) for i in range(2)]

            HC = 512
            yb, fb = pair("yb", [P, Q, D]), pair("fb", [P, Q, 2 * D])
            flow_t, hid = pair("flow_t", [P, 2 * HC]), pair("n_hid", [P, 2 * HC])
            s0, z, sq, res = pair("n_s0", [P, Q, D])[0], pair("n_z", [P, Q, D]), pair("n_sq", [P, Q, D]), pair("res", [P, Q, D])
            q2, mean, var, rs = (pair(n, [P, Q]) for n in ("n_q2", "n_mean", "n_var", "n_rs"))
            nodes_in, res_out = [sem("f_in0"), sem("f_in1")], [sem("res_out0"), sem("res_out1")]
            (turned, turned_out, hid_mm, hid_ready, out_mm, z_ready, sq_ready, var_ready, rs_ready, res_ready, nch
             ) = (sem(f"n_{n}") for n in ("turned", "turned_out", "hid_mm", "hid_ready", "out_mm", "z_ready",
                                                  "sq_ready", "var_ready", "rs_ready", "res_ready", "chain"))
            y_view, flow_view, out_view = node_views(y_table, D), node_views(flows, 2 * D), node_views(out, D)
            with nc.Block() as block:
                @block.sync
                def _(sp):
                    def body(c, h, j, parts):
                        hold(sp, z_ready, c - 1)
                        sp.dma_start(yb[h][0:parts, :, :].rearrange("p q d -> p (q d)"), y_view(c, parts)
                                     ).then_inc(nodes_in[h], 16)
                        sp.dma_start(fb[h][0:parts, :, :].rearrange("p q d -> p (q d)"), flow_view(c, parts)
                                     ).then_inc(nodes_in[h], 16)

                    over_nodes(sp, body)

                @block.tensor
                def _(pe):
                    def body(c, h, j, parts):
                        hold(pe, nodes_in[h], 32 * (j + 1))
                        for g in range(2):
                            hold(pe, turned_out, 2 * c + g - 1)
                            for m in range(4):
                                q = 8 * g + 2 * m
                                ins = nc.tensor.transpose(
                                    bank[g][:, m * P:m * P + parts],
                                    fb[h][0:parts, q:q + 2, :].rearrange("p q d -> p (q d)"), ident[0:parts, 0:parts])
                            ins.then_inc(turned, 1)
                        for g in range(2):
                            hold(pe, turned_out, 2 * c + g + 1)
                            hold(pe, hid_ready, 2 * c + g - 1)
                            ft = flow_t[h][:, g * HC:(g + 1) * HC].rearrange("p (m n) -> p m n", m=4)[:, :, 0:parts]
                            o = bank[2 + g][:, :].rearrange("p (m n) -> p m n", m=4)[:, :, 0:parts]
                            nc.tensor.matmul(o, w1n[:, :], ft, start=True, stop=True).then_inc(hid_mm, 1)
                        hold(pe, z_ready, c - 1)
                        for g in range(2):
                            hold(pe, hid_ready, 2 * c + g + 1)
                            for m in range(4):
                                col0 = g * HC + m * P
                                o = (4 * g + m) * 2 * D
                                ins = nc.tensor.matmul(bank[4 + h][0:parts, o:o + 2 * D],
                                                       hid[h][:, col0:col0 + parts], w2n[:, :], start=True, stop=True)
                        ins.then_inc(out_mm, 1)

                    over_nodes(pe, body)

                @block.scalar
                def _(act):
                    def strip(t, parts):
                        return t.rearrange("p (m n) -> p m n", m=4)[:, :, 0:parts]

                    def body(c, h, j, parts):
                        s = slice(0, parts)
                        hold(act, out_mm, c - 1)
                        for g in range(2):
                            hold(act, turned, 2 * c + g + 1)
                            nc.scalar.copy(strip(flow_t[h][:, g * HC:(g + 1) * HC], parts), strip(bank[g][:, :], parts)
                                           ).then_inc(turned_out, 1)
                        for g in range(2):
                            hold(act, hid_mm, 2 * c + g + 1)
                            nc.scalar.activation(strip(hid[h][:, g * HC:(g + 1) * HC], parts),
                                                 strip(bank[2 + g][:, :], parts), ACT.Relu,
                                                 bias=b1nn[:, 0:1]).then_inc(hid_ready, 1)
                        hold(act, z_ready, c + 1)
                        nc.scalar.activation(sq[h][s, :, :], z[h][s, :, :], ACT.Square).then_inc(sq_ready, 1)
                        hold(act, var_ready, c + 1)
                        nc.scalar.activation(rs[h][s, :], var[h][s, :], ACT.Sqrt, bias=eps[s, 0:1],
                                             scale=1.0 / D).then_inc(rs_ready, 1)

                    over_nodes(act, body)

                @block.vector
                def _(dve):
                    chain = Chain(dve, nch, 4)
                    v = nc.vector

                    def body(c, h, j, parts):
                        chain.body(c)
                        s = slice(0, parts)

                        def wide(t):
                            return t.unsqueeze(2).broadcast_to([parts, Q, D])
                        hold(dve, out_mm, c + 1)
                        hold(dve, nodes_in[h], 32 * (j + 1))
                        chain.step(v.tensor_tensor(out=s0[s, :, :], in0=bank[4 + h][s, :].rearrange(
                            "p (q d) -> p q d", d=D), in1=b2nn[s, :, :], op=ALU.add))
                        chain.step(v.scalar_tensor_tensor(out=s0[s, :, :], in0=s0[s, :, :], scalar=0.0,
                                                          in1=yb[h][s, :, :], op0=ALU.max, op1=ALU.add))
                        chain.step(v.tensor_reduce(mean[h][s, :], s0[s, :, :], AX, ALU.add))
                        v.scalar_tensor_tensor(out=z[h][s, :, :], in0=wide(mean[h][s, :]), scalar=-1.0 / D,
                                               in1=s0[s, :, :], op0=ALU.mult, op1=ALU.add).then_inc(z_ready, 1)
                        hold(dve, sq_ready, c + 1)
                        v.tensor_reduce(var[h][s, :], sq[h][s, :, :], AX, ALU.add).then_inc(var_ready, 1)
                        hold(dve, rs_ready, c + 1)
                        chain.step(v.reciprocal(q2[h][s, :], rs[h][s, :]))
                        hold(dve, res_out[h], 16 * j)
                        v.tensor_tensor(out=res[h][s, :, :], in0=z[h][s, :, :], in1=wide(q2[h][s, :]),
                                        op=ALU.mult).then_inc(res_ready, 1)

                    over_nodes(dve, body)

                @block.gpsimd
                def _(pool):
                    def body(c, h, j, parts):
                        hold(pool, res_ready, c + 1)
                        pool.dma_start(out_view(c, parts), res[h][0:parts, :, :].rearrange("p q d -> p (q d)")
                                       ).then_inc(res_out[h], 16)

                    over_nodes(pool, body)
                    pool.wait_ge(res_out[0], 16 * (NN // 2 + 1))
                    pool.wait_ge(res_out[1], 16 * (NN // 2))


_INS = ['x', 'src', 'dst', 'edge_attr_16', 'L1_gnn_W1f', 'L1_gnn_b1f', 'L1_gnn_W2f', 'L1_gnn_b2f', 'L1_gnn_W1b',
        'L1_gnn_b1b', 'L1_gnn_W2b', 'L1_gnn_b2b', 'L1_gnn_W1n', 'L1_gnn_b1n', 'L1_gnn_W2n', 'L1_gnn_b2n']


def kernel(**inputs):
    import numpy as _np
    import concourse.bacc as _bacc
    from concourse import mybir as _mybir
    from concourse.bass_utils import run_bass_kernel_spmd as _run

    nc = _bacc.Bacc("TRN2", target_bir_lowering=False, num_devices=1)
    arrays, args = {}, []
    for name in _INS:
        a = _np.ascontiguousarray(inputs[name])
        arrays[f"in_{name}_dram"] = a
        args.append(nc.dram_tensor(f"in_{name}_dram", a.shape, _mybir.dt.from_np(a.dtype), kind="ExternalInput").ap())
    out = nc.dram_tensor("out_dram", inputs['x'].shape, _mybir.dt.float32, kind="ExternalOutput").ap()
    gnn(nc, *args, out)
    r = _run(nc, [arrays], core_ids=[0])
    return r.results[0]["out_dram"]
```

```python
from contextlib import ExitStack

import concourse.bass as bass
from concourse import mybir

ALU = mybir.AluOpType
ACT = mybir.ActivationFunctionType
F32 = mybir.dt.float32
I32 = mybir.dt.int32
U32 = mybir.dt.uint32
F16 = mybir.dt.float16
BF16 = mybir.dt.bfloat16
AX = mybir.AxisListType.X

P = 128
U = 4
Q = 16
EPS = 1e-5


def hold(eng, sem, value, alone=False):
    if isinstance(value, int):
        if value > 0:
            eng.wait_ge(sem, value)
        return
    eng.wait_ge(sem, value)
    if alone:
        eng.nop(nofuse=True)


def pool_hold(pool, sem, value):
    hold(pool, sem, value, alone=True)


class Chain:

    def __init__(self, eng, sem, per_body):
        self.eng, self.sem, self.per_body = eng, sem, per_body
        self.base, self.k = 0, 0

    def body(self, n):
        assert self.k in (0, self.per_body), self.k
        self.base, self.k = n * self.per_body, 0

    def step(self, ins):
        self.k += 1
        ins.then_inc(self.sem, 1)
        hold(self.eng, self.sem, self.base + self.k)


def over(eng, count, body, first=2):
    last = 2 if count % 2 == 0 else 1
    for c in range(first):
        body(c, c % 2, c // 2)
    with eng.Fori(0, (count - first - last) // 2) as i:
        body(i * 2 + first, 0, i + first // 2)
        body(i * 2 + first + 1, 1, i + first // 2)
    for c in range(count - last, count):
        body(c, c % 2, c // 2)


def over4(eng, count, body, first=6):
    last = (count - first) % 4 or 4
    for c in range(first):
        body(c, c % 2, c // 2, c % 4, c // 4)
    with eng.Fori(0, (count - first - last) // 4) as i:
        for c in range(first, first + 4):
            body(i * 4 + c, c % 2, i * 2 + c // 2, c % 4, i + c // 4)
    for c in range(count - last, count):
        body(c, c % 2, c // 2, c % 4, c // 4)


def each(eng, count, body):
    body(0)
    with eng.Fori(1, count - 1) as g:
        body(g)
    body(count - 1)


def gnn(nc, x, src, dst, edge_attr, W1f, b1f, W2f, b2f, W1b, b1b, W2b, b2b, W1n, b1n, W2n, b2n, out):
    N, D = x.shape
    E = src.shape[0]
    DE = edge_attr.shape[1]
    H = W1f.shape[1]
    CE = P * U
    NCH = -(-E // CE)
    NCH += NCH % 2
    TILES = NCH * U
    PADS = NCH * CE - E
    TAILT, TAILP = divmod(E - (NCH - 1) * CE, P)
    assert 0 < E - (NCH - 1) * CE and TAILP
    WB = 4
    WIN = WB * P
    GB = 16
    SLACK = 12
    BIG = float(1 << 20)
    NT = -(-(N + P + PADS) // (P * 8)) * P * 8
    NQ = P * Q
    NN = N // NQ
    TAILN = (N - NN * NQ) // Q
    assert NN % 2 == 0 and TAILN * Q + NN * NQ == N and 0 < TAILN < P
    F = 2 * D + DE
    W0 = D + 1

    def dram(name, shape, dt):
        return nc.dram_tensor(name, shape, dt).ap()

    pad_ids = [dram("src_padded", [NCH * CE], I32), dram("dst_padded", [NCH * CE], I32)]
    table = [dram("sums0", [NT, 2 * W0], F32), dram("sums1", [NT, 2 * D], F32), dram("sums2", [NT, 2 * D], F32)]
    means = [dram("means1", [NT, D], F32), dram("means2", [NT, D], F32), dram("y_nodes", [NT, D], F32)]
    NBLK = NT // P
    NG = NBLK // GB
    assert NBLK % GB == 0 and 128 * (E // NCH // U) > 0
    BPT = N * P // (E * P)
    partial = dram("partial", [NG, P, GB * D], F32)
    backward = dram("backward", [NT, D], F32)
    base_dram = dram("base_dram", [TILES], I32)
    flows = dram("flows", [NT, 2 * D], F32)
    y_table = dram("y_table", [N, D], F32)

    with ExitStack() as ctx:
        scope = [ctx]

        def sb(name, shape, dt=F32):
            return ctx.enter_context(nc.sbuf_tensor(name, shape, dt))

        def sem(name):
            return scope[-1].enter_context(nc.semaphore(name))

        bank = [ctx.enter_context(nc.psum_tensor(f"bank{i}", [P, 512], F32)) for i in range(8)]

        ident = sb("ident", [P, P])
        before = sb("before", [P, U, P])
        trash = sb("trash", [P, 1])
        half = sb("half", [P, U])
        pad_row = sb("pad_row", [1, PADS], I32)
        zeros = sb("zeros", [P, 2 * NT // P])
        col = [sb("src_col", [P, NCH, U], I32), sb("dst_col", [P, NCH, U], I32)]
        get = [sb("src_get", [P, NCH, U], I32), sb("dst_get", [P, NCH, U], I32)]
        put_dst = sb("put_dst", [P, NCH, U], I32)
        rden = sb("rden", [P, NCH, U])
        eps = sb("eps", [P, 1])
        ones = sb("ones", [1, P])
        w1e = sb("w1e", [F, 2 * H])
        w2e = sb("w2e", [2 * H, 2 * D])
        w1n = sb("w1n", [4 * D, 2 * H])
        w2n = sb("w2n", [2 * H, 2 * D])
        b1e = sb("b1e", [2 * H, 1])
        b1nn = sb("b1nn", [2 * H, 1])
        b2e = sb("b2e", [1, 2 * D])
        b2nn = sb("b2nn", [P, Q, D])
        rden_n = sb("rden_n", [P, NBLK])
        node_sums = sb("node_sums", [P, NBLK + WB, W0])
        base_row = sb("base_row", [P, TILES], I32)
        hot_at = sb("hot_at", [P, NCH, U])
        steps = sb("steps", [P, WIN], F16)
        flag = sb("flag", [1, 1], I32)

        SRC, DST = 0, 1

        consts_ready, w_clear, loaded, padded, sums_clear = (
            sem("consts_ready"), sem("w_clear"), sem("loaded"), sem("padded"), sem("sums_clear"))
        zeros_ready, mid, pad_written, nat_in, turned_ids, base_out, base_in, ich, counted = (
            sem("zeros_ready"), sem("mid"), sem("pad_written"), sem("nat_in"), sem("turned_ids"),
            sem("base_out"), sem("base_in"), sem("ids_chain"), sem("counted"))
        nat_ready, base_ready, bad_ready = sem("nat_ready"), sem("base_ready"), sem("bad_ready")
        with ExitStack() as lctx:
            def tmp(name, shape, dt=F32):
                return lctx.enter_context(nc.sbuf_tensor(name, shape, dt))

            nat = [tmp("nat_src", [NCH, CE], I32), tmp("nat_dst", [NCH, CE], I32)]
            nat_f = [tmp("nat_src_f", [NCH, CE]), tmp("nat_dst_f", [NCH, CE])]
            base_nat = tmp("base_nat", [NCH, U], I32)
            col_f = tmp("col_f", [P, NCH, U])
            rel, is_pad, low, due = (tmp(n, [P, TILES]) for n in ("rel", "is_pad", "low", "due"))
            tops, bads, bad = tmp("tops", [P, 3]), tmp("bads", [P, 3]), tmp("bad", [P, 1])
            ones_col = tmp("ones_col", [P, 1])
            HB = (NBLK + WB) // 2
            with nc.Block() as block:
                @block.gpsimd
                def _(pool):
                    nc.gpsimd.iota(pad_row[:, :], [[1, PADS]], base=N + P, channel_multiplier=0).then_inc(padded, 1)
                    nc.gpsimd.memset(ident[:, :], 0.0).then_inc(mid, 1)
                    nc.gpsimd.memset(before[:, :, :], 1.0).then_inc(mid, 1)
                    pool.wait_ge(mid, 2)
                    nc.gpsimd.affine_select(out=ident[:, :], in_=ident[:, :], compare_op=ALU.not_equal, fill=1.0,
                                            base=0, pattern=[[-1, P]], channel_multiplier=1
                                            ).then_inc(consts_ready, 1)
                    nc.gpsimd.iota(trash[:, :], [[0, 1]], base=N, channel_multiplier=1,
                                   allow_small_or_imprecise_dtypes=True)
                    nc.gpsimd.iota(half[:, :], [[0, U // 2], [1, 2]], base=0, channel_multiplier=0,
                                   allow_small_or_imprecise_dtypes=True)
                    nc.gpsimd.iota(steps[:, :], [[1, WIN]], base=0, channel_multiplier=0,
                                   allow_small_or_imprecise_dtypes=True)
                    nc.gpsimd.iota(due[:, :], [[-BPT, TILES]], base=SLACK, channel_multiplier=0,
                                   allow_small_or_imprecise_dtypes=True).then_inc(consts_ready, 1)
                    nc.gpsimd.affine_select(out=before[:, :, :], in_=before[:, :, :], compare_op=ALU.is_gt, fill=0.0,
                                            base=0, pattern=[[0, U], [-1, P]], channel_multiplier=1)
                    nc.gpsimd.memset(node_sums[:, 0:HB, :], 0.0)

                @block.vector
                def _(dve):
                    v = nc.vector
                    count = [0]

                    def step(ins):
                        count[0] += 1
                        ins.then_inc(ich, 1)
                        dve.wait_ge(ich, count[0])

                    v.memset(zeros[:, :], 0.0)
                    for t in (w2e, w1n, w2n):
                        v.memset(t[:, :], 0.0).then_inc(w_clear, 1)
                    v.memset(ones[:, :], 1.0)
                    v.memset(eps[:, :], EPS)
                    step(v.memset(ones_col[:, :], 1.0))
                    dve.wait_ge(nat_in, 32)
                    for k in (SRC, DST):
                        v.tensor_scalar(nat_f[k][:, :], nat[k][:, :], 0.0, None, ALU.add).then_inc(nat_ready, 1)
                    firsts = nat[DST][:, :].rearrange("q (a j) -> q a j", a=U)[:, :, 0:1]
                    assert P == 1 << 7
                    v.tensor_scalar(base_nat[:, :].unsqueeze(2), firsts, 7, None, ALU.arith_shift_right
                                    ).then_inc(base_ready, 1)
                    for k in (SRC, DST):
                        dve.wait_ge(turned_ids, k + 1)
                        for a in range(U):
                            ins = v.tensor_copy(col_f[:, :, a], bank[U * k + a][:, 0:NCH])
                        step(ins)
                        step(v.tensor_scalar(col[k][:, :, :], col_f[:, :, :], 0.0, None, ALU.add))
                        step(v.tensor_scalar(get[k][:, :, :], col_f[:, :, :], float(N - 1), None, ALU.min))
                    flat = col_f[:, :, :].rearrange("p c u -> p (c u)")
                    dve.wait_ge(base_in, 16)
                    step(v.scalar_tensor_tensor(out=rel[:, :], in0=base_row[:, :], scalar=float(-P), in1=flat,
                                                op0=ALU.mult, op1=ALU.add))
                    step(v.tensor_scalar(is_pad[:, :], flat, float(N), None, ALU.is_ge))
                    hot = hot_at[:, :, :].rearrange("p c u -> p (c u)")
                    step(v.scalar_tensor_tensor(out=hot, in0=is_pad[:, :], scalar=-BIG, in1=rel[:, :],
                                                op0=ALU.mult, op1=ALU.add))
                    step(v.scalar_tensor_tensor(out=low[:, :], in0=is_pad[:, :], scalar=BIG, in1=rel[:, :],
                                                op0=ALU.mult, op1=ALU.add))
                    dve.wait_ge(consts_ready, 2)
                    step(v.scalar_tensor_tensor(out=due[:, :], in0=base_row[:, :], scalar=1.0, in1=due[:, :],
                                                op0=ALU.mult, op1=ALU.add))
                    v.tensor_reduce(tops[:, 0:1], hot, AX, ALU.max)
                    v.tensor_reduce(tops[:, 1:2], low[:, :], AX, ALU.min)
                    step(v.tensor_reduce(tops[:, 2:3], due[:, :], AX, ALU.min))
                    v.tensor_scalar(bads[:, 0:1], tops[:, 0:1], float(WIN), None, ALU.is_ge)
                    step(v.tensor_scalar(bads[:, 1:3], tops[:, 1:3], 0.0, None, ALU.is_lt))
                    v.tensor_reduce(bad[:, :], bads[:, :], AX, ALU.add).then_inc(bad_ready, 1)
                    v.memset(node_sums[:, HB:, :], 0.0)
                    dve.wait_ge(counted, 1)
                    v.tensor_scalar(flag[:, :], bank[0][0:1, 0:1], 0.0, None, ALU.is_equal)

                @block.tensor
                def _(pe):
                    pe.wait_ge(consts_ready, 1)
                    for k in (SRC, DST):
                        pe.wait_ge(nat_ready, k + 1)
                        for a in range(U):
                            ins = nc.tensor.transpose(bank[U * k + a][:, 0:NCH], nat_f[k][:, a * P:(a + 1) * P],
                                                      ident[0:NCH, 0:NCH])
                        ins.then_inc(turned_ids, 1)
                    pe.wait_ge(bad_ready, 1)
                    nc.tensor.matmul(bank[0][0:1, 0:1], bad[:, :], ones_col[:, :], start=True, stop=True
                                     ).then_inc(counted, 1)

                @block.sync
                def _(sp):
                    for k, ids in ((SRC, src), (DST, dst)):
                        sp.dma_start(pad_ids[k][0:E].rearrange("(a b) -> a b", a=16),
                                     ids.rearrange("(a b) -> a b", a=16)).then_inc(pad_written, 16)
                    sp.wait_ge(padded, 1)
                    for k in (SRC, DST):
                        sp.dma_start(pad_ids[k][E:].unsqueeze(0), pad_row[:, :]).then_inc(pad_written, 16)
                    sp.wait_ge(pad_written, 64)
                    for k in (SRC, DST):
                        sp.dma_start(nat[k][:, :], pad_ids[k].rearrange("(c e) -> c e", c=NCH)).then_inc(nat_in, 16)
                    sp.wait_ge(base_ready, 1)
                    sp.dma_start(base_dram.rearrange("(q a) -> q a", a=U), base_nat[:, :]).then_inc(base_out, 16)
                    sp.wait_ge(base_out, 16)
                    sp.dma_start(base_row[:, :], base_dram.unsqueeze(0).broadcast_to([P, TILES])
                                 ).then_inc(base_in, 16)
                    sp.wait_ge(base_in, 16)

                @block.scalar
                def _(act):
                    act.wait_ge(w_clear, 3)
                    for dst_t, src_t in (
                        (w1e[:, 0:H], W1f), (w1e[0:D, H:], W1b[D:2 * D, :]), (w1e[D:2 * D, H:], W1b[0:D, :]),
                        (w1e[2 * D:, H:], W1b[2 * D:, :]), (w2e[0:H, 0:D], W2f), (w2e[H:, D:], W2b),
                        (w1n[0:2 * D, 0:H], W1n), (w1n[2 * D:, H:], W1n), (w2n[0:H, 0:D], W2n), (w2n[H:, D:], W2n),
                        (b1e[0:H, :], b1f.unsqueeze(1)), (b1e[H:, :], b1b.unsqueeze(1)),
                        (b1nn[0:H, :], b1n.unsqueeze(1)), (b1nn[H:, :], b1n.unsqueeze(1)),
                        (b2e[:, 0:D], b2f.unsqueeze(0)), (b2e[:, D:], b2b.unsqueeze(0)),
                        (b2nn[:, :, :], b2n.unsqueeze(0).unsqueeze(0).broadcast_to([P, Q, D])),
                    ):
                        act.dma_start(dst_t, src_t).then_inc(loaded, 16)
                    act.wait_ge(loaded, 17 * 16)

        def clear_first():
            first_zeroed = sem("first_zeroed")
            with nc.Block() as block:
                @block.sync
                def _(sp):
                    sp.dma_start(table[0].rearrange("(p r) d -> p (r d)", p=P).rearrange("p (a b) -> p a b", a=W0),
                                 zeros[:, :].unsqueeze(1).broadcast_to([P, W0, 2 * NT // P])
                                 ).then_inc(first_zeroed, 16)
                    sp.wait_ge(first_zeroed, 16)

        row_of = [ids.rearrange("(c e) -> c e", e=CE) for ids in pad_ids]

        def same_id(rows, k, c):
            return dict(in0=rows.rearrange("p (u j) -> p u j", u=U),
                        in1=get_col(k, c).broadcast_to([P, U, P]), op=ALU.is_equal)

        def get_col(k, c):
            return col[k][:, bass.ds(c, 1), :].rearrange("p a u -> p (a u)").unsqueeze(2)

        def layer(k):
            w_in = D if k == 0 else table[k - 1].shape[1]
            w_out = table[k].shape[1] // 2
            w_g = w_in + (k == 0)
            halves = table[k].rearrange("n (a w) -> (n a) w", a=2)
            source = x if k == 0 else table[k - 1]
            nxt = (table + [flows])[k + 1]
            zero_rows = NT // NCH // P * P
            assert zero_rows * NCH <= NT
            with ExitStack() as lctx:
                def lsb(name, shape, dt=F32):
                    return [lctx.enter_context(nc.sbuf_tensor(f"{name}{k}_{i}", shape, dt)) for i in range(2)]

                def lsem(name, n=0):
                    if n:
                        return [scope[-1].enter_context(nc.semaphore(f"{name}{k}_{i}")) for i in range(n)]
                    return scope[-1].enter_context(nc.semaphore(f"{name}{k}"))

                rows = lsb("rows", [P, CE], I32)
                same = lsb("same", [P, U, P])
                got = lsb("got", [P, U, w_g])
                vals = lsb("vals", [P, U, D]) if k else got
                sums = lsb("sums_out", [P, U, w_out])
                ix_get = lsb("ix_get", [P, U], I32)
                ix_put = lsb("ix_put", [P, U], I32)
                prod, cnt, t1 = lsb("prod", [P, U, P])[0], lsb("cnt", [P, U])[0], lsb("t1", [P, U])[0]
                rows_in, gathered, scattered = lsem("rows_in", 2), lsem("gathered", 2), lsem("scattered", 2)
                get_ready, put_ready, same_ready = lsem("get_ready"), lsem("put_ready"), lsem("same_ready")
                vals_ready, summed, sums_ready, zeroed = lsem("vals_ready"), lsem("summed"), lsem("sums_ready"), lsem("zeroed")
                dve_chain = lsem("dve_chain")
                ones_set = lsem("ones_set")

                with nc.Block() as block:
                    @block.sync
                    def _(sp):
                        per = NT // P // NCH
                        left = NT - per * P * NCH
                        w = nxt.shape[1]

                        def body(c, h, j):
                            hold(sp, same_ready, c - 1)
                            sp.dma_start(rows[h][:, :], row_of[DST][bass.ds(c, 1), :].broadcast_to([P, CE])
                                         ).then_inc(rows_in[h], 16)
                            sp.dma_start(nxt[bass.ds(c * (per * P), per * P), :].rearrange("(p r) d -> p (r d)", p=P),
                                         zeros[:, 0:per * w]).then_inc(zeroed, 16)

                        over(sp, NCH, body)
                        for r in range(NT - left, NT, P):
                            sp.dma_start(nxt[r:r + P, :], zeros[:, 0:w]).then_inc(zeroed, 16)
                        sp.wait_ge(zeroed, 16 * (NCH + left // P))

                    @block.vector
                    def _(dve):
                        chain = Chain(dve, dve_chain, (7, 4, 1)[k])
                        if k == 0:
                            for h in range(2):
                                nc.vector.memset(got[h][:, :, D:], 1.0).then_inc(ones_set, 1)

                        def stage_get(c, h):
                            nc.vector.tensor_scalar(ix_get[h][:, :], get[SRC][:, bass.ds(c, 1), :].squeeze(1), 0.0,
                                                    None, ALU.add).then_inc(get_ready, 1)

                        def body(c, h, j):
                            if isinstance(c, int) and c == 0:
                                stage_get(0, 0)
                            if not (isinstance(c, int) and c == NCH - 1):
                                hold(dve, gathered[1 - h], 16 * U * (j + h))
                                stage_get(c + 1, 1 - h)
                            chain.body(c)
                            hold(dve, rows_in[h], 16 * (j + 1))
                            hold(dve, summed, c - 1)
                            ins = nc.vector.tensor_tensor(out=same[h][:, :, :], **same_id(rows[h][:, :], DST, c))
                            ins.then_inc(same_ready, 1)
                            if k == 0:
                                hold(dve, same_ready, c + 1)
                                chain.step(nc.vector.tensor_tensor(out=prod[:, :, :], in0=same[h][:, :, :],
                                                                   in1=before[:, :, :], op=ALU.mult))
                                chain.step(nc.vector.tensor_reduce(cnt[:, :], prod[:, :, :], AX, ALU.add))
                                ids = col[DST][:, bass.ds(c, 1), :].squeeze(1)
                                chain.step(nc.vector.tensor_scalar(cnt[:, :], cnt[:, :], 1.0, None, ALU.min))
                                chain.step(nc.vector.tensor_scalar(t1[:, :], ids, -1.0, trash[:, 0:1],
                                                                   ALU.mult, ALU.add))
                                chain.step(nc.vector.tensor_tensor(out=t1[:, :], in0=t1[:, :], in1=cnt[:, :],
                                                                   op=ALU.mult))
                                chain.step(nc.vector.tensor_tensor(out=t1[:, :], in0=t1[:, :], in1=ids, op=ALU.add))
                                chain.step(nc.vector.tensor_scalar(put_dst[:, bass.ds(c, 1), :].squeeze(1), t1[:, :],
                                                                   2.0, None, ALU.mult))
                            else:
                                hold(dve, gathered[h], 16 * U * (j + 1))
                                hold(dve, summed, c - 1)
                                g = got[h][:, :, :]
                                o = w_in // 2
                                r = rden[:, bass.ds(c, 1), :].squeeze(1)
                                hold(dve, vals_ready, c)
                                if k == 1:
                                    chain.step(nc.vector.tensor_tensor(
                                        out=cnt[:, :].unsqueeze(2), in0=g[:, :, D:D + 1], in1=g[:, :, o + D:o + D + 1],
                                        op=ALU.add))
                                    chain.step(nc.vector.tensor_scalar(t1[:, :], cnt[:, :], 1.0, None, ALU.max))
                                    chain.step(nc.vector.reciprocal(cnt[:, :], t1[:, :]))
                                    nc.vector.tensor_scalar(r, cnt[:, :], 1.0, None, ALU.mult)
                                    r = cnt[:, :]
                                chain.step(nc.vector.tensor_tensor(out=vals[h][:, :, :], in0=g[:, :, 0:D],
                                                                   in1=g[:, :, o:o + D], op=ALU.add))
                                nc.vector.tensor_tensor(out=vals[h][:, :, :], in0=vals[h][:, :, :],
                                                        in1=r.unsqueeze(2).broadcast_to([P, U, D]),
                                                        op=ALU.mult).then_inc(vals_ready, 1)
                            for a in range(2):
                                hold(dve, scattered[a], 16 * (U // 2) * (c - 1))
                            nc.vector.tensor_tensor(out=ix_put[h][:, :], in0=put_dst[:, bass.ds(c, 1), :].squeeze(1),
                                                    in1=half[:, :], op=ALU.add).then_inc(put_ready, 1)

                        over(dve, NCH, body)

                    @block.gpsimd
                    def _(pool):
                        if k == 0:
                            pool.wait_ge(ones_set, 2)

                        def body(s, h, j, gather=True, scatter=True):
                            if gather:
                                pool_hold(pool, get_ready, s + 1)
                                pool_hold(pool, vals_ready if k else summed, s - 1)
                            if scatter:
                                pool_hold(pool, put_ready, s - 1)
                                pool_hold(pool, sums_ready, s - 1)
                            for u in range(U):
                                if gather:
                                    pool.indirect_dma_start(
                                        got[h][:, u, 0:w_in], None, source,
                                        bass.IndirectOffsetOnAxis(ix_get[h][:, u:u + 1].bitcast(U32), 0)
                                    ).then_inc(gathered[h], 16)
                                if scatter:
                                    pool_hold(pool, scattered[u % 2], 16 * ((U // 2) * (s - 2) + u // 2))
                                    pool.indirect_dma_start(
                                        halves, bass.IndirectOffsetOnAxis(ix_put[h][:, u:u + 1].bitcast(U32), 0),
                                        sums[h][:, u, :], None, compute_op=ALU.add).then_inc(scattered[u % 2], 16)

                        body(0, 0, 0, scatter=False)
                        body(1, 1, 0, scatter=False)
                        body(2, 0, 1)
                        body(3, 1, 1)
                        with pool.Fori(0, (NCH - 4) // 2) as i:
                            body(i * 2 + 4, 0, i + 2)
                            body(i * 2 + 5, 1, i + 2)
                        body(NCH, 0, NCH // 2, gather=False)
                        body(NCH + 1, 1, NCH // 2, gather=False)
                        for a in range(2):
                            pool.wait_ge(scattered[a], 16 * (U // 2) * NCH)

                    @block.tensor
                    def _(pe):
                        if k == 0:
                            pe.wait_ge(ones_set, 2)

                        def body(c, h, j):
                            hold(pe, same_ready, c + 1)
                            if k:
                                hold(pe, vals_ready, c + 1)
                            else:
                                hold(pe, gathered[h], 16 * U * (j + 1))
                            hold(pe, sums_ready, c - 1)
                            for u in range(U):
                                ins = nc.tensor.matmul(bank[h][:, u * w_out:(u + 1) * w_out], same[h][:, u, :],
                                                       vals[h][:, u, :], start=True, stop=True)
                            ins.then_inc(summed, 1)

                        over(pe, NCH, body)

                    @block.scalar
                    def _(act):
                        def body(c, h, j):
                            hold(act, summed, c + 1)
                            for a in range(2):
                                hold(act, scattered[a], 16 * (U // 2) * (c - 1))
                            nc.scalar.copy(sums[h][:, :, :], bank[h][:, 0:U * w_out].rearrange(
                                "p (u w) -> p u w", u=U)).then_inc(sums_ready, 1)

                        over(act, NCH, body)


        def node_views(t, width):
            main = t[0:NN * NQ, :].rearrange("(c p q) d -> c p (q d)", p=P, q=Q)
            tail = t[NN * NQ:N, :].rearrange("(p q) d -> p (q d)", q=Q)

            def view(c, parts):
                return tail if parts < P else main[bass.ds(c, 1), :, :].squeeze(0)
            return view

        def over_nodes(eng, body):
            body(0, 0, 0, P)
            body(1, 1, 0, P)
            with eng.Fori(0, NN // 2 - 1) as i:
                body(i * 2 + 2, 0, i + 1, P)
                body(i * 2 + 3, 1, i + 1, P)
            body(NN, 0, NN // 2, TAILN)

        def nodes_y():
            with ExitStack() as lctx:
                def pair(name, shape, dt=F32):
                    return [lctx.enter_context(nc.sbuf_tensor(f"{name}_{i}", shape, dt)) for i in range(2)]

                xb, ta, tb, tc = pair("xb", [P, Q, D]), pair("ta", [P, Q, 2 * W0]), pair("tb", [P, Q, 2 * D]), pair("tc", [P, Q, 2 * D])
                tbc, z, sq = pair("tbc", [P, Q, 2 * D]), pair("z", [P, Q, D]), pair("sq", [P, Q, D])
                s0, yo = pair("s0", [P, Q, D])[0], pair("yo", [P, Q, D])
                q1, q2, mean, var, rs = (pair(n, [P, Q]) for n in ("q1", "q2", "mean", "var", "rs"))
                nodes_in, y_out = [sem("nodes_in0"), sem("nodes_in1")], [sem("y_out0"), sem("y_out1")]
                later_summed, z_ready, sq_ready, var_ready, rs_ready, y_ready, ych = (
                    sem("later_summed"), sem("z_ready"), sem("sq_ready"), sem("var_ready"), sem("rs_ready"),
                    sem("y_ready"), sem("ych"))
                views = [node_views(t, 0) for t in (x, table[0], table[1], table[2])]
                y_view = node_views(y_table, D)
                with nc.Block() as block:
                    @block.sync
                    def _(sp):
                        def body(c, h, j, parts):
                            hold(sp, y_ready, c - 1)
                            for b, v in zip((xb, ta, tb, tc), views):
                                sp.dma_start(b[h][0:parts, :, :].rearrange("p q d -> p (q d)"), v(c, parts)
                                             ).then_inc(nodes_in[h], 16)

                        over_nodes(sp, body)

                    @block.gpsimd
                    def _(pool):
                        def body(c, h, j, parts):
                            pool_hold(pool, nodes_in[h], 64 * (j + 1))
                            pool_hold(pool, y_ready, c - 1)
                            nc.gpsimd.tensor_tensor(out=tbc[h][0:parts, :, :], in0=tb[h][0:parts, :, :],
                                                    in1=tc[h][0:parts, :, :], op=ALU.add).then_inc(later_summed, 1)

                        over_nodes(pool, body)

                    @block.vector
                    def _(dve):
                        chain = Chain(dve, ych, 10)
                        v = nc.vector

                        def body(c, h, j, parts):
                            chain.body(c)
                            s = slice(0, parts)

                            def wide(t):
                                return t.unsqueeze(2).broadcast_to([parts, Q, D])
                            hold(dve, nodes_in[h], 64 * (j + 1))
                            t = ta[h][s, :, :]
                            chain.step(v.tensor_tensor(out=q1[h][s, :].unsqueeze(2), in0=t[:, :, D:W0],
                                                       in1=t[:, :, W0 + D:], op=ALU.add))
                            chain.step(v.tensor_scalar(q2[h][s, :], q1[h][s, :], 1.0, None, ALU.max))
                            chain.step(v.reciprocal(q1[h][s, :], q2[h][s, :]))
                            chain.step(v.tensor_tensor(out=s0[s, :, :], in0=t[:, :, 0:D], in1=t[:, :, W0:W0 + D], op=ALU.add))
                            hold(dve, later_summed, c + 1)
                            chain.step(v.tensor_tensor(out=s0[s, :, :], in0=s0[s, :, :], in1=tbc[h][s, :, 0:D], op=ALU.add))
                            chain.step(v.tensor_tensor(out=s0[s, :, :], in0=s0[s, :, :], in1=tbc[h][s, :, D:], op=ALU.add))
                            chain.step(v.scalar_tensor_tensor(out=s0[s, :, :], in0=s0[s, :, :], scalar=0.25,
                                                              in1=wide(q1[h][s, :]), op0=ALU.mult, op1=ALU.mult))
                            chain.step(v.scalar_tensor_tensor(out=s0[s, :, :], in0=xb[h][s, :, :], scalar=1.25,
                                                              in1=s0[s, :, :], op0=ALU.mult, op1=ALU.add))
                            chain.step(v.tensor_reduce(mean[h][s, :], s0[s, :, :], AX, ALU.add))
                            v.scalar_tensor_tensor(out=z[h][s, :, :], in0=wide(mean[h][s, :]), scalar=-1.0 / D,
                                                   in1=s0[s, :, :], op0=ALU.mult, op1=ALU.add).then_inc(z_ready, 1)
                            hold(dve, sq_ready, c + 1)
                            v.tensor_reduce(var[h][s, :], sq[h][s, :, :], AX, ALU.add).then_inc(var_ready, 1)
                            hold(dve, rs_ready, c + 1)
                            chain.step(v.reciprocal(q2[h][s, :], rs[h][s, :]))
                            hold(dve, y_out[h], 16 * j)
                            v.tensor_tensor(out=yo[h][s, :, :], in0=z[h][s, :, :], in1=wide(q2[h][s, :]),
                                            op=ALU.mult).then_inc(y_ready, 1)

                        over_nodes(dve, body)

                    @block.scalar
                    def _(act):
                        def body(c, h, j, parts):
                            s = slice(0, parts)
                            hold(act, z_ready, c + 1)
                            nc.scalar.activation(sq[h][s, :, :], z[h][s, :, :], ACT.Square).then_inc(sq_ready, 1)
                            hold(act, var_ready, c + 1)
                            nc.scalar.activation(rs[h][s, :], var[h][s, :], ACT.Sqrt, bias=eps[s, 0:1],
                                                 scale=1.0 / D).then_inc(rs_ready, 1)
                            hold(act, y_ready, c + 1)
                            act.dma_start(y_view(c, parts), yo[h][s, :, :].rearrange("p q d -> p (q d)")
                                          ).then_inc(y_out[h], 16)

                        over_nodes(act, body)
                        act.wait_ge(y_out[0], 16 * (NN // 2 + 1))
                        act.wait_ge(y_out[1], 16 * (NN // 2))

        def edges_general():
            with ExitStack() as lctx:
                def pair(name, shape, dt=F32):
                    return [lctx.enter_context(nc.sbuf_tensor(f"{name}_{i}", shape, dt)) for i in range(2)]

                rows = [pair("e_rows_src", [P, CE], I32), pair("e_rows_dst", [P, CE], I32)]
                same = [pair("e_same_src", [P, U, P]), pair("e_same_dst", [P, U, P])]
                feat, feat_t, hid = pair("feat", [P, U, F]), pair("feat_t", [F, CE]), pair("hid", [2 * H, CE])
                flow, sums = pair("flow", [P, U, 2 * D]), pair("e_sums", [P, U, 2 * D])
                prod, cnt, t1 = pair("e_prod", [P, U, P])[0], pair("e_cnt", [P, U])[0], pair("e_t1", [P, U])[0]
                ix_get = [pair("e_get_src", [P, U], I32), pair("e_get_dst", [P, U], I32)]
                ix_put = [pair("e_put_src", [P, U], I32), pair("e_put_dst", [P, U], I32)]
                rows_in, attrs_in, gathered = ([sem(f"{n}{h}") for h in range(2)] for n in ("e_rows_in", "e_attrs_in", "e_gathered"))
                scattered = [sem("e_scattered_src"), sem("e_scattered_dst")]
                (get_ready, put_ready, same_ready, turned, turned_out, hid_mm, hid_ready, flow_mm, flow_ready, summed,
                 sums_ready, ech) = (sem(f"e_{n}") for n in (
                     "get_ready", "put_ready", "same_ready", "turned", "turned_out", "hid_mm", "hid_ready", "flow_mm",
                     "flow_ready", "summed", "sums_ready", "chain"))
                flow_rows = flows.rearrange("n (a w) -> (n a) w", a=2)
                attr_main = edge_attr[0:(NCH - 1) * CE, :].rearrange("(c u p) d -> c p u d", p=P, u=U)
                attr_tail = edge_attr[(NCH - 1) * CE:E - TAILP, :].rearrange("(u p) d -> p u d", p=P)
                with nc.Block() as block:
                    @block.sync
                    def _(sp):
                        def body(c, h, j):
                            hold(sp, same_ready, c - 1)
                            for k in (SRC, DST):
                                sp.dma_start(rows[k][h][:, :], row_of[k][bass.ds(c, 1), :].broadcast_to([P, CE])
                                             ).then_inc(rows_in[h], 16)
                            hold(sp, turned, c - 1)
                            if isinstance(c, int) and c == NCH - 1:
                                sp.dma_start(feat[h][:, 0:TAILT, 2 * D:], attr_tail).then_inc(attrs_in[h], 16)
                                sp.dma_start(feat[h][0:TAILP, TAILT:TAILT + 1, 2 * D:], edge_attr[E - TAILP:E, :]
                                             .unsqueeze(1)).then_inc(attrs_in[h], 16)
                            else:
                                sp.dma_start(feat[h][:, :, 2 * D:], attr_main[bass.ds(c, 1), :, :, :].squeeze(0)
                                             ).then_inc(attrs_in[h], 16)

                        over(sp, NCH, body)

                    @block.gpsimd
                    def _(pool):
                        def body(s, h, j, gather=True, scatter=True):
                            if gather:
                                pool_hold(pool, get_ready, s + 1)
                                pool_hold(pool, turned, s - 1)
                            if scatter:
                                pool_hold(pool, put_ready, s - 1)
                                pool_hold(pool, sums_ready, s - 1)
                            for u in range(U):
                                for k, at in ((DST, 0), (SRC, D)):
                                    if gather:
                                        pool.indirect_dma_start(
                                            feat[h][:, u, at:at + D], None, y_table,
                                            bass.IndirectOffsetOnAxis(ix_get[k][h][:, u:u + 1].bitcast(U32), 0)
                                        ).then_inc(gathered[h], 16)
                                for k, at in ((DST, 0), (SRC, D)):
                                    if scatter:
                                        pool_hold(pool, scattered[k], 16 * (U * (s - 2) + u))
                                        pool.indirect_dma_start(
                                            flow_rows, bass.IndirectOffsetOnAxis(ix_put[k][h][:, u:u + 1].bitcast(U32), 0),
                                            sums[h][:, u, at:at + D], None, compute_op=ALU.add).then_inc(scattered[k], 16)

                        body(0, 0, 0, scatter=False)
                        body(1, 1, 0, scatter=False)
                        body(2, 0, 1)
                        body(3, 1, 1)
                        with pool.Fori(0, (NCH - 4) // 2) as i:
                            body(i * 2 + 4, 0, i + 2)
                            body(i * 2 + 5, 1, i + 2)
                        body(NCH, 0, NCH // 2, gather=False)
                        body(NCH + 1, 1, NCH // 2, gather=False)
                        for k in (SRC, DST):
                            pool.wait_ge(scattered[k], 16 * U * NCH)

                    @block.vector
                    def _(dve):
                        chain = Chain(dve, ech, 6)
                        v = nc.vector

                        def stage_get(c, h):
                            for k in (SRC, DST):
                                ins = v.tensor_scalar(ix_get[k][h][:, :], get[k][:, bass.ds(c, 1), :].squeeze(1), 0.0,
                                                      None, ALU.add)
                            ins.then_inc(get_ready, 1)

                        def body(c, h, j):
                            if isinstance(c, int) and c == 0:
                                stage_get(0, 0)
                            if not (isinstance(c, int) and c == NCH - 1):
                                hold(dve, gathered[1 - h], 32 * U * (j + h))
                                stage_get(c + 1, 1 - h)
                            chain.body(c)
                            hold(dve, rows_in[h], 32 * (j + 1))
                            hold(dve, summed, c - 1)
                            v.tensor_tensor(out=same[DST][h][:, :, :], **same_id(rows[DST][h][:, :], DST, c))
                            v.tensor_tensor(out=same[SRC][h][:, :, :], **same_id(rows[SRC][h][:, :], SRC, c)
                                            ).then_inc(same_ready, 1)
                            hold(dve, same_ready, c + 1)
                            ids = col[SRC][:, bass.ds(c, 1), :].squeeze(1)
                            hold(dve, put_ready, c)
                            chain.step(v.tensor_tensor(out=prod[:, :, :], in0=same[SRC][h][:, :, :], in1=before[:, :, :],
                                                       op=ALU.mult))
                            chain.step(v.tensor_reduce(cnt[:, :], prod[:, :, :], AX, ALU.add))
                            chain.step(v.tensor_scalar(cnt[:, :], cnt[:, :], 1.0, None, ALU.min))
                            chain.step(v.tensor_scalar(t1[:, :], ids, -1.0, trash[:, 0:1], ALU.mult, ALU.add))
                            chain.step(v.tensor_tensor(out=t1[:, :], in0=t1[:, :], in1=cnt[:, :], op=ALU.mult))
                            chain.step(v.tensor_tensor(out=t1[:, :], in0=t1[:, :], in1=ids, op=ALU.add))
                            for k in (SRC, DST):
                                hold(dve, scattered[k], 16 * U * (c - 1))
                            v.tensor_scalar(ix_put[SRC][h][:, :], t1[:, :], 2.0, 1.0, ALU.mult, ALU.add)
                            v.tensor_scalar(ix_put[DST][h][:, :], put_dst[:, bass.ds(c, 1), :].squeeze(1), 0.0, None,
                                            ALU.add).then_inc(put_ready, 1)
                            hold(dve, flow_mm, c + 1)
                            v.tensor_scalar(flow[h][:, :, :], bank[4 + h][:, 0:U * 2 * D].rearrange(
                                "p (u w) -> p u w", u=U), 0.0, None, ALU.max).then_inc(flow_ready, 1)

                        over(dve, NCH, body)

                    @block.tensor
                    def _(pe):
                        def body(c, h, j):
                            hold(pe, gathered[h], 32 * U * (j + 1))
                            hold(pe, attrs_in[h], 16 * (j + 1) + 16 * (isinstance(c, int) and c == NCH - 1))
                            hold(pe, turned_out, c - 1)
                            for u in range(U):
                                ins = nc.tensor.transpose(bank[h][0:F, u * P:(u + 1) * P], feat[h][:, u, :], ident[:, :])
                            ins.then_inc(turned, 1)
                            hold(pe, turned_out, c + 1)
                            hold(pe, hid_ready, c - 1)
                            nc.tensor.matmul(bank[2 + h][:, :], w1e[:, :], feat_t[h][:, :], start=True, stop=True
                                             ).then_inc(hid_mm, 1)
                            hold(pe, hid_ready, c + 1)
                            hold(pe, flow_ready, c - 1)
                            for u in range(U):
                                o = bank[4 + h][:, u * 2 * D:(u + 1) * 2 * D]
                                nc.tensor.matmul(o, hid[h][:, u * P:(u + 1) * P], w2e[:, :], start=True, stop=False)
                                ins = nc.tensor.matmul(o, ones[:, :], b2e[:, :], start=False, stop=True)
                            ins.then_inc(flow_mm, 1)
                            hold(pe, flow_ready, c + 1)
                            hold(pe, same_ready, c + 1)
                            hold(pe, sums_ready, c - 1)
                            for u in range(U):
                                for k, at in ((DST, 0), (SRC, D)):
                                    ins = nc.tensor.matmul(bank[6 + h][:, u * 2 * D + at:u * 2 * D + at + D],
                                                           same[k][h][:, u, :], flow[h][:, u, at:at + D],
                                                           start=True, stop=True)
                            ins.then_inc(summed, 1)

                        over(pe, NCH, body)

                    @block.scalar
                    def _(act):
                        def body(c, h, j):
                            hold(act, turned, c + 1)
                            hold(act, hid_mm, c - 1)
                            nc.scalar.copy(feat_t[h][:, :], bank[h][0:F, :]).then_inc(turned_out, 1)
                            hold(act, hid_mm, c + 1)
                            hold(act, flow_mm, c - 1)
                            nc.scalar.activation(hid[h][:, :], bank[2 + h][:, :], ACT.Relu, bias=b1e[:, 0:1]
                                                 ).then_inc(hid_ready, 1)
                            hold(act, summed, c + 1)
                            for k in (SRC, DST):
                                hold(act, scattered[k], 16 * U * (c - 1))
                            nc.scalar.copy(sums[h][:, :, :], bank[6 + h][:, 0:U * 2 * D].rearrange(
                                "p (u w) -> p u w", u=U)).then_inc(sums_ready, 1)

                        over(act, NCH, body)

        def by_block(t, g, rows):
            return t[0:rows // P * P, :].rearrange("(b p) d -> p b d", p=P)[:, bass.ds(g * GB, GB), :]

        def last_group(t, buf, store):
            full, rest = divmod(N - (NG - 1) * GB * P, P)
            at = (NG - 1) * GB * P
            whole = t[at:at + full * P, :].rearrange("(b p) d -> p b d", p=P)
            pairs = [(buf[:, 0:full, :], whole), (buf[0:rest, full:full + 1, :], t[at + full * P:N, :].unsqueeze(1))]
            return [(d, s) for s, d in pairs] if store else pairs

        def set_window(hot, c, u):
            return nc.vector.tensor_scalar(hot[:, u, :], steps[:, :], hot_at[:, bass.ds(c, 1), u:u + 1].squeeze(1),
                                           None, ALU.is_equal)

        def sum_windows(hot, parts, banks, w):
            for u in range(U):
                for m in range(WB):
                    at = ((u % 2) * WB + m) * W0
                    for i, part in enumerate(parts):
                        ins = nc.tensor.matmul(banks[u // 2][:, at:at + w], hot[:, u, m * P:(m + 1) * P],
                                               part[:, u, 0:w], start=(i == 0), stop=(i == len(parts) - 1))
            return ins

        def window_bases(c):
            return nc.values_load_multi_w_load_instructions(
                base_row[0:1, bass.ds(c * U, U)], engines=[nc.vector.engine], min_val=0, max_val=NBLK,
                skip_runtime_bounds_check_because="a base is an id below NT, over 128")[1]

        def add_window(added, banks, base, u, w):
            t = node_sums[:, bass.ds(base, WB), 0:w]
            at = (u % 2) * WB * W0
            nc.vector.tensor_tensor(
                out=t, in0=t, in1=banks[u // 2][:, at:at + WB * W0].rearrange("p (m w) -> p m w", w=W0)[:, :, 0:w],
                op=ALU.add).then_inc(added, 1)

        def windows(dve, hot, c, banks, w, added, do_set, do_add):
            if do_add:
                bases = window_bases(c - 1)
            for u in range(U):
                if do_add:
                    hold(dve, added, U * (c - 1) + u)
                    add_window(added, banks, bases[u], u, w)
                if do_set and u < U // 2:
                    ins = set_window(hot, c, u + U // 2)
                    if u == U // 2 - 1:
                        ins.then_inc(do_set, 1)

        def layer_fast(k):
            source = x if k == 0 else means[k - 1]
            w = W0 if k == 0 else D
            with ExitStack() as lctx:
                def buf(name, shape, dt=F32):
                    return lctx.enter_context(nc.sbuf_tensor(f"f{k}_{name}", shape, dt))

                def pair(name, shape, dt=F32):
                    return [buf(f"{name}{h}", shape, dt) for h in range(2)]

                def fsem(name):
                    return scope[-1].enter_context(nc.semaphore(f"f{k}_{name}"))

                got = [buf(f"got{q}", [P, U, D]) for q in range(4)]
                ix_get = [buf(f"ix_get{q}", [P, U], I32) for q in range(4)]
                hi, mid_, lo = pair("hi", [P, U, W0], BF16), pair("mid", [P, U, W0], BF16), pair("lo", [P, U, W0], BF16)
                rest, hot = pair("rest", [P, U, D]), pair("hot", [P, U, WIN], BF16)
                part_in, (part_out, mean_out) = buf("part_in", [P, GB, D]), (pair(n, [P, GB, D]) for n in ("part_out", "mean_out"))
                scaled, z, sq = (buf(n, [P, GB, D]) for n in ("scaled", "z", "sq"))
                n1, n2, avg, var, rs = (buf(n, [P, GB]) for n in ("n1", "n2", "avg", "var", "rs"))
                gathered = [fsem(f"gathered{q}") for q in range(4)]
                (get_ready, hot_ready, hi_ready, rest_ready, mid_ready, lo_ready, summed, added, part_loaded, mean_ready,
                 part_ready, scaled_ready, cleared, set_up, gch, z_ready, sq_ready, var_ready, rs_ready,
                 zeroed, inverted) = (fsem(n) for n in (
                     "get_ready", "hot_ready", "hi_ready", "rest_ready", "mid_ready", "lo_ready", "summed", "added",
                     "part_loaded", "mean_ready", "part_ready", "scaled_ready", "cleared", "set_up",
                     "group_chain", "z_ready", "sq_ready", "var_ready", "rs_ready", "zeroed", "inverted"))
                stored = [fsem("stored0"), fsem("stored1")]
                mine = [bank[0:2], bank[2:4]]

                def last(g):
                    return isinstance(g, int) and g == NG - 1

                with nc.Block() as block:
                    @block.sync
                    def _(sp):
                        def load(g):
                            if k:
                                sp.dma_start(part_in[:, :, :].rearrange("p b d -> p (b d)"),
                                             partial[bass.ds(g, 1), :, :].squeeze(0)).then_inc(part_loaded, 16)
                            elif last(g):
                                for d, s in last_group(x, part_in, False):
                                    sp.dma_start(d, s).then_inc(part_loaded, 16)
                            else:
                                sp.dma_start(part_in[:, :, :], by_block(x, g, N)).then_inc(part_loaded, 16)

                        def body(g, gh, *_):
                            if not last(g):
                                hold(sp, (scaled_ready, part_ready, z_ready)[k], g + 1)
                                load(g + 1)
                            hold(sp, part_ready, g + 1)
                            out_tile = (part_out if k == 2 else mean_out)[gh]
                            sp.dma_start(by_block(means[k], g, NT), out_tile[:, :, :]).then_inc(stored[gh], 16)
                            sp.dma_start(partial[bass.ds(g, 1), :, :].squeeze(0),
                                         part_out[gh][:, :, :].rearrange("p b d -> p (b d)")).then_inc(stored[gh], 16)
                            if k == 1:
                                sp.dma_start(backward[bass.ds(g * (GB * P), GB * P), :].rearrange(
                                    "(p r) d -> p (r d)", p=P), zeros[:, 0:GB * D]).then_inc(zeroed, 16)

                        load(0)
                        over4(sp, NG, body, first=2)
                        sp.wait_ge(stored[0], 32 * (NG - NG // 2))
                        sp.wait_ge(stored[1], 32 * (NG // 2))
                        if k == 1:
                            sp.wait_ge(zeroed, 16 * NG)

                    @block.gpsimd
                    def _(pool):
                        def body(c, h, j, q, r):
                            pool_hold(pool, get_ready, c + 1)
                            for u in range(U):
                                pool.indirect_dma_start(
                                    got[q][:, u, :], None, source,
                                    bass.IndirectOffsetOnAxis(ix_get[q][:, u:u + 1].bitcast(U32), 0)
                                ).then_inc(gathered[q], 16)

                        over4(pool, NCH, body)

                    @block.scalar
                    def _(act):
                        act.wait_ge(set_up, 6)

                        def body(c, h, j, q, r):
                            hold(act, gathered[q], 16 * U * (r + 1))
                            hold(act, summed, c - 1)
                            hold(act, rest_ready, c - 1)
                            nc.scalar.copy(hi[h][:, :, 0:D], got[q][:, :, :]).then_inc(hi_ready, 1)
                            hold(act, rest_ready, c + 1)
                            hold(act, lo_ready, c - 1)
                            nc.scalar.copy(mid_[h][:, :, 0:D], rest[h][:, :, :]).then_inc(mid_ready, 1)
                            if h == 0 and not (isinstance(c, int) and c < 6):
                                root(j - 3)
                            if h == 0 and not (isinstance(c, int) and c < 4):
                                scale(j - 2)
                            if h == 1 and not (isinstance(c, int) and c < 4):
                                group(j - 2)

                        def scale(g):
                            if k == 0:
                                hold(act, part_loaded, 16 * (g + 1) + 16 * last(g))
                                hold(act, part_ready, g)
                                nc.scalar.mul(scaled[:, :, :], part_in[:, :, :], 1.25).then_inc(scaled_ready, 1)

                        def group(g):
                            if k == 2:
                                hold(act, z_ready, g + 1)
                                nc.scalar.activation(sq[:, :, :], z[:, :, :], ACT.Square).then_inc(sq_ready, 1)
                            hold(act, mean_ready, g + 1, alone=True)
                            nc.scalar.copy(node_sums[:, bass.ds(g * GB, GB), 0:D], zeros[:, 0:GB * D].rearrange(
                                "p (b d) -> p b d", d=D)).then_inc(cleared, 1)

                        def root(g):
                            if k == 2:
                                hold(act, var_ready, g + 1)
                                nc.scalar.activation(rs[:, :], var[:, :], ACT.Sqrt, bias=eps[:, 0:1],
                                                     scale=1.0 / D).then_inc(rs_ready, 1)

                        over4(act, NCH, body)
                        root(NG - 3)
                        for g in (NG - 2, NG - 1):
                            scale(g)
                            group(g)
                            root(g)
                        act.wait_ge(cleared, NG)

                    @block.tensor
                    def _(pe):
                        def body(c, h, j):
                            hold(pe, hot_ready, c + 1)
                            hold(pe, hi_ready, c + 1)
                            hold(pe, mid_ready, c + 1)
                            hold(pe, lo_ready, c + 1)
                            hold(pe, added, U * (c - 1))
                            sum_windows(hot[h], (hi[h], mid_[h], lo[h]), mine[h], w).then_inc(summed, 1)

                        over(pe, NCH, body)

                    @block.vector
                    def _(dve):
                        v = nc.vector
                        gchain = Chain(dve, gch, (2, 0, 2)[k])
                        for h in range(2):
                            v.memset(hi[h][:, :, D:], 1.0).then_inc(set_up, 1)
                            v.memset(mid_[h][:, :, D:], 0.0).then_inc(set_up, 1)
                            v.memset(lo[h][:, :, D:], 0.0).then_inc(set_up, 1)

                        def stage_get(c, q):
                            v.tensor_scalar(ix_get[q][:, :], get[SRC][:, bass.ds(c, 1), :].squeeze(1), 0.0,
                                            None, ALU.add).then_inc(get_ready, 1)

                        def wide(t):
                            return t.unsqueeze(2).broadcast_to([P, GB, D])

                        def average(g, gh, gj):
                            gchain.body(g)
                            sums = node_sums[:, bass.ds(g * GB, GB), 0:D]
                            r = rden_n[:, bass.ds(g * GB, GB)]
                            if k == 0:
                                hold(dve, mean_ready, g)
                                gchain.step(v.tensor_scalar(n1[:, :].unsqueeze(2), node_sums[:, bass.ds(g * GB, GB), D:W0],
                                                            1.0, None, ALU.max))
                                gchain.step(v.reciprocal(n2[:, :], n1[:, :]))
                                v.tensor_scalar(r, n2[:, :], 1.0, None, ALU.mult)
                                r = n2[:, :]
                            hold(dve, stored[gh], 32 * gj)
                            hold(dve, part_ready, g)
                            v.tensor_tensor(out=mean_out[gh][:, :, :], in0=sums, in1=wide(r), op=ALU.mult
                                            ).then_inc(mean_ready, 1)

                        def blend(g, gh):
                            hold(dve, mean_ready, g + 1)
                            if k == 0:
                                hold(dve, scaled_ready, g + 1)
                            else:
                                hold(dve, part_loaded, 16 * (g + 1))
                            ins = v.scalar_tensor_tensor(
                                out=(mean_out if k == 2 else part_out)[gh][:, :, :], in0=mean_out[gh][:, :, :],
                                scalar=0.25, in1=(part_in if k else scaled)[:, :, :], op0=ALU.mult, op1=ALU.add)
                            if k < 2:
                                ins.then_inc(part_ready, 1)
                            else:
                                gchain.step(ins)

                        def centre(g, gh):
                            if k == 2:
                                gchain.step(v.tensor_reduce(avg[:, :], mean_out[gh][:, :, :], AX, ALU.add))
                                v.scalar_tensor_tensor(out=z[:, :, :], in0=wide(avg[:, :]), scalar=-1.0 / D,
                                                       in1=mean_out[gh][:, :, :], op0=ALU.mult, op1=ALU.add
                                                       ).then_inc(z_ready, 1)

                        def spread(g):
                            if k == 2:
                                hold(dve, sq_ready, g + 1)
                                v.tensor_reduce(var[:, :], sq[:, :, :], AX, ALU.add).then_inc(var_ready, 1)

                        def invert(g):
                            if k == 2:
                                hold(dve, rs_ready, g + 1)
                                v.reciprocal(n1[:, :], rs[:, :]).then_inc(inverted, 1)

                        def finish(g, gh):
                            if k == 2:
                                hold(dve, inverted, g + 1)
                                v.tensor_tensor(out=part_out[gh][:, :, :], in0=z[:, :, :], in1=wide(n1[:, :]),
                                                op=ALU.mult).then_inc(part_ready, 1)

                        def body(c, h, j, q, r):
                            first = isinstance(c, int) and c == 0
                            first_half = h == 1 and not (isinstance(c, int) and c < 5)
                            second_half = h == 0 and not (isinstance(c, int) and c < 6)
                            if first:
                                for ahead in range(4):
                                    stage_get(ahead, ahead)
                            if first_half:
                                hold(dve, added, U * (c - 1))
                                average(j - 2, q // 2, r - 1)
                            hold(dve, hi_ready, c + 1)
                            hold(dve, mid_ready, c - 1)
                            hold(dve, lo_ready, c - 1)
                            v.tensor_tensor(out=rest[h][:, :, :], in0=got[q][:, :, :], in1=hi[h][:, :, 0:D],
                                            op=ALU.subtract).then_inc(rest_ready, 1)
                            if not (isinstance(c, int) and c >= NCH - 4):
                                stage_get(c + 4, q)
                            if second_half:
                                spread(j - 3)
                            hold(dve, summed, c - 1)
                            set_window(hot[h], c, 0)
                            if first_half:
                                blend(j - 2, q // 2)
                            set_window(hot[h], c, 1)
                            hold(dve, rest_ready, c + 1)
                            hold(dve, mid_ready, c + 1)
                            v.tensor_tensor(out=lo[h][:, :, 0:D], in0=rest[h][:, :, :], in1=mid_[h][:, :, 0:D],
                                            op=ALU.subtract).then_inc(lo_ready, 1)
                            if first_half:
                                centre(j - 2, q // 2)
                            if second_half:
                                invert(j - 3)
                            hold(dve, summed, c)
                            windows(dve, hot[h], c, mine[1 - h], w, added, hot_ready, not first)
                            if second_half:
                                finish(j - 3, 1 - q // 2)

                        over4(dve, NCH, body)
                        spread(NG - 3)
                        hold(dve, summed, NCH)
                        windows(dve, None, NCH, mine[1], w, added, None, True)
                        invert(NG - 3)
                        finish(NG - 3, 0)
                        hold(dve, added, U * NCH)
                        for g in (NG - 2, NG - 1):
                            average(g, g % 2, g // 2)
                            blend(g, g % 2)
                            centre(g, g % 2)
                            spread(g)
                            invert(g)
                            finish(g, g % 2)

        def edges_fast():
            with ExitStack() as lctx:
                def pair(name, shape, dt=F32):
                    return [lctx.enter_context(nc.sbuf_tensor(f"h_{name}{h}", shape, dt)) for h in range(2)]

                rows, same = pair("rows", [P, CE], I32), pair("same", [P, U, P])
                feat, feat_t, hid = pair("feat", [P, U, F]), pair("feat_t", [F, CE]), pair("hid", [2 * H, CE])
                flow, sums = pair("flow", [P, U, 2 * D]), pair("sums", [P, U, D])
                hi, mid_, lo = (pair(n, [P, U, D], BF16) for n in ("hi", "mid", "lo"))
                rest, hot = pair("rest", [P, U, D]), pair("hot", [P, U, WIN], BF16)
                prod, cnt, t1 = pair("prod", [P, U, P])[0], pair("cnt", [P, U])[0], pair("t1", [P, U])[0]
                ix_get = [pair("get_src", [P, U], I32), pair("get_dst", [P, U], I32)]
                ix_put = pair("put_src", [P, U], I32)
                rows_in, attrs_in, gathered = ([sem(f"h_{n}{h}") for h in range(2)] for n in ("rows_in", "attrs_in", "gathered"))
                (scattered, get_ready, put_ready, same_ready, turned, turned_out, hid_mm, hid_ready, flow_mm, flow_ready,
                 summed, sums_ready, ech, hot_ready, hi_ready, rest_ready, mid_ready, lo_ready, windowed, added) = (
                     sem(f"h_{n}") for n in (
                         "scattered", "get_ready", "put_ready", "same_ready", "turned", "turned_out", "hid_mm",
                         "hid_ready", "flow_mm", "flow_ready", "summed", "sums_ready", "chain", "hot_ready", "hi_ready",
                         "rest_ready", "mid_ready", "lo_ready", "windowed", "added"))
                attr_main = edge_attr[0:(NCH - 1) * CE, :].rearrange("(c u p) d -> c p u d", p=P, u=U)
                attr_tail = edge_attr[(NCH - 1) * CE:E - TAILP, :].rearrange("(u p) d -> p u d", p=P)
                flow_bank, hid_bank, win_banks = bank[3], bank[2], bank[6:8]

                with nc.Block() as block:
                    @block.sync
                    def _(sp):
                        def body(c, h, j):
                            hold(sp, same_ready, c - 1)
                            sp.dma_start(rows[h][:, :], row_of[SRC][bass.ds(c, 1), :].broadcast_to([P, CE])
                                         ).then_inc(rows_in[h], 16)
                            hold(sp, turned, c - 1)
                            if isinstance(c, int) and c == NCH - 1:
                                sp.dma_start(feat[h][:, 0:TAILT, 2 * D:], attr_tail).then_inc(attrs_in[h], 16)
                                sp.dma_start(feat[h][0:TAILP, TAILT:TAILT + 1, 2 * D:], edge_attr[E - TAILP:E, :]
                                             .unsqueeze(1)).then_inc(attrs_in[h], 16)
                            else:
                                sp.dma_start(feat[h][:, :, 2 * D:], attr_main[bass.ds(c, 1), :, :, :].squeeze(0)
                                             ).then_inc(attrs_in[h], 16)

                        over(sp, NCH, body)

                    @block.gpsimd
                    def _(pool):
                        def body(s, h, j, gather=True, scatter=True):
                            if gather:
                                pool_hold(pool, get_ready, s + 1)
                                pool_hold(pool, turned, s - 1)
                            if scatter:
                                pool_hold(pool, put_ready, s - 1)
                                pool_hold(pool, sums_ready, s - 1)
                            for u in range(U):
                                for k, at in ((DST, 0), (SRC, D)):
                                    if gather:
                                        pool.indirect_dma_start(
                                            feat[h][:, u, at:at + D], None, means[2],
                                            bass.IndirectOffsetOnAxis(ix_get[k][h][:, u:u + 1].bitcast(U32), 0)
                                        ).then_inc(gathered[h], 16)
                                if scatter:
                                    pool_hold(pool, scattered, 16 * (U * (s - 2) + u))
                                    pool.indirect_dma_start(
                                        backward, bass.IndirectOffsetOnAxis(ix_put[h][:, u:u + 1].bitcast(U32), 0),
                                        sums[h][:, u, :], None, compute_op=ALU.add).then_inc(scattered, 16)

                        body(0, 0, 0, scatter=False)
                        body(1, 1, 0, scatter=False)
                        body(2, 0, 1)
                        body(3, 1, 1)
                        with pool.Fori(0, (NCH - 4) // 2) as i:
                            body(i * 2 + 4, 0, i + 2)
                            body(i * 2 + 5, 1, i + 2)
                        body(NCH, 0, NCH // 2, gather=False)
                        body(NCH + 1, 1, NCH // 2, gather=False)
                        pool.wait_ge(scattered, 16 * U * NCH)

                    @block.vector
                    def _(dve):
                        chain = Chain(dve, ech, 6)
                        v = nc.vector

                        def stage_get(c, h):
                            for k in (SRC, DST):
                                ins = v.tensor_scalar(ix_get[k][h][:, :], get[k][:, bass.ds(c, 1), :].squeeze(1), 0.0,
                                                      None, ALU.add)
                            ins.then_inc(get_ready, 1)

                        def body(c, h, j):
                            first = isinstance(c, int) and c == 0
                            if first:
                                stage_get(0, 0)
                            if not (isinstance(c, int) and c == NCH - 1):
                                hold(dve, gathered[1 - h], 32 * U * (j + h))
                                stage_get(c + 1, 1 - h)
                            chain.body(c)
                            hold(dve, rows_in[h], 16 * (j + 1))
                            hold(dve, summed, c - 1)
                            v.tensor_tensor(out=same[h][:, :, :], **same_id(rows[h][:, :], SRC, c)).then_inc(same_ready, 1)
                            hold(dve, windowed, c)
                            for u in range(U // 2):
                                set_window(hot[h], c, u)
                            windows(dve, hot[h], c, win_banks, D, added, hot_ready, not first)
                            hold(dve, same_ready, c + 1)
                            ids = col[SRC][:, bass.ds(c, 1), :].squeeze(1)
                            hold(dve, put_ready, c)
                            chain.step(v.tensor_tensor(out=prod[:, :, :], in0=same[h][:, :, :], in1=before[:, :, :],
                                                       op=ALU.mult))
                            chain.step(v.tensor_reduce(cnt[:, :], prod[:, :, :], AX, ALU.add))
                            chain.step(v.tensor_scalar(cnt[:, :], cnt[:, :], 1.0, None, ALU.min))
                            chain.step(v.tensor_scalar(t1[:, :], ids, -1.0, trash[:, 0:1], ALU.mult, ALU.add))
                            chain.step(v.tensor_tensor(out=t1[:, :], in0=t1[:, :], in1=cnt[:, :], op=ALU.mult))
                            hold(dve, scattered, 16 * U * (c - 1))
                            chain.step(v.tensor_tensor(out=t1[:, :], in0=t1[:, :], in1=ids, op=ALU.add))
                            v.tensor_scalar(ix_put[h][:, :], t1[:, :], 0.0, None, ALU.add).then_inc(put_ready, 1)
                            hold(dve, flow_mm, c + 1)
                            v.tensor_scalar(flow[h][:, :, :], flow_bank[:, 0:U * 2 * D].rearrange(
                                "p (u w) -> p u w", u=U), 0.0, None, ALU.max).then_inc(flow_ready, 1)
                            hold(dve, hi_ready, c + 1)
                            v.tensor_tensor(out=rest[h][:, :, :], in0=flow[h][:, :, 0:D], in1=hi[h][:, :, :],
                                            op=ALU.subtract).then_inc(rest_ready, 1)
                            hold(dve, mid_ready, c + 1)
                            v.tensor_tensor(out=lo[h][:, :, :], in0=rest[h][:, :, :], in1=mid_[h][:, :, :],
                                            op=ALU.subtract).then_inc(lo_ready, 1)

                        over(dve, NCH, body)
                        hold(dve, windowed, NCH)
                        windows(dve, None, NCH, win_banks, D, added, None, True)

                    @block.tensor
                    def _(pe):
                        def body(c, h, j):
                            hold(pe, gathered[h], 32 * U * (j + 1))
                            hold(pe, attrs_in[h], 16 * (j + 1) + 16 * (isinstance(c, int) and c == NCH - 1))
                            hold(pe, turned_out, c - 1)
                            for u in range(U):
                                ins = nc.tensor.transpose(bank[h][0:F, u * P:(u + 1) * P], feat[h][:, u, :], ident[:, :])
                            ins.then_inc(turned, 1)
                            hold(pe, turned_out, c + 1)
                            hold(pe, hid_ready, c)
                            nc.tensor.matmul(hid_bank[:, :], w1e[:, :], feat_t[h][:, :], start=True, stop=True
                                             ).then_inc(hid_mm, 1)
                            hold(pe, hid_ready, c + 1)
                            hold(pe, flow_ready, c)
                            for u in range(U):
                                o = flow_bank[:, u * 2 * D:(u + 1) * 2 * D]
                                nc.tensor.matmul(o, hid[h][:, u * P:(u + 1) * P], w2e[:, :], start=True, stop=False)
                                ins = nc.tensor.matmul(o, ones[:, :], b2e[:, :], start=False, stop=True)
                            ins.then_inc(flow_mm, 1)
                            hold(pe, flow_ready, c + 1)
                            hold(pe, same_ready, c + 1)
                            hold(pe, sums_ready, c - 1)
                            for u in range(U):
                                ins = nc.tensor.matmul(bank[4 + h][:, u * D:(u + 1) * D], same[h][:, u, :],
                                                       flow[h][:, u, D:], start=True, stop=True)
                            ins.then_inc(summed, 1)
                            hold(pe, hot_ready, c + 1)
                            hold(pe, lo_ready, c + 1)
                            hold(pe, added, U * c)
                            sum_windows(hot[h], (hi[h], mid_[h], lo[h]), win_banks, D).then_inc(windowed, 1)

                        over(pe, NCH, body)

                    @block.scalar
                    def _(act):
                        def body(c, h, j):
                            hold(act, turned, c + 1)
                            hold(act, hid_mm, c - 1)
                            nc.scalar.copy(feat_t[h][:, :], bank[h][0:F, :]).then_inc(turned_out, 1)
                            hold(act, hid_mm, c + 1)
                            hold(act, flow_mm, c - 1)
                            nc.scalar.activation(hid[h][:, :], hid_bank[:, :], ACT.Relu, bias=b1e[:, 0:1]
                                                 ).then_inc(hid_ready, 1)
                            hold(act, flow_ready, c + 1)
                            hold(act, windowed, c - 1)
                            nc.scalar.copy(hi[h][:, :, :], flow[h][:, :, 0:D]).then_inc(hi_ready, 1)
                            hold(act, rest_ready, c + 1)
                            nc.scalar.copy(mid_[h][:, :, :], rest[h][:, :, :]).then_inc(mid_ready, 1)
                            hold(act, summed, c + 1)
                            hold(act, scattered, 16 * U * (c - 1))
                            nc.scalar.copy(sums[h][:, :, :], bank[4 + h][:, 0:U * D].rearrange(
                                "p (u w) -> p u w", u=U)).then_inc(sums_ready, 1)

                        over(act, NCH, body)

        def nodes_out(fast):
            n = "s" if fast else "n"
            tail_parts = P if fast else TAILN
            with ExitStack() as lctx:
                def pair(name, shape, dt=F32):
                    return [lctx.enter_context(nc.sbuf_tensor(f"{n}_{name}{i}", shape, dt)) for i in range(2)]

                def nsem(name):
                    return scope[-1].enter_context(nc.semaphore(f"{n}_{name}"))

                HC = 512
                yb, fb = pair("yb", [P, Q, D]), pair("fb", [P, Q, 2 * D])
                flow_t, hid = pair("flow_t", [P, 2 * HC]), pair("hid", [P, 2 * HC])
                s0, z, sq, res = pair("s0", [P, Q, D])[0], pair("z", [P, Q, D]), pair("sq", [P, Q, D]), pair("res", [P, Q, D])
                q2, mean, var, rs = (pair(m, [P, Q]) for m in ("q2", "mean", "var", "rs"))
                y_in, flows_in, res_out = ([nsem(f"{m}{i}") for i in range(2)] for m in ("y_in", "flows_in", "res_out"))
                (turned, turned_out, hid_mm, hid_ready, out_mm, z_ready, sq_ready, var_ready, rs_ready, res_ready, nch,
                 sums_in) = (nsem(m) for m in ("turned", "turned_out", "hid_mm", "hid_ready", "out_mm", "z_ready",
                                               "sq_ready", "var_ready", "rs_ready", "res_ready", "chain", "sums_in"))
                inverted = nsem("inverted")
                y_view, flow_view, out_view = node_views(y_table, D), node_views(flows, 2 * D), node_views(out, D)

                def over_chunks(eng, body):
                    body(0, 0, 0, P)
                    body(1, 1, 0, P)
                    body(2, 0, 1, P)
                    body(3, 1, 1, P)
                    with eng.Fori(0, NN // 2 - 2) as i:
                        body(i * 2 + 4, 0, i + 2, P)
                        body(i * 2 + 5, 1, i + 2, P)
                    body(NN, 0, NN // 2, tail_parts)

                with nc.Block() as block:
                    @block.sync
                    def _(sp):
                        def body(c, h, j, parts):
                            hold(sp, turned, 2 * (c - 1))
                            if fast:
                                sp.dma_start(fb[h][:, :, D:], by_block(backward, c, NT)).then_inc(flows_in[h], 16)
                            else:
                                sp.dma_start(fb[h][0:parts, :, :].rearrange("p q d -> p (q d)"), flow_view(c, parts)
                                             ).then_inc(flows_in[h], 16)
                            hold(sp, z_ready, c - 1)
                            if fast:
                                sp.dma_start(yb[h][:, :, :].rearrange("p q d -> p (q d)"),
                                             partial[bass.ds(c, 1), :, :].squeeze(0)).then_inc(y_in[h], 16)
                            else:
                                sp.dma_start(yb[h][0:parts, :, :].rearrange("p q d -> p (q d)"), y_view(c, parts)
                                             ).then_inc(y_in[h], 16)

                        over_chunks(sp, body)
                        sp.wait_ge(res_out[0], 16 * (NN // 2 + 1) + 16 * fast)
                        sp.wait_ge(res_out[1], 16 * (NN // 2))

                    @block.gpsimd
                    def _(pool):
                        def body(c, h, j, parts):
                            if fast:
                                pool_hold(pool, turned, 2 * (c - 1))
                                nc.gpsimd.tensor_copy(fb[h][:, :, 0:D], node_sums[:, bass.ds(c * GB, GB), 0:D]
                                                      ).then_inc(sums_in, 1)
                            else:
                                square(c, h, parts)

                        def square(c, h, parts):
                            s = slice(0, parts)
                            pool_hold(pool, z_ready, c + 1)
                            nc.gpsimd.tensor_tensor(out=sq[h][s, :, :], in0=z[h][s, :, :], in1=z[h][s, :, :],
                                                    op=ALU.mult).then_inc(sq_ready, 1)

                        over_chunks(pool, body)

                    @block.tensor
                    def _(pe):
                        def turn(c, h, j, parts):
                            hold(pe, flows_in[h], 16 * (j + 1))
                            if fast:
                                hold(pe, sums_in, c + 1)
                            for g in range(2):
                                hold(pe, turned_out, 2 * c + g - 1)
                                for m in range(4):
                                    q = 8 * g + 2 * m
                                    ins = nc.tensor.transpose(
                                        bank[g][:, m * P:m * P + parts],
                                        fb[h][0:parts, q:q + 2, :].rearrange("p q d -> p (q d)"), ident[0:parts, 0:parts])
                                ins.then_inc(turned, 1)

                        def hidden(c, h, parts):
                            for g in range(2):
                                hold(pe, turned_out, 2 * c + g + 1)
                                hold(pe, hid_ready, 2 * c + g - 1)
                                ft = flow_t[h][:, g * HC:(g + 1) * HC].rearrange("p (m n) -> p m n", m=4)[:, :, 0:parts]
                                o = bank[2 + g][:, :].rearrange("p (m n) -> p m n", m=4)[:, :, 0:parts]
                                nc.tensor.matmul(o, w1n[:, :], ft, start=True, stop=True).then_inc(hid_mm, 1)

                        def result(c, h, parts):
                            hold(pe, z_ready, c - 1)
                            for g in range(2):
                                hold(pe, hid_ready, 2 * c + g + 1)
                                for m in range(4):
                                    col0 = g * HC + m * P
                                    o = (4 * g + m) * 2 * D
                                    ins = nc.tensor.matmul(bank[4 + h][0:parts, o:o + 2 * D],
                                                           hid[h][:, col0:col0 + parts], w2n[:, :], start=True, stop=True)
                            ins.then_inc(out_mm, 1)

                        def body(c, h, j, parts):
                            turn(c, h, j, parts)
                            if not (isinstance(c, int) and c == 0):
                                result(c - 1, 1 - h, P)
                            hidden(c, h, parts)

                        over_chunks(pe, body)
                        result(NN, 0, tail_parts)

                    @block.scalar
                    def _(act):
                        def strip(t, parts):
                            return t.rearrange("p (m n) -> p m n", m=4)[:, :, 0:parts]

                        def root(c, h, parts):
                            s = slice(0, parts)
                            hold(act, var_ready, c + 1)
                            nc.scalar.activation(rs[h][s, :], var[h][s, :], ACT.Sqrt, bias=eps[s, 0:1],
                                                 scale=1.0 / D).then_inc(rs_ready, 1)

                        def square(c, h, parts):
                            s = slice(0, parts)
                            hold(act, z_ready, c + 1)
                            hold(act, var_ready, c - 1)
                            nc.scalar.activation(sq[h][s, :, :], z[h][s, :, :], ACT.Square).then_inc(sq_ready, 1)

                        def store(c, h, parts):
                            hold(act, res_ready, c + 1)
                            if not fast:
                                act.dma_start(out_view(c, parts), res[h][0:parts, :, :].rearrange("p q d -> p (q d)")
                                              ).then_inc(res_out[h], 16)
                            elif isinstance(c, int) and c == NN:
                                for d, s in last_group(out, res[h], True):
                                    act.dma_start(d, s).then_inc(res_out[h], 16)
                            else:
                                act.dma_start(by_block(out, c, N), res[h][:, :, :]).then_inc(res_out[h], 16)

                        def body(c, h, j, parts):
                            hold(act, hid_mm, 2 * (c - 1))
                            for g in range(2):
                                hold(act, turned, 2 * c + g + 1)
                                nc.scalar.copy(strip(flow_t[h][:, g * HC:(g + 1) * HC], parts), strip(bank[g][:, :], parts)
                                               ).then_inc(turned_out, 1)
                            hold(act, out_mm, c - 1)
                            for g in range(2):
                                hold(act, hid_mm, 2 * c + g + 1)
                                nc.scalar.activation(strip(hid[h][:, g * HC:(g + 1) * HC], parts),
                                                     strip(bank[2 + g][:, :], parts), ACT.Relu,
                                                     bias=b1nn[:, 0:1]).then_inc(hid_ready, 1)
                            if fast and not (isinstance(c, int) and c == 0):
                                square(c - 1, 1 - h, P)
                            if not (isinstance(c, int) and c < 2):
                                root(c - 2, h, P)
                            if not (isinstance(c, int) and c < 3):
                                store(c - 3, 1 - h, P)

                        over_chunks(act, body)
                        if fast:
                            square(NN, 0, tail_parts)
                        root(NN - 1, 1, P)
                        root(NN, 0, tail_parts)
                        store(NN - 2, 0, P)
                        store(NN - 1, 1, P)
                        store(NN, 0, tail_parts)

                    @block.vector
                    def _(dve):
                        chain = Chain(dve, nch, 3)
                        v = nc.vector

                        def wide(t, parts):
                            return t.unsqueeze(2).broadcast_to([parts, Q, D])

                        def centre(c, h, j, parts):
                            chain.body(c)
                            s = slice(0, parts)
                            hold(dve, out_mm, c + 1)
                            hold(dve, y_in[h], 16 * (j + 1))
                            hold(dve, z_ready, c)
                            hold(dve, sq_ready, c - 1)
                            hold(dve, res_ready, c - 1)
                            chain.step(v.tensor_tensor(out=s0[s, :, :], in0=bank[4 + h][s, :].rearrange(
                                "p (q d) -> p q d", d=D), in1=b2nn[s, :, :], op=ALU.add))
                            chain.step(v.scalar_tensor_tensor(out=s0[s, :, :], in0=s0[s, :, :], scalar=0.0,
                                                              in1=yb[h][s, :, :], op0=ALU.max, op1=ALU.add))
                            chain.step(v.tensor_reduce(mean[h][s, :], s0[s, :, :], AX, ALU.add))
                            v.scalar_tensor_tensor(out=z[h][s, :, :], in0=wide(mean[h][s, :], parts), scalar=-1.0 / D,
                                                   in1=s0[s, :, :], op0=ALU.mult, op1=ALU.add).then_inc(z_ready, 1)

                        def norm(c, h, j, parts):
                            s = slice(0, parts)
                            hold(dve, rs_ready, c + 1)
                            hold(dve, res_ready, c)
                            v.reciprocal(q2[h][s, :], rs[h][s, :]).then_inc(inverted, 1)
                            hold(dve, inverted, c + 1)
                            hold(dve, res_out[h], 16 * j)
                            v.tensor_tensor(out=res[h][s, :, :], in0=z[h][s, :, :], in1=wide(q2[h][s, :], parts),
                                            op=ALU.mult).then_inc(res_ready, 1)

                        def spread(c, h, parts):
                            s = slice(0, parts)
                            hold(dve, sq_ready, c + 1)
                            v.tensor_reduce(var[h][s, :], sq[h][s, :, :], AX, ALU.add).then_inc(var_ready, 1)

                        def body(c, h, j, parts):
                            if not (isinstance(c, int) and c < 2):
                                norm(c - 2, h, j - 1, P)
                            centre(c, h, j, parts)
                            if not (isinstance(c, int) and c == 0):
                                spread(c - 1, 1 - h, P)

                        over_chunks(dve, body)
                        norm(NN - 1, 1, NN // 2 - 1, P)
                        spread(NN, 0, tail_parts)
                        norm(NN, 0, NN // 2, tail_parts)


        short_way = nc.values_load(flag[0:1, 0:1], min_val=0, max_val=1)
        with nc.If(short_way), ExitStack() as way:
            scope.append(way)
            for k in range(3):
                layer_fast(k)
            edges_fast()
            nodes_out(True)
            scope.pop()
        with nc.Else(), ExitStack() as way:
            scope.append(way)
            clear_first()
            for k in range(3):
                layer(k)
            nodes_y()
            edges_general()
            nodes_out(False)


_INS = ['x', 'src', 'dst', 'edge_attr_16', 'L1_gnn_W1f', 'L1_gnn_b1f', 'L1_gnn_W2f', 'L1_gnn_b2f', 'L1_gnn_W1b',
        'L1_gnn_b1b', 'L1_gnn_W2b', 'L1_gnn_b2b', 'L1_gnn_W1n', 'L1_gnn_b1n', 'L1_gnn_W2n', 'L1_gnn_b2n']


def kernel(**inputs):
    import numpy as _np
    import concourse.bacc as _bacc
    from concourse import mybir as _mybir
    from concourse.bass_utils import run_bass_kernel_spmd as _run

    nc = _bacc.Bacc("TRN2", target_bir_lowering=False, num_devices=1)
    arrays, args = {}, []
    for name in _INS:
        a = _np.ascontiguousarray(inputs[name])
        arrays[f"in_{name}_dram"] = a
        args.append(nc.dram_tensor(f"in_{name}_dram", a.shape, _mybir.dt.from_np(a.dtype), kind="ExternalInput").ap())
    out = nc.dram_tensor("out_dram", inputs['x'].shape, _mybir.dt.float32, kind="ExternalOutput").ap()
    gnn(nc, *args, out)
    r = _run(nc, [arrays], core_ids=[0])
    return r.results[0]["out_dram"]
```

```python
from contextlib import ExitStack

import concourse.bass as bass
from concourse import mybir

ALU = mybir.AluOpType
ACT = mybir.ActivationFunctionType
F32 = mybir.dt.float32
I32 = mybir.dt.int32
U32 = mybir.dt.uint32
F16 = mybir.dt.float16
BF16 = mybir.dt.bfloat16
AX = mybir.AxisListType.X

P = 128
U = 4
Q = 16
EPS = 1e-5


def hold(eng, sem, value, alone=False):
    if isinstance(value, int):
        if value > 0:
            eng.wait_ge(sem, value)
        return
    eng.wait_ge(sem, value)
    if alone:
        eng.nop(nofuse=True)


def pool_hold(pool, sem, value):
    hold(pool, sem, value, alone=True)


class Chain:

    def __init__(self, eng, sem, per_body):
        self.eng, self.sem, self.per_body = eng, sem, per_body
        self.base, self.k = 0, 0

    def body(self, n):
        assert self.k in (0, self.per_body), self.k
        self.base, self.k = n * self.per_body, 0

    def step(self, ins):
        self.k += 1
        ins.then_inc(self.sem, 1)
        hold(self.eng, self.sem, self.base + self.k)


def over(eng, count, body, first=2):
    last = 2 if count % 2 == 0 else 1
    for c in range(first):
        body(c, c % 2, c // 2)
    with eng.Fori(0, (count - first - last) // 2) as i:
        body(i * 2 + first, 0, i + first // 2)
        body(i * 2 + first + 1, 1, i + first // 2)
    for c in range(count - last, count):
        body(c, c % 2, c // 2)


def over4(eng, count, body, first=6, by=4):
    assert by % 4 == 0
    last = (count - first) % by or by
    for c in range(first):
        body(c, c % 2, c // 2, c % 4, c // 4)
    with eng.Fori(0, (count - first - last) // by) as i:
        for c in range(first, first + by):
            body(i * by + c, c % 2, i * (by // 2) + c // 2, c % 4, i * (by // 4) + c // 4)
    for c in range(count - last, count):
        body(c, c % 2, c // 2, c % 4, c // 4)


def gnn(nc, x, src, dst, edge_attr, W1f, b1f, W2f, b2f, W1b, b1b, W2b, b2b, W1n, b1n, W2n, b2n, out):
    N, D = x.shape
    E = src.shape[0]
    DE = edge_attr.shape[1]
    H = W1f.shape[1]
    CE = P * U
    NCH = -(-E // CE)
    NCH += NCH % 2
    TILES = NCH * U
    PADS = NCH * CE - E
    TAILT, TAILP = divmod(E - (NCH - 1) * CE, P)
    assert 0 < E - (NCH - 1) * CE and TAILP
    WB = 4
    WIN = WB * P
    GB = 16
    SLACK = 12
    BIG = float(1 << 20)
    NT = -(-(N + P + PADS) // (P * 8)) * P * 8
    NQ = P * Q
    NN = N // NQ
    TAILN = (N - NN * NQ) // Q
    assert NN % 4 == 0 and TAILN * Q + NN * NQ == N and 0 < TAILN < P
    F = 2 * D + DE
    W0 = D + 1

    def dram(name, shape, dt):
        return nc.dram_tensor(name, shape, dt).ap()

    pad_ids = [dram("src_padded", [NCH * CE], I32), dram("dst_padded", [NCH * CE], I32)]
    table = [dram("sums0", [NT, 2 * W0], F32), dram("sums1", [NT, 2 * D], F32), dram("sums2", [NT, 2 * D], F32)]
    means = [dram("means1", [NT, D], F32), dram("means2", [NT, D], F32), dram("y_rows", [NT, D], F32)]
    NBLK = NT // P
    NG = NBLK // GB
    assert NBLK % GB == 0
    BPT = N * P // (E * P)
    partial = dram("partial", [NG, P, GB * D], F32)
    backward = [dram(f"backward{i}", [NT, D], F32) for i in range(2)]
    y_lanes = dram("y_lanes", [P, NT // P + WB, D], F32)
    place_dram = dram("place_dram", [NCH, CE], F16)
    base_dram = dram("base_dram", [TILES], I32)
    flows = dram("flows", [NT, 2 * D], F32)
    y_table = dram("y_table", [N, D], F32)

    with ExitStack() as ctx:
        scope = [ctx]

        def sb(name, shape, dt=F32):
            return ctx.enter_context(nc.sbuf_tensor(name, shape, dt))

        def sem(name):
            return scope[-1].enter_context(nc.semaphore(name))

        bank = [ctx.enter_context(nc.psum_tensor(f"bank{i}", [P, 512], F32)) for i in range(8)]

        ident = sb("ident", [P, P])
        before = sb("before", [P, U, P])
        trash = sb("trash", [P, 1])
        half = sb("half", [P, U])
        pad_row = sb("pad_row", [1, PADS], I32)
        zeros = sb("zeros", [P, 2 * NT // P])
        col = [sb("src_col", [P, NCH, U], I32), sb("dst_col", [P, NCH, U], I32)]
        get = [sb("src_get", [P, NCH, U], I32), sb("dst_get", [P, NCH, U], I32)]
        get_row = sb("src_get_row", [P, NCH, U], I32)
        put_row = sb("src_put_row", [P, NCH, U], I32)
        trash_row = sb("trash_row", [P, 1])
        put_dst = sb("put_dst", [P, NCH, U], I32)
        rden = sb("rden", [P, NCH, U])
        eps = sb("eps", [P, 1])
        ones = sb("ones", [1, P])
        w1e = sb("w1e", [F, 2 * H])
        w2e = sb("w2e", [2 * H, 2 * D])
        w1n = sb("w1n", [4 * D, 2 * H])
        w2n = sb("w2n", [2 * H, 2 * D])
        b1e = sb("b1e", [2 * H, 1])
        b1nn = sb("b1nn", [2 * H, 1])
        b2e = sb("b2e", [1, 2 * D])
        b2nn = sb("b2nn", [P, Q, D])
        rden_n = sb("rden_n", [P, NBLK])
        node_sums = sb("node_sums", [P, NBLK + WB, W0])
        base_row = sb("base_row", [P, TILES], I32)
        hot_at = sb("hot_at", [P, NCH, U])
        steps = sb("steps", [P, WIN], F16)
        flag = sb("flag", [1, 1], I32)

        SRC, DST = 0, 1

        consts_ready, w_clear, loaded, padded = (
            sem("consts_ready"), sem("w_clear"), sem("loaded"), sem("padded"))
        mid, pad_written, nat_in, turned_ids, base_out, base_in, ich, counted = (
            sem("mid"), sem("pad_written"), sem("nat_in"), sem("turned_ids"),
            sem("base_out"), sem("base_in"), sem("ids_chain"), sem("counted"))
        nat_ready, base_ready, bad_ready = sem("nat_ready"), sem("base_ready"), sem("bad_ready")
        with ExitStack() as lctx:
            def tmp(name, shape, dt=F32):
                return lctx.enter_context(nc.sbuf_tensor(name, shape, dt))

            nat = [tmp("nat_src", [NCH, CE], I32), tmp("nat_dst", [NCH, CE], I32)]
            nat_f = [tmp("nat_src_f", [NCH, CE]), tmp("nat_dst_f", [NCH, CE])]
            base_nat = tmp("base_nat", [NCH, U], I32)
            col_f = tmp("col_f", [P, NCH, U])
            rel, is_pad, low, due = (tmp(n, [P, TILES]) for n in ("rel", "is_pad", "low", "due"))
            tops, bads, bad = tmp("tops", [P, 3]), tmp("bads", [P, 3]), tmp("bad", [P, 1])
            ones_col = tmp("ones_col", [P, 1])
            blocks, groups, row_part = tmp("blocks", [P, NCH, U], I32), tmp("groups", [P, NCH, U], I32), tmp("row_part", [P, NCH, U])
            trash_i = tmp("trash_i", [P, 1, 1], I32)
            place, place_nat = tmp("place", [P, NCH, U]), tmp("place_nat", [NCH, U, P], F16)
            place_ready, place_turned, place_out = sem("place_ready"), sem("place_turned"), sem("place_out")
            HB = (NBLK + WB) * 3 // 4
            with nc.Block() as block:
                @block.gpsimd
                def _(pool):
                    nc.gpsimd.iota(pad_row[:, :], [[1, PADS]], base=N + P, channel_multiplier=0).then_inc(padded, 1)
                    nc.gpsimd.memset(ident[:, :], 0.0).then_inc(mid, 1)
                    nc.gpsimd.memset(before[:, :, :], 1.0).then_inc(mid, 1)
                    pool.wait_ge(mid, 2)
                    nc.gpsimd.affine_select(out=ident[:, :], in_=ident[:, :], compare_op=ALU.not_equal, fill=1.0,
                                            base=0, pattern=[[-1, P]], channel_multiplier=1
                                            ).then_inc(consts_ready, 1)
                    nc.gpsimd.iota(trash[:, :], [[0, 1]], base=N, channel_multiplier=1,
                                   allow_small_or_imprecise_dtypes=True)
                    nc.gpsimd.iota(half[:, :], [[0, U // 2], [1, 2]], base=0, channel_multiplier=0,
                                   allow_small_or_imprecise_dtypes=True)
                    nc.gpsimd.iota(steps[:, :], [[1, WIN]], base=0, channel_multiplier=0,
                                   allow_small_or_imprecise_dtypes=True)
                    nc.gpsimd.iota(due[:, :], [[-BPT, TILES]], base=SLACK, channel_multiplier=0,
                                   allow_small_or_imprecise_dtypes=True).then_inc(consts_ready, 1)
                    nc.gpsimd.affine_select(out=before[:, :, :], in_=before[:, :, :], compare_op=ALU.is_gt, fill=0.0,
                                            base=0, pattern=[[0, U], [-1, P]], channel_multiplier=1)
                    nc.gpsimd.memset(node_sums[:, 0:HB, :], 0.0)

                @block.vector
                def _(dve):
                    v = nc.vector
                    count = [0]

                    def step(ins):
                        count[0] += 1
                        ins.then_inc(ich, 1)
                        dve.wait_ge(ich, count[0])

                    v.memset(zeros[:, :], 0.0)
                    for t in (w2e, w1n, w2n):
                        v.memset(t[:, :], 0.0).then_inc(w_clear, 1)
                    v.memset(ones[:, :], 1.0)
                    v.memset(eps[:, :], EPS)
                    v.memset(node_sums[:, HB:, :], 0.0)
                    step(v.memset(ones_col[:, :], 1.0))
                    dve.wait_ge(nat_in, 32)
                    for k in (SRC, DST):
                        v.tensor_scalar(nat_f[k][:, :], nat[k][:, :], 0.0, None, ALU.add).then_inc(nat_ready, 1)
                    firsts = nat[DST][:, :].rearrange("q (a j) -> q a j", a=U)[:, :, 0:1]
                    assert P == 1 << 7
                    v.tensor_scalar(base_nat[:, :].unsqueeze(2), firsts, 7, None, ALU.arith_shift_right
                                    ).then_inc(base_ready, 1)
                    for k in (SRC, DST):
                        dve.wait_ge(turned_ids, k + 1)
                        for a in range(U):
                            ins = v.tensor_copy(col_f[:, :, a], bank[U * k + a][:, 0:NCH])
                        step(ins)
                        step(v.tensor_scalar(col[k][:, :, :], col_f[:, :, :], 0.0, None, ALU.add))
                        step(v.tensor_scalar(get[k][:, :, :], col_f[:, :, :], float(N - 1), None, ALU.min))

                    def rows_of(out, ids):
                        assert P == 128 and GB == 16
                        at = tuple(slice(0, m) for m in out.shape)
                        lo7, lo11, part = (t[at] for t in (blocks, groups, row_part))
                        step(v.tensor_scalar(lo7, ids, 7, None, ALU.arith_shift_right))
                        step(v.tensor_scalar(lo11, ids, 11, None, ALU.arith_shift_right))
                        step(v.tensor_scalar(part, ids, float(GB), None, ALU.mult))
                        step(v.scalar_tensor_tensor(out=part, in0=lo7, scalar=float(1 - GB * P), in1=part,
                                                    op0=ALU.mult, op1=ALU.add))
                        step(v.scalar_tensor_tensor(out=out, in0=lo11, scalar=float(GB * P - GB), in1=part,
                                                    op0=ALU.mult, op1=ALU.add))

                    rows_of(get_row[:, :, :], get[SRC][:, :, :])
                    rows_of(put_row[:, :, :], col[SRC][:, :, :])
                    flat = col_f[:, :, :].rearrange("p c u -> p (c u)")
                    dve.wait_ge(base_in, 16)
                    step(v.scalar_tensor_tensor(out=rel[:, :], in0=base_row[:, :], scalar=float(-P), in1=flat,
                                                op0=ALU.mult, op1=ALU.add))
                    step(v.tensor_scalar(is_pad[:, :], flat, float(N), None, ALU.is_ge))
                    hot = hot_at[:, :, :].rearrange("p c u -> p (c u)")
                    step(v.scalar_tensor_tensor(out=hot, in0=is_pad[:, :], scalar=-BIG, in1=rel[:, :],
                                                op0=ALU.mult, op1=ALU.add))
                    step(v.scalar_tensor_tensor(out=low[:, :], in0=is_pad[:, :], scalar=BIG, in1=rel[:, :],
                                                op0=ALU.mult, op1=ALU.add))
                    dve.wait_ge(consts_ready, 2)
                    step(v.tensor_scalar(trash_i[:, :, :], trash[:, :].unsqueeze(2), 0.0, None, ALU.add))
                    rows_of(trash_row[:, :].unsqueeze(2), trash_i[:, :, :])
                    step(v.scalar_tensor_tensor(out=due[:, :], in0=base_row[:, :], scalar=1.0, in1=due[:, :],
                                                op0=ALU.mult, op1=ALU.add))
                    v.tensor_reduce(tops[:, 0:1], hot, AX, ALU.max)
                    v.tensor_reduce(tops[:, 1:2], low[:, :], AX, ALU.min)
                    step(v.tensor_reduce(tops[:, 2:3], due[:, :], AX, ALU.min))
                    v.tensor_scalar(bads[:, 0:1], tops[:, 0:1], float(WIN), None, ALU.is_ge)
                    step(v.tensor_scalar(bads[:, 1:3], tops[:, 1:3], 0.0, None, ALU.is_lt))
                    v.tensor_reduce(bad[:, :], bads[:, :], AX, ALU.add).then_inc(bad_ready, 1)
                    v.tensor_scalar(place[:, :, :], hot_at[:, :, :], -1.0, float(WIN), ALU.max, ALU.min
                                    ).then_inc(place_ready, 1)
                    dve.wait_ge(place_turned, 1)
                    for u in range(U):
                        ins = v.tensor_copy(place_nat[:, u, :], bank[U + u][0:NCH, 0:P])
                    ins.then_inc(place_ready, 1)
                    dve.wait_ge(counted, 1)
                    v.tensor_scalar(flag[:, :], bank[0][0:1, 0:1], 0.0, None, ALU.is_equal)

                @block.tensor
                def _(pe):
                    pe.wait_ge(consts_ready, 1)
                    for k in (SRC, DST):
                        pe.wait_ge(nat_ready, k + 1)
                        for a in range(U):
                            ins = nc.tensor.transpose(bank[U * k + a][:, 0:NCH], nat_f[k][:, a * P:(a + 1) * P],
                                                      ident[0:NCH, 0:NCH])
                        ins.then_inc(turned_ids, 1)
                    pe.wait_ge(bad_ready, 1)
                    nc.tensor.matmul(bank[0][0:1, 0:1], bad[:, :], ones_col[:, :], start=True, stop=True
                                     ).then_inc(counted, 1)
                    pe.wait_ge(place_ready, 1)
                    for u in range(U):
                        ins = nc.tensor.transpose(bank[U + u][0:NCH, 0:P], place[:, :, u], ident[:, :])
                    ins.then_inc(place_turned, 1)

                @block.sync
                def _(sp):
                    for k, ids in ((SRC, src), (DST, dst)):
                        sp.dma_start(pad_ids[k][0:E].rearrange("(a b) -> a b", a=16),
                                     ids.rearrange("(a b) -> a b", a=16)).then_inc(pad_written, 16)
                    sp.wait_ge(padded, 1)
                    for k in (SRC, DST):
                        sp.dma_start(pad_ids[k][E:].unsqueeze(0), pad_row[:, :]).then_inc(pad_written, 16)
                    sp.wait_ge(pad_written, 64)
                    for k in (SRC, DST):
                        sp.dma_start(nat[k][:, :], pad_ids[k].rearrange("(c e) -> c e", c=NCH)).then_inc(nat_in, 16)
                    sp.wait_ge(base_ready, 1)
                    sp.dma_start(base_dram.rearrange("(q a) -> q a", a=U), base_nat[:, :]).then_inc(base_out, 16)
                    sp.wait_ge(base_out, 16)
                    sp.dma_start(base_row[:, :], base_dram.unsqueeze(0).broadcast_to([P, TILES])
                                 ).then_inc(base_in, 16)
                    sp.wait_ge(base_in, 16)
                    sp.wait_ge(place_ready, 2)
                    sp.dma_start(place_dram, place_nat[:, :, :].rearrange("c u p -> c (u p)")).then_inc(place_out, 16)
                    sp.wait_ge(place_out, 16)

                @block.scalar
                def _(act):
                    act.wait_ge(w_clear, 3)
                    for dst_t, src_t in (
                        (w1e[:, 0:H], W1f), (w1e[0:D, H:], W1b[D:2 * D, :]), (w1e[D:2 * D, H:], W1b[0:D, :]),
                        (w1e[2 * D:, H:], W1b[2 * D:, :]), (w2e[0:H, 0:D], W2f), (w2e[H:, D:], W2b),
                        (w1n[0:2 * D, 0:H], W1n), (w1n[2 * D:, H:], W1n), (w2n[0:H, 0:D], W2n), (w2n[H:, D:], W2n),
                        (b1e[0:H, :], b1f.unsqueeze(1)), (b1e[H:, :], b1b.unsqueeze(1)),
                        (b1nn[0:H, :], b1n.unsqueeze(1)), (b1nn[H:, :], b1n.unsqueeze(1)),
                        (b2e[:, 0:D], b2f.unsqueeze(0)), (b2e[:, D:], b2b.unsqueeze(0)),
                        (b2nn[:, :, :], b2n.unsqueeze(0).unsqueeze(0).broadcast_to([P, Q, D])),
                    ):
                        act.dma_start(dst_t, src_t).then_inc(loaded, 16)
                    act.wait_ge(loaded, 17 * 16)

        def clear_first():
            first_zeroed = sem("first_zeroed")
            with nc.Block() as block:
                @block.sync
                def _(sp):
                    sp.dma_start(table[0].rearrange("(p r) d -> p (r d)", p=P).rearrange("p (a b) -> p a b", a=W0),
                                 zeros[:, :].unsqueeze(1).broadcast_to([P, W0, 2 * NT // P])
                                 ).then_inc(first_zeroed, 16)
                    sp.wait_ge(first_zeroed, 16)

        row_of = [ids.rearrange("(c e) -> c e", e=CE) for ids in pad_ids]

        def same_id(rows, k, c):
            return dict(in0=rows.rearrange("p (u j) -> p u j", u=U),
                        in1=get_col(k, c).broadcast_to([P, U, P]), op=ALU.is_equal)

        def get_col(k, c):
            return col[k][:, bass.ds(c, 1), :].rearrange("p a u -> p (a u)").unsqueeze(2)

        def layer(k):
            w_in = D if k == 0 else table[k - 1].shape[1]
            w_out = table[k].shape[1] // 2
            w_g = w_in + (k == 0)
            halves = table[k].rearrange("n (a w) -> (n a) w", a=2)
            source = x if k == 0 else table[k - 1]
            nxt = (table + [flows])[k + 1]
            zero_rows = NT // NCH // P * P
            assert zero_rows * NCH <= NT
            with ExitStack() as lctx:
                def lsb(name, shape, dt=F32):
                    return [lctx.enter_context(nc.sbuf_tensor(f"{name}{k}_{i}", shape, dt)) for i in range(2)]

                def lsem(name, n=0):
                    if n:
                        return [scope[-1].enter_context(nc.semaphore(f"{name}{k}_{i}")) for i in range(n)]
                    return scope[-1].enter_context(nc.semaphore(f"{name}{k}"))

                rows = lsb("rows", [P, CE], I32)
                same = lsb("same", [P, U, P])
                got = lsb("got", [P, U, w_g])
                vals = lsb("vals", [P, U, D]) if k else got
                sums = lsb("sums_out", [P, U, w_out])
                ix_get = lsb("ix_get", [P, U], I32)
                ix_put = lsb("ix_put", [P, U], I32)
                prod, cnt, t1 = lsb("prod", [P, U, P])[0], lsb("cnt", [P, U])[0], lsb("t1", [P, U])[0]
                rows_in, gathered, scattered = lsem("rows_in", 2), lsem("gathered", 2), lsem("scattered", 2)
                get_ready, put_ready, same_ready = lsem("get_ready"), lsem("put_ready"), lsem("same_ready")
                vals_ready, summed, sums_ready, zeroed = lsem("vals_ready"), lsem("summed"), lsem("sums_ready"), lsem("zeroed")
                dve_chain = lsem("dve_chain")
                ones_set = lsem("ones_set")

                with nc.Block() as block:
                    @block.sync
                    def _(sp):
                        per = NT // P // NCH
                        left = NT - per * P * NCH
                        w = nxt.shape[1]

                        def body(c, h, j):
                            hold(sp, same_ready, c - 1)
                            sp.dma_start(rows[h][:, :], row_of[DST][bass.ds(c, 1), :].broadcast_to([P, CE])
                                         ).then_inc(rows_in[h], 16)
                            sp.dma_start(nxt[bass.ds(c * (per * P), per * P), :].rearrange("(p r) d -> p (r d)", p=P),
                                         zeros[:, 0:per * w]).then_inc(zeroed, 16)

                        over(sp, NCH, body)
                        for r in range(NT - left, NT, P):
                            sp.dma_start(nxt[r:r + P, :], zeros[:, 0:w]).then_inc(zeroed, 16)
                        sp.wait_ge(zeroed, 16 * (NCH + left // P))

                    @block.vector
                    def _(dve):
                        chain = Chain(dve, dve_chain, (7, 4, 1)[k])
                        if k == 0:
                            for h in range(2):
                                nc.vector.memset(got[h][:, :, D:], 1.0).then_inc(ones_set, 1)

                        def stage_get(c, h):
                            nc.vector.tensor_scalar(ix_get[h][:, :], get[SRC][:, bass.ds(c, 1), :].squeeze(1), 0.0,
                                                    None, ALU.add).then_inc(get_ready, 1)

                        def body(c, h, j):
                            if isinstance(c, int) and c == 0:
                                stage_get(0, 0)
                            if not (isinstance(c, int) and c == NCH - 1):
                                hold(dve, gathered[1 - h], 16 * U * (j + h))
                                stage_get(c + 1, 1 - h)
                            chain.body(c)
                            hold(dve, rows_in[h], 16 * (j + 1))
                            hold(dve, summed, c - 1)
                            ins = nc.vector.tensor_tensor(out=same[h][:, :, :], **same_id(rows[h][:, :], DST, c))
                            ins.then_inc(same_ready, 1)
                            if k == 0:
                                hold(dve, same_ready, c + 1)
                                chain.step(nc.vector.tensor_tensor(out=prod[:, :, :], in0=same[h][:, :, :],
                                                                   in1=before[:, :, :], op=ALU.mult))
                                chain.step(nc.vector.tensor_reduce(cnt[:, :], prod[:, :, :], AX, ALU.add))
                                ids = col[DST][:, bass.ds(c, 1), :].squeeze(1)
                                chain.step(nc.vector.tensor_scalar(cnt[:, :], cnt[:, :], 1.0, None, ALU.min))
                                chain.step(nc.vector.tensor_scalar(t1[:, :], ids, -1.0, trash[:, 0:1],
                                                                   ALU.mult, ALU.add))
                                chain.step(nc.vector.tensor_tensor(out=t1[:, :], in0=t1[:, :], in1=cnt[:, :],
                                                                   op=ALU.mult))
                                chain.step(nc.vector.tensor_tensor(out=t1[:, :], in0=t1[:, :], in1=ids, op=ALU.add))
                                chain.step(nc.vector.tensor_scalar(put_dst[:, bass.ds(c, 1), :].squeeze(1), t1[:, :],
                                                                   2.0, None, ALU.mult))
                            else:
                                hold(dve, gathered[h], 16 * U * (j + 1))
                                hold(dve, summed, c - 1)
                                g = got[h][:, :, :]
                                o = w_in // 2
                                r = rden[:, bass.ds(c, 1), :].squeeze(1)
                                hold(dve, vals_ready, c)
                                if k == 1:
                                    chain.step(nc.vector.tensor_tensor(
                                        out=cnt[:, :].unsqueeze(2), in0=g[:, :, D:D + 1], in1=g[:, :, o + D:o + D + 1],
                                        op=ALU.add))
                                    chain.step(nc.vector.tensor_scalar(t1[:, :], cnt[:, :], 1.0, None, ALU.max))
                                    chain.step(nc.vector.reciprocal(cnt[:, :], t1[:, :]))
                                    nc.vector.tensor_scalar(r, cnt[:, :], 1.0, None, ALU.mult)
                                    r = cnt[:, :]
                                chain.step(nc.vector.tensor_tensor(out=vals[h][:, :, :], in0=g[:, :, 0:D],
                                                                   in1=g[:, :, o:o + D], op=ALU.add))
                                nc.vector.tensor_tensor(out=vals[h][:, :, :], in0=vals[h][:, :, :],
                                                        in1=r.unsqueeze(2).broadcast_to([P, U, D]),
                                                        op=ALU.mult).then_inc(vals_ready, 1)
                            for a in range(2):
                                hold(dve, scattered[a], 16 * (U // 2) * (c - 1))
                            nc.vector.tensor_tensor(out=ix_put[h][:, :], in0=put_dst[:, bass.ds(c, 1), :].squeeze(1),
                                                    in1=half[:, :], op=ALU.add).then_inc(put_ready, 1)

                        over(dve, NCH, body)

                    @block.gpsimd
                    def _(pool):
                        if k == 0:
                            pool.wait_ge(ones_set, 2)

                        def body(s, h, j, gather=True, scatter=True):
                            if gather:
                                pool_hold(pool, get_ready, s + 1)
                                pool_hold(pool, vals_ready if k else summed, s - 1)
                            if scatter:
                                pool_hold(pool, put_ready, s - 1)
                                pool_hold(pool, sums_ready, s - 1)
                            for u in range(U):
                                if gather:
                                    pool.indirect_dma_start(
                                        got[h][:, u, 0:w_in], None, source,
                                        bass.IndirectOffsetOnAxis(ix_get[h][:, u:u + 1].bitcast(U32), 0)
                                    ).then_inc(gathered[h], 16)
                                if scatter:
                                    pool_hold(pool, scattered[u % 2], 16 * ((U // 2) * (s - 2) + u // 2))
                                    pool.indirect_dma_start(
                                        halves, bass.IndirectOffsetOnAxis(ix_put[h][:, u:u + 1].bitcast(U32), 0),
                                        sums[h][:, u, :], None, compute_op=ALU.add).then_inc(scattered[u % 2], 16)

                        body(0, 0, 0, scatter=False)
                        body(1, 1, 0, scatter=False)
                        body(2, 0, 1)
                        body(3, 1, 1)
                        with pool.Fori(0, (NCH - 4) // 2) as i:
                            body(i * 2 + 4, 0, i + 2)
                            body(i * 2 + 5, 1, i + 2)
                        body(NCH, 0, NCH // 2, gather=False)
                        body(NCH + 1, 1, NCH // 2, gather=False)
                        for a in range(2):
                            pool.wait_ge(scattered[a], 16 * (U // 2) * NCH)

                    @block.tensor
                    def _(pe):
                        if k == 0:
                            pe.wait_ge(ones_set, 2)

                        def body(c, h, j):
                            hold(pe, same_ready, c + 1)
                            if k:
                                hold(pe, vals_ready, c + 1)
                            else:
                                hold(pe, gathered[h], 16 * U * (j + 1))
                            hold(pe, sums_ready, c - 1)
                            for u in range(U):
                                ins = nc.tensor.matmul(bank[h][:, u * w_out:(u + 1) * w_out], same[h][:, u, :],
                                                       vals[h][:, u, :], start=True, stop=True)
                            ins.then_inc(summed, 1)

                        over(pe, NCH, body)

                    @block.scalar
                    def _(act):
                        def body(c, h, j):
                            hold(act, summed, c + 1)
                            for a in range(2):
                                hold(act, scattered[a], 16 * (U // 2) * (c - 1))
                            nc.scalar.copy(sums[h][:, :, :], bank[h][:, 0:U * w_out].rearrange(
                                "p (u w) -> p u w", u=U)).then_inc(sums_ready, 1)

                        over(act, NCH, body)


        def node_views(t, width):
            main = t[0:NN * NQ, :].rearrange("(c p q) d -> c p (q d)", p=P, q=Q)
            tail = t[NN * NQ:N, :].rearrange("(p q) d -> p (q d)", q=Q)

            def view(c, parts):
                return tail if parts < P else main[bass.ds(c, 1), :, :].squeeze(0)
            return view

        def over_nodes(eng, body):
            body(0, 0, 0, P)
            body(1, 1, 0, P)
            with eng.Fori(0, NN // 2 - 1) as i:
                body(i * 2 + 2, 0, i + 1, P)
                body(i * 2 + 3, 1, i + 1, P)
            body(NN, 0, NN // 2, TAILN)

        def nodes_y():
            with ExitStack() as lctx:
                def pair(name, shape, dt=F32):
                    return [lctx.enter_context(nc.sbuf_tensor(f"{name}_{i}", shape, dt)) for i in range(2)]

                xb, ta, tb, tc = pair("xb", [P, Q, D]), pair("ta", [P, Q, 2 * W0]), pair("tb", [P, Q, 2 * D]), pair("tc", [P, Q, 2 * D])
                tbc, z, sq = pair("tbc", [P, Q, 2 * D]), pair("z", [P, Q, D]), pair("sq", [P, Q, D])
                s0, yo = pair("s0", [P, Q, D])[0], pair("yo", [P, Q, D])
                q1, q2, mean, var, rs = (pair(n, [P, Q]) for n in ("q1", "q2", "mean", "var", "rs"))
                nodes_in, y_out = [sem("nodes_in0"), sem("nodes_in1")], [sem("y_out0"), sem("y_out1")]
                later_summed, z_ready, sq_ready, var_ready, rs_ready, y_ready, ych = (
                    sem("later_summed"), sem("z_ready"), sem("sq_ready"), sem("var_ready"), sem("rs_ready"),
                    sem("y_ready"), sem("ych"))
                views = [node_views(t, 0) for t in (x, table[0], table[1], table[2])]
                y_view = node_views(y_table, D)
                with nc.Block() as block:
                    @block.sync
                    def _(sp):
                        def body(c, h, j, parts):
                            hold(sp, y_ready, c - 1)
                            for b, v in zip((xb, ta, tb, tc), views):
                                sp.dma_start(b[h][0:parts, :, :].rearrange("p q d -> p (q d)"), v(c, parts)
                                             ).then_inc(nodes_in[h], 16)

                        over_nodes(sp, body)

                    @block.gpsimd
                    def _(pool):
                        def body(c, h, j, parts):
                            pool_hold(pool, nodes_in[h], 64 * (j + 1))
                            pool_hold(pool, y_ready, c - 1)
                            nc.gpsimd.tensor_tensor(out=tbc[h][0:parts, :, :], in0=tb[h][0:parts, :, :],
                                                    in1=tc[h][0:parts, :, :], op=ALU.add).then_inc(later_summed, 1)

                        over_nodes(pool, body)

                    @block.vector
                    def _(dve):
                        chain = Chain(dve, ych, 10)
                        v = nc.vector

                        def body(c, h, j, parts):
                            chain.body(c)
                            s = slice(0, parts)

                            def wide(t):
                                return t.unsqueeze(2).broadcast_to([parts, Q, D])
                            hold(dve, nodes_in[h], 64 * (j + 1))
                            t = ta[h][s, :, :]
                            chain.step(v.tensor_tensor(out=q1[h][s, :].unsqueeze(2), in0=t[:, :, D:W0],
                                                       in1=t[:, :, W0 + D:], op=ALU.add))
                            chain.step(v.tensor_scalar(q2[h][s, :], q1[h][s, :], 1.0, None, ALU.max))
                            chain.step(v.reciprocal(q1[h][s, :], q2[h][s, :]))
                            chain.step(v.tensor_tensor(out=s0[s, :, :], in0=t[:, :, 0:D], in1=t[:, :, W0:W0 + D], op=ALU.add))
                            hold(dve, later_summed, c + 1)
                            chain.step(v.tensor_tensor(out=s0[s, :, :], in0=s0[s, :, :], in1=tbc[h][s, :, 0:D], op=ALU.add))
                            chain.step(v.tensor_tensor(out=s0[s, :, :], in0=s0[s, :, :], in1=tbc[h][s, :, D:], op=ALU.add))
                            chain.step(v.scalar_tensor_tensor(out=s0[s, :, :], in0=s0[s, :, :], scalar=0.25,
                                                              in1=wide(q1[h][s, :]), op0=ALU.mult, op1=ALU.mult))
                            chain.step(v.scalar_tensor_tensor(out=s0[s, :, :], in0=xb[h][s, :, :], scalar=1.25,
                                                              in1=s0[s, :, :], op0=ALU.mult, op1=ALU.add))
                            chain.step(v.tensor_reduce(mean[h][s, :], s0[s, :, :], AX, ALU.add))
                            v.scalar_tensor_tensor(out=z[h][s, :, :], in0=wide(mean[h][s, :]), scalar=-1.0 / D,
                                                   in1=s0[s, :, :], op0=ALU.mult, op1=ALU.add).then_inc(z_ready, 1)
                            hold(dve, sq_ready, c + 1)
                            v.tensor_reduce(var[h][s, :], sq[h][s, :, :], AX, ALU.add).then_inc(var_ready, 1)
                            hold(dve, rs_ready, c + 1)
                            chain.step(v.reciprocal(q2[h][s, :], rs[h][s, :]))
                            hold(dve, y_out[h], 16 * j)
                            v.tensor_tensor(out=yo[h][s, :, :], in0=z[h][s, :, :], in1=wide(q2[h][s, :]),
                                            op=ALU.mult).then_inc(y_ready, 1)

                        over_nodes(dve, body)

                    @block.scalar
                    def _(act):
                        def body(c, h, j, parts):
                            s = slice(0, parts)
                            hold(act, z_ready, c + 1)
                            nc.scalar.activation(sq[h][s, :, :], z[h][s, :, :], ACT.Square).then_inc(sq_ready, 1)
                            hold(act, var_ready, c + 1)
                            nc.scalar.activation(rs[h][s, :], var[h][s, :], ACT.Sqrt, bias=eps[s, 0:1],
                                                 scale=1.0 / D).then_inc(rs_ready, 1)
                            hold(act, y_ready, c + 1)
                            act.dma_start(y_view(c, parts), yo[h][s, :, :].rearrange("p q d -> p (q d)")
                                          ).then_inc(y_out[h], 16)

                        over_nodes(act, body)
                        act.wait_ge(y_out[0], 16 * (NN // 2 + 1))
                        act.wait_ge(y_out[1], 16 * (NN // 2))

        def edges_general():
            with ExitStack() as lctx:
                def pair(name, shape, dt=F32):
                    return [lctx.enter_context(nc.sbuf_tensor(f"{name}_{i}", shape, dt)) for i in range(2)]

                rows = [pair("e_rows_src", [P, CE], I32), pair("e_rows_dst", [P, CE], I32)]
                same = [pair("e_same_src", [P, U, P]), pair("e_same_dst", [P, U, P])]
                feat, feat_t, hid = pair("feat", [P, U, F]), pair("feat_t", [F, CE]), pair("hid", [2 * H, CE])
                flow, sums = pair("flow", [P, U, 2 * D]), pair("e_sums", [P, U, 2 * D])
                prod, cnt, t1 = pair("e_prod", [P, U, P])[0], pair("e_cnt", [P, U])[0], pair("e_t1", [P, U])[0]
                ix_get = [pair("e_get_src", [P, U], I32), pair("e_get_dst", [P, U], I32)]
                ix_put = [pair("e_put_src", [P, U], I32), pair("e_put_dst", [P, U], I32)]
                rows_in, attrs_in, gathered = ([sem(f"{n}{h}") for h in range(2)] for n in ("e_rows_in", "e_attrs_in", "e_gathered"))
                scattered = [sem("e_scattered_src"), sem("e_scattered_dst")]
                (get_ready, put_ready, same_ready, turned, turned_out, hid_mm, hid_ready, flow_mm, flow_ready, summed,
                 sums_ready, ech) = (sem(f"e_{n}") for n in (
                     "get_ready", "put_ready", "same_ready", "turned", "turned_out", "hid_mm", "hid_ready", "flow_mm",
                     "flow_ready", "summed", "sums_ready", "chain"))
                flow_rows = flows.rearrange("n (a w) -> (n a) w", a=2)
                attr_main = edge_attr[0:(NCH - 1) * CE, :].rearrange("(c u p) d -> c p u d", p=P, u=U)
                attr_tail = edge_attr[(NCH - 1) * CE:E - TAILP, :].rearrange("(u p) d -> p u d", p=P)
                with nc.Block() as block:
                    @block.sync
                    def _(sp):
                        def body(c, h, j):
                            hold(sp, same_ready, c - 1)
                            for k in (SRC, DST):
                                sp.dma_start(rows[k][h][:, :], row_of[k][bass.ds(c, 1), :].broadcast_to([P, CE])
                                             ).then_inc(rows_in[h], 16)
                            hold(sp, turned, c - 1)
                            if isinstance(c, int) and c == NCH - 1:
                                sp.dma_start(feat[h][:, 0:TAILT, 2 * D:], attr_tail).then_inc(attrs_in[h], 16)
                                sp.dma_start(feat[h][0:TAILP, TAILT:TAILT + 1, 2 * D:], edge_attr[E - TAILP:E, :]
                                             .unsqueeze(1)).then_inc(attrs_in[h], 16)
                            else:
                                sp.dma_start(feat[h][:, :, 2 * D:], attr_main[bass.ds(c, 1), :, :, :].squeeze(0)
                                             ).then_inc(attrs_in[h], 16)

                        over(sp, NCH, body)

                    @block.gpsimd
                    def _(pool):
                        def body(s, h, j, gather=True, scatter=True):
                            if gather:
                                pool_hold(pool, get_ready, s + 1)
                                pool_hold(pool, turned, s - 1)
                            if scatter:
                                pool_hold(pool, put_ready, s - 1)
                                pool_hold(pool, sums_ready, s - 1)
                            for u in range(U):
                                for k, at in ((DST, 0), (SRC, D)):
                                    if gather:
                                        pool.indirect_dma_start(
                                            feat[h][:, u, at:at + D], None, y_table,
                                            bass.IndirectOffsetOnAxis(ix_get[k][h][:, u:u + 1].bitcast(U32), 0)
                                        ).then_inc(gathered[h], 16)
                                for k, at in ((DST, 0), (SRC, D)):
                                    if scatter:
                                        pool_hold(pool, scattered[k], 16 * (U * (s - 2) + u))
                                        pool.indirect_dma_start(
                                            flow_rows, bass.IndirectOffsetOnAxis(ix_put[k][h][:, u:u + 1].bitcast(U32), 0),
                                            sums[h][:, u, at:at + D], None, compute_op=ALU.add).then_inc(scattered[k], 16)

                        body(0, 0, 0, scatter=False)
                        body(1, 1, 0, scatter=False)
                        body(2, 0, 1)
                        body(3, 1, 1)
                        with pool.Fori(0, (NCH - 4) // 2) as i:
                            body(i * 2 + 4, 0, i + 2)
                            body(i * 2 + 5, 1, i + 2)
                        body(NCH, 0, NCH // 2, gather=False)
                        body(NCH + 1, 1, NCH // 2, gather=False)
                        for k in (SRC, DST):
                            pool.wait_ge(scattered[k], 16 * U * NCH)

                    @block.vector
                    def _(dve):
                        chain = Chain(dve, ech, 6)
                        v = nc.vector

                        def stage_get(c, h):
                            for k in (SRC, DST):
                                ins = v.tensor_scalar(ix_get[k][h][:, :], get[k][:, bass.ds(c, 1), :].squeeze(1), 0.0,
                                                      None, ALU.add)
                            ins.then_inc(get_ready, 1)

                        def body(c, h, j):
                            if isinstance(c, int) and c == 0:
                                stage_get(0, 0)
                            if not (isinstance(c, int) and c == NCH - 1):
                                hold(dve, gathered[1 - h], 32 * U * (j + h))
                                stage_get(c + 1, 1 - h)
                            chain.body(c)
                            hold(dve, rows_in[h], 32 * (j + 1))
                            hold(dve, summed, c - 1)
                            v.tensor_tensor(out=same[DST][h][:, :, :], **same_id(rows[DST][h][:, :], DST, c))
                            v.tensor_tensor(out=same[SRC][h][:, :, :], **same_id(rows[SRC][h][:, :], SRC, c)
                                            ).then_inc(same_ready, 1)
                            hold(dve, same_ready, c + 1)
                            ids = col[SRC][:, bass.ds(c, 1), :].squeeze(1)
                            hold(dve, put_ready, c)
                            chain.step(v.tensor_tensor(out=prod[:, :, :], in0=same[SRC][h][:, :, :], in1=before[:, :, :],
                                                       op=ALU.mult))
                            chain.step(v.tensor_reduce(cnt[:, :], prod[:, :, :], AX, ALU.add))
                            chain.step(v.tensor_scalar(cnt[:, :], cnt[:, :], 1.0, None, ALU.min))
                            chain.step(v.tensor_scalar(t1[:, :], ids, -1.0, trash[:, 0:1], ALU.mult, ALU.add))
                            chain.step(v.tensor_tensor(out=t1[:, :], in0=t1[:, :], in1=cnt[:, :], op=ALU.mult))
                            chain.step(v.tensor_tensor(out=t1[:, :], in0=t1[:, :], in1=ids, op=ALU.add))
                            for k in (SRC, DST):
                                hold(dve, scattered[k], 16 * U * (c - 1))
                            v.tensor_scalar(ix_put[SRC][h][:, :], t1[:, :], 2.0, 1.0, ALU.mult, ALU.add)
                            v.tensor_scalar(ix_put[DST][h][:, :], put_dst[:, bass.ds(c, 1), :].squeeze(1), 0.0, None,
                                            ALU.add).then_inc(put_ready, 1)
                            hold(dve, flow_mm, c + 1)
                            v.tensor_scalar(flow[h][:, :, :], bank[4 + h][:, 0:U * 2 * D].rearrange(
                                "p (u w) -> p u w", u=U), 0.0, None, ALU.max).then_inc(flow_ready, 1)

                        over(dve, NCH, body)

                    @block.tensor
                    def _(pe):
                        def body(c, h, j):
                            hold(pe, gathered[h], 32 * U * (j + 1))
                            hold(pe, attrs_in[h], 16 * (j + 1) + 16 * (isinstance(c, int) and c == NCH - 1))
                            hold(pe, turned_out, c - 1)
                            for u in range(U):
                                ins = nc.tensor.transpose(bank[h][0:F, u * P:(u + 1) * P], feat[h][:, u, :], ident[:, :])
                            ins.then_inc(turned, 1)
                            hold(pe, turned_out, c + 1)
                            hold(pe, hid_ready, c - 1)
                            nc.tensor.matmul(bank[2 + h][:, :], w1e[:, :], feat_t[h][:, :], start=True, stop=True
                                             ).then_inc(hid_mm, 1)
                            hold(pe, hid_ready, c + 1)
                            hold(pe, flow_ready, c - 1)
                            for u in range(U):
                                o = bank[4 + h][:, u * 2 * D:(u + 1) * 2 * D]
                                nc.tensor.matmul(o, hid[h][:, u * P:(u + 1) * P], w2e[:, :], start=True, stop=False)
                                ins = nc.tensor.matmul(o, ones[:, :], b2e[:, :], start=False, stop=True)
                            ins.then_inc(flow_mm, 1)
                            hold(pe, flow_ready, c + 1)
                            hold(pe, same_ready, c + 1)
                            hold(pe, sums_ready, c - 1)
                            for u in range(U):
                                for k, at in ((DST, 0), (SRC, D)):
                                    ins = nc.tensor.matmul(bank[6 + h][:, u * 2 * D + at:u * 2 * D + at + D],
                                                           same[k][h][:, u, :], flow[h][:, u, at:at + D],
                                                           start=True, stop=True)
                            ins.then_inc(summed, 1)

                        over(pe, NCH, body)

                    @block.scalar
                    def _(act):
                        def body(c, h, j):
                            hold(act, turned, c + 1)
                            hold(act, hid_mm, c - 1)
                            nc.scalar.copy(feat_t[h][:, :], bank[h][0:F, :]).then_inc(turned_out, 1)
                            hold(act, hid_mm, c + 1)
                            hold(act, flow_mm, c - 1)
                            nc.scalar.activation(hid[h][:, :], bank[2 + h][:, :], ACT.Relu, bias=b1e[:, 0:1]
                                                 ).then_inc(hid_ready, 1)
                            hold(act, summed, c + 1)
                            for k in (SRC, DST):
                                hold(act, scattered[k], 16 * U * (c - 1))
                            nc.scalar.copy(sums[h][:, :, :], bank[6 + h][:, 0:U * 2 * D].rearrange(
                                "p (u w) -> p u w", u=U)).then_inc(sums_ready, 1)

                        over(act, NCH, body)

        def by_block(t, g, rows):
            return t[0:rows // P * P, :].rearrange("(b p) d -> p b d", p=P)[:, bass.ds(g * GB, GB), :]

        def by_run(t, g):
            return t[bass.ds(g * (GB * P), GB * P), :].rearrange("(p b) d -> p (b d)", p=P)

        def last_group(t, buf, store):
            full, rest = divmod(N - (NG - 1) * GB * P, P)
            at = (NG - 1) * GB * P
            whole = t[at:at + full * P, :].rearrange("(b p) d -> p b d", p=P)
            pairs = [(buf[:, 0:full, :], whole), (buf[0:rest, full:full + 1, :], t[at + full * P:N, :].unsqueeze(1))]
            return [(d, s) for s, d in pairs] if store else pairs

        def set_window(hot, c, u):
            return nc.vector.tensor_scalar(hot[:, u, :], steps[:, :], hot_at[:, bass.ds(c, 1), u:u + 1].squeeze(1),
                                           None, ALU.is_equal)

        def sum_windows(hot, parts, banks, w):
            for u in range(U):
                for m in range(WB):
                    at = ((u % 2) * WB + m) * W0
                    for i, part in enumerate(parts):
                        ins = nc.tensor.matmul(banks[u // 2][:, at:at + w], hot[:, u, m * P:(m + 1) * P],
                                               part[:, u, 0:w], start=(i == 0), stop=(i == len(parts) - 1))
            return ins

        def window_bases(c, eng):
            return nc.values_load_multi_w_load_instructions(
                base_row[0:1, bass.ds(c * U, U)], engines=[eng.engine], min_val=0, max_val=NBLK,
                skip_runtime_bounds_check_because="a base is an id below NT, over 128")[1]

        def add_window(added, banks, base, u, w):
            t = node_sums[:, bass.ds(base, WB), 0:w]
            at = (u % 2) * WB * W0
            nc.vector.tensor_tensor(
                out=t, in0=t, in1=banks[u // 2][:, at:at + WB * W0].rearrange("p (m w) -> p m w", w=W0)[:, :, 0:w],
                op=ALU.add).then_inc(added, 1)

        def windows(dve, hot, c, banks, w, added, do_set, do_add):
            if do_add:
                bases = window_bases(c - 1, nc.vector)
            for u in range(U):
                if do_add:
                    hold(dve, added, U * (c - 1) + u)
                    add_window(added, banks, bases[u], u, w)
                if do_set and u < U - 1:
                    ins = set_window(hot, c, u + 1)
                    if u == U - 2:
                        ins.then_inc(do_set, 1)

        def layer_fast(k):
            source = x if k == 0 else means[k - 1]
            w = W0 if k == 0 else D
            with ExitStack() as lctx:
                def buf(name, shape, dt=F32):
                    return lctx.enter_context(nc.sbuf_tensor(f"f{k}_{name}", shape, dt))

                def pair(name, shape, dt=F32):
                    return [buf(f"{name}{h}", shape, dt) for h in range(2)]

                def fsem(name):
                    return scope[-1].enter_context(nc.semaphore(f"f{k}_{name}"))

                got = [buf(f"got{q}", [P, U, D]) for q in range(4)]
                ix_get = [buf(f"ix_get{q}", [P, U], I32) for q in range(4)]
                hi, mid_, lo = pair("hi", [P, U, W0], BF16), pair("mid", [P, U, W0], BF16), pair("lo", [P, U, W0], BF16)
                rest, hot = pair("rest", [P, U, D]), pair("hot", [P, U, WIN], BF16)
                part_in, (part_out, mean_out) = buf("part_in", [P, GB, D]), (pair(n, [P, GB, D]) for n in ("part_out", "mean_out"))
                scaled, z, sq = (buf(n, [P, GB, D]) for n in ("scaled", "z", "sq"))
                n1, n2, avg, var, rs = (buf(n, [P, GB]) for n in ("n1", "n2", "avg", "var", "rs"))
                gathered = [fsem(f"gathered{q}") for q in range(4)]
                (get_ready, hot_ready, hi_ready, rest_ready, mid_ready, lo_ready, summed, added, part_loaded, mean_ready,
                 part_ready, scaled_ready, cleared, set_up, gch, zeroed) = (fsem(n) for n in (
                     "get_ready", "hot_ready", "hi_ready", "rest_ready", "mid_ready", "lo_ready", "summed", "added",
                     "part_loaded", "mean_ready", "part_ready", "scaled_ready", "cleared", "set_up",
                     "group_chain", "zeroed"))
                z_ready, sq_ready, var_ready, rs_ready, inverted = (
                    fsem(n) if k == 2 else None for n in ("z_ready", "sq_ready", "var_ready", "rs_ready", "inverted"))
                stored = [fsem("stored0"), fsem("stored1")]
                mine = [bank[0:2], bank[2:4]]

                def last(g):
                    return isinstance(g, int) and g == NG - 1

                with nc.Block() as block:
                    @block.sync
                    def _(sp):
                        def load(g):
                            if k:
                                sp.dma_start(part_in[:, :, :].rearrange("p b d -> p (b d)"),
                                             partial[bass.ds(g, 1), :, :].squeeze(0)).then_inc(part_loaded, 16)
                            elif last(g):
                                for d, s in last_group(x, part_in, False):
                                    sp.dma_start(d, s).then_inc(part_loaded, 16)
                            else:
                                sp.dma_start(part_in[:, :, :], by_block(x, g, N)).then_inc(part_loaded, 16)

                        def body(g, gh, *_):
                            if not last(g):
                                hold(sp, (scaled_ready, part_ready, z_ready)[k], g + 1)
                                load(g + 1)
                            hold(sp, part_ready, g + 1)
                            out_tile = (part_out if k == 2 else mean_out)[gh]
                            sp.dma_start(by_run(means[k], g), out_tile[:, :, :].rearrange("p b d -> p (b d)")
                                         ).then_inc(stored[gh], 16)
                            if k == 2:
                                sp.dma_start(y_lanes[:, bass.ds(g * GB, GB), :], part_out[gh][:, :, :]
                                             ).then_inc(stored[gh], 16)
                            else:
                                sp.dma_start(partial[bass.ds(g, 1), :, :].squeeze(0),
                                             part_out[gh][:, :, :].rearrange("p b d -> p (b d)")).then_inc(stored[gh], 16)
                            if k < 2:
                                sp.dma_start(backward[k][bass.ds(g * (GB * P), GB * P), :].rearrange(
                                    "(p r) d -> p (r d)", p=P), zeros[:, 0:GB * D]).then_inc(zeroed, 16)

                        load(0)
                        over4(sp, NG, body, first=2)
                        sp.wait_ge(stored[0], 32 * (NG - NG // 2))
                        sp.wait_ge(stored[1], 32 * (NG // 2))
                        if k < 2:
                            sp.wait_ge(zeroed, 16 * NG)
                        else:
                            sp.dma_start(y_lanes[:, NBLK:, :], zeros[:, 0:WB * D].rearrange("p (b d) -> p b d", d=D)
                                         ).then_inc(zeroed, 16)
                            sp.wait_ge(zeroed, 16)

                    @block.gpsimd
                    def _(pool):
                        def body(c, h, j, q, r):
                            pool_hold(pool, get_ready, c + 1)
                            for u in range(U):
                                pool.indirect_dma_start(
                                    got[q][:, u, :], None, source,
                                    bass.IndirectOffsetOnAxis(ix_get[q][:, u:u + 1].bitcast(U32), 0)
                                ).then_inc(gathered[q], 16)

                        over4(pool, NCH, body)

                    @block.scalar
                    def _(act):
                        act.wait_ge(set_up, 6)

                        def body(c, h, j, q, r):
                            hold(act, gathered[q], 16 * U * (r + 1))
                            hold(act, summed, c - 1)
                            hold(act, rest_ready, c - 1)
                            nc.scalar.copy(hi[h][:, :, 0:D], got[q][:, :, :]).then_inc(hi_ready, 1)
                            hold(act, rest_ready, c + 1)
                            hold(act, lo_ready, c - 1)
                            nc.scalar.copy(mid_[h][:, :, 0:D], rest[h][:, :, :]).then_inc(mid_ready, 1)
                            if h == 0 and not (isinstance(c, int) and c < 6):
                                root(j - 3)
                            if h == 0 and not (isinstance(c, int) and c < 4):
                                scale(j - 2)
                            if h == 1 and not (isinstance(c, int) and c < 4):
                                group(j - 2)

                        def scale(g):
                            if k == 0:
                                hold(act, part_loaded, 16 * (g + 1) + 16 * last(g))
                                hold(act, part_ready, g)
                                nc.scalar.mul(scaled[:, :, :], part_in[:, :, :], 1.25).then_inc(scaled_ready, 1)

                        def group(g):
                            if k == 2:
                                hold(act, z_ready, g + 1)
                                nc.scalar.activation(sq[:, :, :], z[:, :, :], ACT.Square).then_inc(sq_ready, 1)
                            hold(act, mean_ready, g + 1, alone=True)
                            nc.scalar.copy(node_sums[:, bass.ds(g * GB, GB), 0:D], zeros[:, 0:GB * D].rearrange(
                                "p (b d) -> p b d", d=D)).then_inc(cleared, 1)

                        def root(g):
                            if k == 2:
                                hold(act, var_ready, g + 1)
                                nc.scalar.activation(rs[:, :], var[:, :], ACT.Sqrt, bias=eps[:, 0:1],
                                                     scale=1.0 / D).then_inc(rs_ready, 1)

                        over4(act, NCH, body)
                        root(NG - 3)
                        for g in (NG - 2, NG - 1):
                            scale(g)
                            group(g)
                            root(g)
                        act.wait_ge(cleared, NG)

                    @block.tensor
                    def _(pe):
                        def body(c, h, j):
                            hold(pe, hot_ready, c + 1)
                            hold(pe, hi_ready, c + 1)
                            hold(pe, mid_ready, c + 1)
                            hold(pe, lo_ready, c + 1)
                            hold(pe, added, U * (c - 1))
                            sum_windows(hot[h], (hi[h], mid_[h], lo[h]), mine[h], w).then_inc(summed, 1)

                        over(pe, NCH, body)

                    @block.vector
                    def _(dve):
                        v = nc.vector
                        gchain = Chain(dve, gch, (2, 0, 2)[k])
                        for h in range(2):
                            v.memset(hi[h][:, :, D:], 1.0).then_inc(set_up, 1)
                            v.memset(mid_[h][:, :, D:], 0.0).then_inc(set_up, 1)
                            v.memset(lo[h][:, :, D:], 0.0).then_inc(set_up, 1)

                        def stage_get(c, q):
                            v.tensor_scalar(ix_get[q][:, :], (get_row if k else get[SRC])[:, bass.ds(c, 1), :].squeeze(1), 0.0,
                                            None, ALU.add).then_inc(get_ready, 1)

                        def wide(t):
                            return t.unsqueeze(2).broadcast_to([P, GB, D])

                        def average(g, gh, gj):
                            gchain.body(g)
                            sums = node_sums[:, bass.ds(g * GB, GB), 0:D]
                            r = rden_n[:, bass.ds(g * GB, GB)]
                            if k == 0:
                                hold(dve, mean_ready, g)
                                gchain.step(v.tensor_scalar(n1[:, :].unsqueeze(2), node_sums[:, bass.ds(g * GB, GB), D:W0],
                                                            1.0, None, ALU.max))
                                gchain.step(v.reciprocal(n2[:, :], n1[:, :]))
                                v.tensor_scalar(r, n2[:, :], 1.0, None, ALU.mult)
                                r = n2[:, :]
                            hold(dve, stored[gh], 32 * gj)
                            v.tensor_tensor(out=mean_out[gh][:, :, :], in0=sums, in1=wide(r), op=ALU.mult
                                            ).then_inc(mean_ready, 1)

                        def blend(g, gh):
                            hold(dve, mean_ready, g + 1)
                            if k == 0:
                                hold(dve, scaled_ready, g + 1)
                            else:
                                hold(dve, part_loaded, 16 * (g + 1))
                            ins = v.scalar_tensor_tensor(
                                out=(mean_out if k == 2 else part_out)[gh][:, :, :], in0=mean_out[gh][:, :, :],
                                scalar=0.25, in1=(part_in if k else scaled)[:, :, :], op0=ALU.mult, op1=ALU.add)
                            if k < 2:
                                ins.then_inc(part_ready, 1)
                            else:
                                gchain.step(ins)

                        def centre(g, gh):
                            if k == 2:
                                gchain.step(v.tensor_reduce(avg[:, :], mean_out[gh][:, :, :], AX, ALU.add))
                                hold(dve, part_ready, g)
                                v.scalar_tensor_tensor(out=z[:, :, :], in0=wide(avg[:, :]), scalar=-1.0 / D,
                                                       in1=mean_out[gh][:, :, :], op0=ALU.mult, op1=ALU.add
                                                       ).then_inc(z_ready, 1)

                        def spread(g):
                            if k == 2:
                                hold(dve, sq_ready, g + 1)
                                v.tensor_reduce(var[:, :], sq[:, :, :], AX, ALU.add).then_inc(var_ready, 1)

                        def invert(g):
                            if k == 2:
                                hold(dve, rs_ready, g + 1)
                                v.reciprocal(n1[:, :], rs[:, :]).then_inc(inverted, 1)

                        def finish(g, gh):
                            if k == 2:
                                hold(dve, inverted, g + 1)
                                v.tensor_tensor(out=part_out[gh][:, :, :], in0=z[:, :, :], in1=wide(n1[:, :]),
                                                op=ALU.mult).then_inc(part_ready, 1)

                        def body(c, h, j, q, r):
                            first = isinstance(c, int) and c == 0
                            first_half = h == 1 and not (isinstance(c, int) and c < 5)
                            second_half = h == 0 and not (isinstance(c, int) and c < 6)
                            if first:
                                for ahead in range(4):
                                    stage_get(ahead, ahead)
                            if first_half:
                                hold(dve, added, U * (c - 1))
                                average(j - 2, q // 2, r - 1)
                            hold(dve, hi_ready, c + 1)
                            hold(dve, mid_ready, c - 1)
                            hold(dve, lo_ready, c - 1)
                            v.tensor_tensor(out=rest[h][:, :, :], in0=got[q][:, :, :], in1=hi[h][:, :, 0:D],
                                            op=ALU.subtract).then_inc(rest_ready, 1)
                            if not (isinstance(c, int) and c >= NCH - 4):
                                stage_get(c + 4, q)
                            if second_half:
                                spread(j - 3)
                            hold(dve, summed, c - 1)
                            set_window(hot[h], c, 0)
                            if first_half:
                                blend(j - 2, q // 2)
                            hold(dve, rest_ready, c + 1)
                            hold(dve, mid_ready, c + 1)
                            v.tensor_tensor(out=lo[h][:, :, 0:D], in0=rest[h][:, :, :], in1=mid_[h][:, :, 0:D],
                                            op=ALU.subtract).then_inc(lo_ready, 1)
                            if first_half:
                                centre(j - 2, q // 2)
                            if second_half:
                                invert(j - 3)
                            hold(dve, summed, c)
                            windows(dve, hot[h], c, mine[1 - h], w, added, hot_ready, not first)
                            if second_half:
                                finish(j - 3, 1 - q // 2)

                        over4(dve, NCH, body)
                        spread(NG - 3)
                        hold(dve, summed, NCH)
                        windows(dve, None, NCH, mine[1], w, added, None, True)
                        invert(NG - 3)
                        finish(NG - 3, 0)
                        hold(dve, added, U * NCH)
                        for g in (NG - 2, NG - 1):
                            average(g, g % 2, g // 2)
                            blend(g, g % 2)
                            centre(g, g % 2)
                            spread(g)
                            invert(g)
                            finish(g, g % 2)

        def edges_fast():
            with ExitStack() as lctx:
                def buf(name, shape, dt=F32):
                    return lctx.enter_context(nc.sbuf_tensor(f"h_{name}", shape, dt))

                def pair(name, shape, dt=F32):
                    return [buf(f"{name}{h}", shape, dt) for h in range(2)]

                DS = D + 1
                rows, same = pair("rows", [P, CE], I32), pair("same", [P, U, P], BF16)
                at, y_win, pick = pair("at", [P, CE], F16), pair("y_win", [P, U, WB, D]), buf("pick", [P, WB, CE], BF16)
                y_hi, y_mid, y_lo = (buf(n, [P, U, WB, D], BF16) for n in ("y_hi", "y_mid", "y_lo"))
                y_rest = buf("y_rest", [P, U, WB, D])
                feat, feat_t, hid = pair("feat", [P, U, F]), pair("feat_t", [F, CE]), pair("hid", [2 * H, CE])
                flow, sums = pair("flow", [P, U, 2 * D]), pair("sums", [P, U, DS])
                hi, mid_, lo = (pair(n, [P, U, 2 * D + 1], BF16) for n in ("hi", "mid", "lo"))
                rest, hot = pair("rest", [P, U, 2 * D]), pair("hot", [P, U, WIN], BF16)
                ix_get, ix_put = pair("get_src", [P, U], I32), pair("put_src", [P, U], I32)
                away, later, put = (buf(n, [P, U]) for n in ("away", "later", "put"))
                node_of = buf("node_of", [P, WB])
                rank, weight, twice = buf("rank", [P, 1]), buf("weight", [P, 1]), buf("twice", [P, 1])
                ones16 = buf("ones16", [1, P], BF16)
                b2_rest = [buf(f"b2_rest{i}", [1, 2 * D]) for i in range(2)]
                b2_part = [buf(f"b2_part{i}", [1, U, 2 * D], BF16) for i in range(3)]
                rows_in, attrs_in, gathered, scattered, at_in, y_in = (
                    [sem(f"h_{n}{h}") for h in range(2)]
                    for n in ("rows_in", "attrs_in", "gathered", "scattered", "at_in", "y_in"))
                (get_ready, put_ready, same_ready, pick_ready, picked, placed, turned, turned_out, hid_mm, hid_ready,
                 flow_mm, flow_ready, summed, sums_ready, ech, hot_ready, hi_ready, rest_ready, mid_ready, lo_ready,
                 windowed, added, set_up, rank_ready, weight_ready, y_hi_ready, y_rest_ready, y_mid_ready) = (
                     sem(f"h_{n}") for n in (
                         "get_ready", "put_ready", "same_ready", "pick_ready", "picked", "placed", "turned",
                         "turned_out", "hid_mm", "hid_ready", "flow_mm", "flow_ready", "summed", "sums_ready", "chain",
                         "hot_ready", "hi_ready", "rest_ready", "mid_ready", "lo_ready", "windowed", "added", "set_up",
                         "rank_ready", "weight_ready", "y_hi_ready", "y_rest_ready", "y_mid_ready"))
                attr_main = edge_attr[0:(NCH - 1) * CE, :].rearrange("(c u p) d -> c p u d", p=P, u=U)
                attr_tail = edge_attr[(NCH - 1) * CE:E - TAILP, :].rearrange("(u p) d -> p u d", p=P)
                flow_bank, hid_bank, win_banks = bank[3], bank[2], bank[6:8]
                sums_bank, y_bank = bank[4], bank[5]

                def edges_over(eng, body):
                    over4(eng, NCH, lambda c, h, j, q, r: body(c, h, j), first=4)

                def known(c, test):
                    return isinstance(c, int) and test(c)

                with nc.Block() as block:
                    @block.sync
                    def _(sp):
                        def body(c, h, j):
                            hold(sp, pick_ready, c - 1, alone=True)
                            sp.dma_start(at[h][:, :], place_dram[bass.ds(c, 1), :].broadcast_to([P, CE])
                                         ).then_inc(at_in[h], 16)
                            bases = window_bases(c, nc.sync)
                            hold(sp, picked, c - 1, alone=True)
                            for u in range(U):
                                sp.dma_start(y_win[h][:, u, :, :], y_lanes[:, bass.ds(bases[u], WB), :]
                                             ).then_inc(y_in[h], 16)
                            hold(sp, same_ready, c - 1, alone=True)
                            sp.dma_start(rows[h][:, :], row_of[SRC][bass.ds(c, 1), :].broadcast_to([P, CE])
                                         ).then_inc(rows_in[h], 16)
                            hold(sp, turned, c - 1, alone=True)
                            if known(c, lambda c: c == NCH - 1):
                                sp.dma_start(feat[h][:, 0:TAILT, 2 * D:], attr_tail).then_inc(attrs_in[h], 16)
                                sp.dma_start(feat[h][0:TAILP, TAILT:TAILT + 1, 2 * D:], edge_attr[E - TAILP:E, :]
                                             .unsqueeze(1)).then_inc(attrs_in[h], 16)
                            else:
                                sp.dma_start(feat[h][:, :, 2 * D:], attr_main[bass.ds(c, 1), :, :, :].squeeze(0)
                                             ).then_inc(attrs_in[h], 16)

                        edges_over(sp, body)

                    @block.gpsimd
                    def _(pool):
                        def body(s, h, gather=True, scatter=True):
                            if gather:
                                pool_hold(pool, get_ready, s + 1)
                                pool_hold(pool, turned, s - 1)
                            if scatter:
                                pool_hold(pool, put_ready, s - 2)
                                pool_hold(pool, sums_ready, s - 2)
                            for u in range(U):
                                if gather:
                                    pool.indirect_dma_start(
                                        feat[h][:, u, D:2 * D], None, means[2],
                                        bass.IndirectOffsetOnAxis(ix_get[h][:, u:u + 1].bitcast(U32), 0)
                                    ).then_inc(gathered[h], 16)
                                if scatter:
                                    pool_hold(pool, scattered[u % 2], 16 * (U // 2 * (s - 3) + u // 2))
                                    pool.indirect_dma_start(
                                        backward[u % 2], bass.IndirectOffsetOnAxis(
                                            ix_put[1 - h][:, u:u + 1].bitcast(U32), 0),
                                        sums[1 - h][:, u, 0:D], None, compute_op=ALU.add).then_inc(scattered[u % 2], 16)

                        edges_over(pool, lambda c, h, j: body(c, h, scatter=not known(c, lambda c: c < 3)))
                        for s in range(NCH, NCH + 3):
                            body(s, s % 2, gather=False)
                        for half_sem in scattered:
                            pool.wait_ge(half_sem, 16 * U // 2 * NCH)

                    @block.vector
                    def _(dve):
                        chain = Chain(dve, ech, 3)
                        v = nc.vector
                        setup = Chain(dve, set_up, 11)
                        setup.step(v.tensor_scalar(rank[:, :], trash[:, :], float(-N), None, ALU.add))
                        v.tensor_scalar(rank[:, :], rank[:, :], -1.1, 70.0, ALU.mult, ALU.add).then_inc(rank_ready, 1)
                        for m in range(WB):
                            v.tensor_scalar(node_of[:, m:m + 1], trash[:, :], float(m * P - N), None, ALU.add)
                        setup.step(v.memset(ones16[:, :], 1.0))

                        def all_tiles(t):
                            return t.unsqueeze(1).broadcast_to([1, U, 2 * D])

                        setup.step(v.tensor_scalar(b2_part[0][:, :, :], all_tiles(b2e[:, :]), 0.0, None, ALU.add))
                        for i, t in enumerate((b2e, b2_rest[0])):
                            setup.step(v.tensor_tensor(out=b2_rest[i][:, :], in0=t[:, :], in1=b2_part[i][:, 0:1, :].squeeze(1),
                                                       op=ALU.subtract))
                            setup.step(v.tensor_scalar(b2_part[i + 1][:, :, :], all_tiles(b2_rest[i][:, :]), 0.0, None,
                                                       ALU.add))
                        dve.wait_ge(weight_ready, 1)
                        for h in range(2):
                            v.memset(mid_[h][:, :, 2 * D:], 0.0)
                            setup.step(v.memset(lo[h][:, :, 2 * D:], 0.0))
                            setup.step(v.tensor_scalar(hi[h][:, :, 2 * D:], weight[:, :].unsqueeze(1).broadcast_to(
                                [P, U, 1]), 0.0, None, ALU.add))
                        setup.step(v.tensor_scalar(twice[:, :], weight[:, :], 2.0, None, ALU.mult))

                        def stage_get(c, h):
                            v.tensor_scalar(ix_get[h][:, :], get_row[:, bass.ds(c, 1), :].squeeze(1), 0.0,
                                            None, ALU.add).then_inc(get_ready, 1)

                        def pick_block(m, h):
                            return v.tensor_scalar(pick[:, m, :], at[h][:, :], node_of[:, m:m + 1], None, ALU.is_equal)

                        def y_split_rest(c, h):
                            hold(dve, y_hi_ready, c + 1)
                            v.tensor_tensor(out=y_rest[:, :, :, :], in0=y_win[h][:, :, :, :], in1=y_hi[:, :, :, :],
                                            op=ALU.subtract).then_inc(y_rest_ready, 1)

                        def y_split_lo(c):
                            hold(dve, y_mid_ready, c + 1)
                            v.tensor_tensor(out=y_lo[:, :, :, :], in0=y_rest[:, :, :, :], in1=y_mid[:, :, :, :],
                                            op=ALU.subtract)

                        stage_get(0, 0)
                        stage_get(1, 1)
                        y_split_rest(0, 0)
                        y_split_lo(0)
                        dve.wait_ge(at_in[0], 16)
                        for m in range(WB):
                            ins = pick_block(m, 0)
                        ins.then_inc(pick_ready, 1)

                        def add_windows(c, one_hots=None):
                            adding = not known(c, lambda c: c < 0)
                            if adding:
                                bases = window_bases(c, nc.vector)
                                hold(dve, windowed, c + 1)
                            for u in range(U):
                                if adding:
                                    hold(dve, added, U * c + u)
                                    add_window(added, win_banks, bases[u], u, D)
                                if one_hots is not None:
                                    ins = set_window(one_hots, c + 2, u)
                            if one_hots is not None:
                                ins.then_inc(hot_ready, 1)

                        def flows(c, h):
                            hold(dve, flow_mm, c + 1)
                            hold(dve, hi_ready, c - 1)
                            v.tensor_scalar(flow[h][:, :, :], flow_bank[:, 0:U * 2 * D].rearrange(
                                "p (u w) -> p u w", u=U), 0.0, None, ALU.max).then_inc(flow_ready, 1)

                        def split_rest(c, h):
                            hold(dve, hi_ready, c + 1)
                            hold(dve, mid_ready, c - 1)
                            v.tensor_tensor(out=rest[h][:, :, :], in0=flow[h][:, :, :], in1=hi[h][:, :, 0:2 * D],
                                            op=ALU.subtract).then_inc(rest_ready, 1)

                        def split_lo(c, h):
                            hold(dve, mid_ready, c + 1)
                            v.tensor_tensor(out=lo[h][:, :, 0:2 * D], in0=rest[h][:, :, :], in1=mid_[h][:, :, 0:2 * D],
                                            op=ALU.subtract).then_inc(lo_ready, 1)

                        def targets(c, h):
                            chain.body(c)
                            ids = put_row[:, bass.ds(c, 1), :].squeeze(1)
                            hold(dve, put_ready, c)
                            chain.step(v.tensor_scalar(away[:, :], ids, -1.0, trash_row[:, 0:1], ALU.mult, ALU.add))
                            hold(dve, sums_ready, c + 1)
                            chain.step(v.scalar_tensor_tensor(
                                out=later[:, :].unsqueeze(2), in0=sums[h][:, :, D:], scalar=twice[:, 0:1],
                                in1=away[:, :].unsqueeze(2), op0=ALU.is_ge, op1=ALU.mult))
                            for half_sem in scattered:
                                hold(dve, half_sem, 16 * U // 2 * (c - 1))
                            chain.step(v.tensor_tensor(out=put[:, :], in0=later[:, :], in1=ids, op=ALU.add))
                            v.tensor_scalar(ix_put[h][:, :], put[:, :], 0.0, None, ALU.add).then_inc(put_ready, 1)

                        def body(c, h, j):
                            lag = not known(c, lambda c: c < 1)
                            ahead = not known(c, lambda c: c == NCH - 1)
                            add_windows(c - 2, hot[h])
                            if ahead:
                                y_split_rest(c + 1, 1 - h)
                            if lag:
                                flows(c - 1, 1 - h)
                            hold(dve, rows_in[h], 16 * (j + 1))
                            v.tensor_tensor(out=same[h][:, :, :], **same_id(rows[h][:, :], SRC, c)).then_inc(same_ready, 1)
                            if ahead:
                                y_split_lo(c + 1)
                            if lag:
                                split_rest(c - 1, 1 - h)
                            if ahead:
                                hold(dve, at_in[1 - h], 16 * (j + h + 1))
                                hold(dve, picked, c + 1)
                                for m in range(WB // 2):
                                    pick_block(m, 1 - h)
                            if lag:
                                split_lo(c - 1, 1 - h)
                            if ahead:
                                for m in range(WB // 2, WB):
                                    ins = pick_block(m, 1 - h)
                                ins.then_inc(pick_ready, 1)
                            if not known(c, lambda c: c >= NCH - 2):
                                hold(dve, gathered[h], 16 * U * (j + 1))
                                stage_get(c + 2, h)
                            if lag:
                                targets(c - 1, 1 - h)

                        edges_over(dve, body)
                        add_windows(NCH - 2)
                        flows(NCH - 1, 1)
                        split_rest(NCH - 1, 1)
                        split_lo(NCH - 1, 1)
                        targets(NCH - 1, 1)
                        add_windows(NCH - 1)

                    @block.tensor
                    def _(pe):
                        def y_at_dst(c, h, j):
                            hold(pe, pick_ready, c + 1)
                            hold(pe, placed, c)
                            parts = (y_hi, y_mid, y_lo)
                            for u in range(U):
                                for m in range(WB):
                                    for i, part in enumerate(parts):
                                        ins = nc.tensor.matmul(
                                            y_bank[:, u * D:(u + 1) * D], pick[:, m, u * P:(u + 1) * P],
                                            part[:, u, m, :], start=(m == i == 0),
                                            stop=(m == WB - 1 and i == len(parts) - 1))
                            ins.then_inc(picked, 1)

                        def flow_products(c, h):
                            hold(pe, hid_ready, c + 1)
                            hold(pe, flow_ready, c)
                            for i, part in enumerate(b2_part):
                                nc.tensor.matmul(flow_bank[:, 0:U * 2 * D], ones16[:, :],
                                                 part[:, :, :].rearrange("p u w -> p (u w)"), start=(i == 0), stop=False)
                            for u in range(U):
                                o = flow_bank[:, u * 2 * D:(u + 1) * 2 * D]
                                ins = nc.tensor.matmul(o, hid[h][:, u * P:(u + 1) * P], w2e[:, :], start=False, stop=(u == U - 1))
                            ins.then_inc(flow_mm, 1)

                        def flow_sums(c, h):
                            hold(pe, lo_ready, c + 1)
                            hold(pe, mid_ready, c + 1)
                            hold(pe, same_ready, c + 1)
                            hold(pe, sums_ready, c)
                            for u in range(U):
                                for i, part in enumerate((hi[h], mid_[h], lo[h])):
                                    ins = nc.tensor.matmul(sums_bank[:, u * DS:(u + 1) * DS], same[h][:, u, :],
                                                           part[:, u, D:], start=(i == 0), stop=(i == 2))
                            ins.then_inc(summed, 1)
                            hold(pe, hot_ready, c + 1)
                            hold(pe, added, U * c)
                            sum_windows(hot[h], (hi[h], mid_[h], lo[h]), win_banks, D).then_inc(windowed, 1)

                        def body(c, h, j):
                            lag = not known(c, lambda c: c < 1)
                            if lag:
                                flow_products(c - 1, 1 - h)
                            hold(pe, gathered[h], 16 * U * (j + 1))
                            hold(pe, attrs_in[h], 16 * (j + 1) + 16 * known(c, lambda c: c == NCH - 1))
                            hold(pe, placed, c + 1)
                            hold(pe, turned_out, c - 1)
                            for u in range(U):
                                ins = nc.tensor.transpose(bank[h][0:F, u * P:(u + 1) * P], feat[h][:, u, :], ident[:, :])
                            ins.then_inc(turned, 1)
                            hold(pe, turned_out, c + 1)
                            hold(pe, hid_ready, c)
                            nc.tensor.matmul(hid_bank[:, :], w1e[:, :], feat_t[h][:, :], start=True, stop=True
                                             ).then_inc(hid_mm, 1)
                            if lag:
                                flow_sums(c - 1, 1 - h)
                            if not known(c, lambda c: c == NCH - 1):
                                y_at_dst(c + 1, 1 - h, j + h)

                        pe.wait_ge(set_up, 11)
                        y_at_dst(0, 0, 0)
                        edges_over(pe, body)
                        flow_products(NCH - 1, 1)
                        flow_sums(NCH - 1, 1)

                    @block.scalar
                    def _(act):
                        def split(c, h):
                            hold(act, flow_ready, c + 1)
                            hold(act, windowed, c - 1)
                            nc.scalar.copy(hi[h][:, :, 0:2 * D], flow[h][:, :, :]).then_inc(hi_ready, 1)
                            hold(act, rest_ready, c + 1)
                            nc.scalar.copy(mid_[h][:, :, 0:2 * D], rest[h][:, :, :]).then_inc(mid_ready, 1)

                        def take_sums(c, h):
                            hold(act, summed, c + 1)
                            hold(act, put_ready, c - 1)
                            for half_sem in scattered:
                                hold(act, half_sem, 16 * U // 2 * (c - 1))
                            nc.scalar.copy(sums[h][:, :, :], sums_bank[:, 0:U * DS].rearrange("p (u w) -> p u w", w=DS)
                                           ).then_inc(sums_ready, 1)

                        def y_split_hi(c, h, j):
                            hold(act, y_in[h], 16 * U * (j + 1))
                            hold(act, picked, c)
                            nc.scalar.copy(y_hi[:, :, :, :], y_win[h][:, :, :, :]).then_inc(y_hi_ready, 1)

                        def y_split_mid(c):
                            hold(act, y_rest_ready, c + 1)
                            nc.scalar.copy(y_mid[:, :, :, :], y_rest[:, :, :, :]).then_inc(y_mid_ready, 1)

                        def body(c, h, j):
                            lag = not known(c, lambda c: c < 1)
                            ahead = not known(c, lambda c: c == NCH - 1)
                            hold(act, picked, c + 1)
                            hold(act, turned, c - 1)
                            nc.scalar.copy(feat[h][:, :, 0:D], y_bank[:, 0:U * D].rearrange(
                                "p (u w) -> p u w", u=U)).then_inc(placed, 1)
                            if ahead:
                                y_split_hi(c + 1, 1 - h, j + h)
                            hold(act, turned, c + 1)
                            hold(act, hid_mm, c - 1)
                            nc.scalar.copy(feat_t[h][:, :], bank[h][0:F, :]).then_inc(turned_out, 1)
                            if ahead:
                                y_split_mid(c + 1)
                            if lag:
                                split(c - 1, 1 - h)
                            hold(act, hid_mm, c + 1)
                            hold(act, flow_mm, c - 1)
                            nc.scalar.activation(hid[h][:, :], hid_bank[:, :], ACT.Relu, bias=b1e[:, 0:1]
                                                 ).then_inc(hid_ready, 1)
                            if lag:
                                take_sums(c - 1, 1 - h)

                        act.wait_ge(rank_ready, 1)
                        nc.scalar.activation(weight[:, :], rank[:, :], ACT.Exp).then_inc(weight_ready, 1)
                        y_split_hi(0, 0, 0)
                        y_split_mid(0)
                        edges_over(act, body)
                        split(NCH - 1, 1)
                        take_sums(NCH - 1, 1)

        def nodes_out(fast):
            n = "s" if fast else "n"
            tail_parts = P if fast else TAILN
            with ExitStack() as lctx:
                def pair(name, shape, dt=F32):
                    return [lctx.enter_context(nc.sbuf_tensor(f"{n}_{name}{i}", shape, dt)) for i in range(2)]

                def nsem(name):
                    return scope[-1].enter_context(nc.semaphore(f"{n}_{name}"))

                HC = 512
                yb, fb, odd = pair("yb", [P, Q, D]), pair("fb", [P, Q, 2 * D]), pair("odd", [P, Q, D])
                even = pair("even", [P, Q, D])
                flow_t, hid = pair("flow_t", [P, 2 * HC]), pair("hid", [P, 2 * HC])
                s0, z, sq, res = pair("s0", [P, Q, D])[0], pair("z", [P, Q, D]), pair("sq", [P, Q, D]), pair("res", [P, Q, D])
                q2, mean, var, rs = (pair(m, [P, Q]) for m in ("q2", "mean", "var", "rs"))
                y_in, flows_in, res_out = ([nsem(f"{m}{i}") for i in range(2)] for m in ("y_in", "flows_in", "res_out"))
                (turned, turned_out, hid_mm, hid_ready, out_mm, z_ready, sq_ready, var_ready, rs_ready, res_ready, nch,
                 sums_in) = (nsem(m) for m in ("turned", "turned_out", "hid_mm", "hid_ready", "out_mm", "z_ready",
                                               "sq_ready", "var_ready", "rs_ready", "res_ready", "chain", "sums_in"))
                inverted = nsem("inverted")
                y_view, flow_view, out_view = node_views(y_table, D), node_views(flows, 2 * D), node_views(out, D)

                def over_chunks(eng, body):
                    body(0, 0, 0, P)
                    body(1, 1, 0, P)
                    body(2, 0, 1, P)
                    body(3, 1, 1, P)
                    with eng.Fori(0, NN // 4 - 1) as i:
                        for c in range(4, 8):
                            body(i * 4 + c, c % 2, i * 2 + c // 2, P)
                    body(NN, 0, NN // 2, tail_parts)

                with nc.Block() as block:
                    @block.sync
                    def _(sp):
                        def body(c, h, j, parts):
                            if fast:
                                hold(sp, sums_in, 2 * (c - 1))
                                sp.dma_start(even[h][:, :, :].rearrange("p q d -> p (q d)"), by_run(backward[0], c)).then_inc(flows_in[h], 16)
                                sp.dma_start(odd[h][:, :, :].rearrange("p q d -> p (q d)"), by_run(backward[1], c)).then_inc(flows_in[h], 16)
                            else:
                                hold(sp, turned, 2 * (c - 1))
                                sp.dma_start(fb[h][0:parts, :, :].rearrange("p q d -> p (q d)"), flow_view(c, parts)
                                             ).then_inc(flows_in[h], 16)
                            if not fast:
                                hold(sp, z_ready, c - 1)
                                sp.dma_start(yb[h][0:parts, :, :].rearrange("p q d -> p (q d)"), y_view(c, parts)
                                             ).then_inc(y_in[h], 16)

                        over_chunks(sp, body)
                        sp.wait_ge(res_out[0], 16 * (NN // 2 + 1) + 16 * fast)
                        sp.wait_ge(res_out[1], 16 * (NN // 2))

                    @block.gpsimd
                    def _(pool):
                        def body(c, h, j, parts):
                            if fast:
                                pool_hold(pool, turned, 2 * (c - 1))
                                nc.gpsimd.tensor_copy(fb[h][:, :, 0:D], node_sums[:, bass.ds(c * GB, GB), 0:D]
                                                      ).then_inc(sums_in, 1)
                                pool_hold(pool, flows_in[h], 32 * (j + 1))
                                nc.gpsimd.tensor_tensor(out=fb[h][:, :, D:], in0=even[h][:, :, :], in1=odd[h][:, :, :],
                                                        op=ALU.add).then_inc(sums_in, 1)
                            else:
                                square(c, h, parts)

                        def square(c, h, parts):
                            s = slice(0, parts)
                            pool_hold(pool, z_ready, c + 1)
                            nc.gpsimd.tensor_tensor(out=sq[h][s, :, :], in0=z[h][s, :, :], in1=z[h][s, :, :],
                                                    op=ALU.mult).then_inc(sq_ready, 1)

                        over_chunks(pool, body)

                    @block.tensor
                    def _(pe):
                        def turn(c, h, j, parts):
                            if fast:
                                hold(pe, sums_in, 2 * (c + 1))
                            else:
                                hold(pe, flows_in[h], 16 * (j + 1))
                            for g in range(2):
                                hold(pe, turned_out, 2 * c + g - 1)
                                for m in range(4):
                                    q = 8 * g + 2 * m
                                    ins = nc.tensor.transpose(
                                        bank[g][:, m * P:m * P + parts],
                                        fb[h][0:parts, q:q + 2, :].rearrange("p q d -> p (q d)"), ident[0:parts, 0:parts])
                                ins.then_inc(turned, 1)

                        def hidden(c, h, parts):
                            for g in range(2):
                                hold(pe, turned_out, 2 * c + g + 1)
                                hold(pe, hid_ready, 2 * c + g - 1)
                                ft = flow_t[h][:, g * HC:(g + 1) * HC].rearrange("p (m n) -> p m n", m=4)[:, :, 0:parts]
                                o = bank[2 + g][:, :].rearrange("p (m n) -> p m n", m=4)[:, :, 0:parts]
                                nc.tensor.matmul(o, w1n[:, :], ft, start=True, stop=True).then_inc(hid_mm, 1)

                        def result(c, h, parts):
                            hold(pe, z_ready, c - 1)
                            for g in range(2):
                                hold(pe, hid_ready, 2 * c + g + 1)
                                for m in range(4):
                                    col0 = g * HC + m * P
                                    o = (4 * g + m) * 2 * D
                                    ins = nc.tensor.matmul(bank[4 + h][0:parts, o:o + 2 * D],
                                                           hid[h][:, col0:col0 + parts], w2n[:, :], start=True, stop=True)
                            ins.then_inc(out_mm, 1)

                        def body(c, h, j, parts):
                            turn(c, h, j, parts)
                            if not (isinstance(c, int) and c == 0):
                                result(c - 1, 1 - h, P)
                            hidden(c, h, parts)

                        over_chunks(pe, body)
                        result(NN, 0, tail_parts)

                    @block.scalar
                    def _(act):
                        def strip(t, parts):
                            return t.rearrange("p (m n) -> p m n", m=4)[:, :, 0:parts]

                        def root(c, h, parts):
                            s = slice(0, parts)
                            hold(act, var_ready, c + 1)
                            nc.scalar.activation(rs[h][s, :], var[h][s, :], ACT.Sqrt, bias=eps[s, 0:1],
                                                 scale=1.0 / D).then_inc(rs_ready, 1)

                        def square(c, h, parts):
                            s = slice(0, parts)
                            hold(act, z_ready, c + 1)
                            hold(act, var_ready, c - 1)
                            nc.scalar.activation(sq[h][s, :, :], z[h][s, :, :], ACT.Square).then_inc(sq_ready, 1)

                        def load_y(c, h):
                            hold(act, z_ready, c - 1)
                            act.dma_start(yb[h][:, :, :], y_lanes[:, bass.ds(c * GB, GB), :]).then_inc(y_in[h], 16)

                        def store(c, h, parts):
                            hold(act, res_ready, c + 1)
                            if not fast:
                                act.dma_start(out_view(c, parts), res[h][0:parts, :, :].rearrange("p q d -> p (q d)")
                                              ).then_inc(res_out[h], 16)
                            elif isinstance(c, int) and c == NN:
                                for d, s in last_group(out, res[h], True):
                                    act.dma_start(d, s).then_inc(res_out[h], 16)
                            else:
                                act.dma_start(by_block(out, c, N), res[h][:, :, :]).then_inc(res_out[h], 16)

                        def body(c, h, j, parts):
                            hold(act, hid_mm, 2 * (c - 1))
                            for g in range(2):
                                hold(act, turned, 2 * c + g + 1)
                                nc.scalar.copy(strip(flow_t[h][:, g * HC:(g + 1) * HC], parts), strip(bank[g][:, :], parts)
                                               ).then_inc(turned_out, 1)
                            hold(act, out_mm, c - 1)
                            for g in range(2):
                                hold(act, hid_mm, 2 * c + g + 1)
                                nc.scalar.activation(strip(hid[h][:, g * HC:(g + 1) * HC], parts),
                                                     strip(bank[2 + g][:, :], parts), ACT.Relu,
                                                     bias=b1nn[:, 0:1]).then_inc(hid_ready, 1)
                            if fast and not (isinstance(c, int) and c == 0):
                                square(c - 1, 1 - h, P)
                                if not (isinstance(c, int) and c == NN):
                                    load_y(c + 1, 1 - h)
                            if not (isinstance(c, int) and c < 2):
                                root(c - 2, h, P)
                            if not (isinstance(c, int) and c < 3):
                                store(c - 3, 1 - h, P)

                        if fast:
                            load_y(0, 0)
                            load_y(1, 1)
                        over_chunks(act, body)
                        if fast:
                            square(NN, 0, tail_parts)
                        root(NN - 1, 1, P)
                        root(NN, 0, tail_parts)
                        store(NN - 2, 0, P)
                        store(NN - 1, 1, P)
                        store(NN, 0, tail_parts)

                    @block.vector
                    def _(dve):
                        chain = Chain(dve, nch, 3)
                        v = nc.vector

                        def wide(t, parts):
                            return t.unsqueeze(2).broadcast_to([parts, Q, D])

                        def centre(c, h, j, parts):
                            chain.body(c)
                            s = slice(0, parts)
                            hold(dve, out_mm, c + 1)
                            hold(dve, y_in[h], 16 * (j + 1))
                            hold(dve, z_ready, c)
                            hold(dve, sq_ready, c - 1)
                            hold(dve, res_ready, c - 1)
                            chain.step(v.tensor_tensor(out=s0[s, :, :], in0=bank[4 + h][s, :].rearrange(
                                "p (q d) -> p q d", d=D), in1=b2nn[s, :, :], op=ALU.add))
                            chain.step(v.scalar_tensor_tensor(out=s0[s, :, :], in0=s0[s, :, :], scalar=0.0,
                                                              in1=yb[h][s, :, :], op0=ALU.max, op1=ALU.add))
                            chain.step(v.tensor_reduce(mean[h][s, :], s0[s, :, :], AX, ALU.add))
                            v.scalar_tensor_tensor(out=z[h][s, :, :], in0=wide(mean[h][s, :], parts), scalar=-1.0 / D,
                                                   in1=s0[s, :, :], op0=ALU.mult, op1=ALU.add).then_inc(z_ready, 1)

                        def norm(c, h, j, parts):
                            s = slice(0, parts)
                            hold(dve, rs_ready, c + 1)
                            hold(dve, res_ready, c)
                            v.reciprocal(q2[h][s, :], rs[h][s, :]).then_inc(inverted, 1)
                            hold(dve, inverted, c + 1)
                            hold(dve, res_out[h], 16 * j)
                            v.tensor_tensor(out=res[h][s, :, :], in0=z[h][s, :, :], in1=wide(q2[h][s, :], parts),
                                            op=ALU.mult).then_inc(res_ready, 1)

                        def spread(c, h, parts):
                            s = slice(0, parts)
                            hold(dve, sq_ready, c + 1)
                            v.tensor_reduce(var[h][s, :], sq[h][s, :, :], AX, ALU.add).then_inc(var_ready, 1)

                        def body(c, h, j, parts):
                            if not (isinstance(c, int) and c < 2):
                                norm(c - 2, h, j - 1, P)
                            centre(c, h, j, parts)
                            if not (isinstance(c, int) and c == 0):
                                spread(c - 1, 1 - h, P)

                        over_chunks(dve, body)
                        norm(NN - 1, 1, NN // 2 - 1, P)
                        spread(NN, 0, tail_parts)
                        norm(NN, 0, NN // 2, tail_parts)


        short_way = nc.values_load(flag[0:1, 0:1], min_val=0, max_val=1)
        with nc.If(short_way), ExitStack() as way:
            scope.append(way)
            for k in range(3):
                layer_fast(k)
            edges_fast()
            nodes_out(True)
            scope.pop()
        with nc.Else(), ExitStack() as way:
            scope.append(way)
            clear_first()
            for k in range(3):
                layer(k)
            nodes_y()
            edges_general()
            nodes_out(False)


_INS = ['x', 'src', 'dst', 'edge_attr_16', 'L1_gnn_W1f', 'L1_gnn_b1f', 'L1_gnn_W2f', 'L1_gnn_b2f', 'L1_gnn_W1b',
        'L1_gnn_b1b', 'L1_gnn_W2b', 'L1_gnn_b2b', 'L1_gnn_W1n', 'L1_gnn_b1n', 'L1_gnn_W2n', 'L1_gnn_b2n']


def kernel(**inputs):
    import numpy as _np
    import concourse.bacc as _bacc
    from concourse import mybir as _mybir
    from concourse.bass_utils import run_bass_kernel_spmd as _run

    nc = _bacc.Bacc("TRN2", target_bir_lowering=False, num_devices=1)
    arrays, args = {}, []
    for name in _INS:
        a = _np.ascontiguousarray(inputs[name])
        arrays[f"in_{name}_dram"] = a
        args.append(nc.dram_tensor(f"in_{name}_dram", a.shape, _mybir.dt.from_np(a.dtype), kind="ExternalInput").ap())
    out = nc.dram_tensor("out_dram", inputs['x'].shape, _mybir.dt.float32, kind="ExternalOutput").ap()
    gnn(nc, *args, out)
    r = _run(nc, [arrays], core_ids=[0])
    return r.results[0]["out_dram"]
```
